# Optimizing a Trainium2 kernel written in Bass

```python
import numpy as np
import jax
import jax.numpy as jnp

def _softmax(x, axis=-1):
    return jax.nn.softmax(x, axis=axis)

def _gelu(x):
    return jax.nn.gelu(x, approximate=True)

def _silu(x):
    return jax.nn.silu(x)

def _sigmoid(x):
    return jax.nn.sigmoid(x)

def _layernorm(x, axis=-1, eps=1e-05):
    m = jnp.mean(x, axis=axis, keepdims=True)
    v = jnp.var(x, axis=axis, keepdims=True)
    return (x - m) / jnp.sqrt(v + eps)

def _scatter_add(tgt, idx, src, axis=0):
    return tgt.at[idx].add(src)

def _segment_sum(src, seg, n):
    return jax.ops.segment_sum(src, seg, n)
kernel_name = 'mk_perceiver_d1_seqx_r4_e07e36'

def setup_inputs(seed: int=0):
    np.random.seed(seed)
    _w = jnp.asarray

    def _rec_inputs():
        import jax
        import jax.numpy as jnp
        _rk = jax.random.key(seed)
        x = -0.0003929 + 0.9999 * jax.random.normal(jax.random.fold_in(_rk, 1), (64, 32, 512), jnp.float32)
        _lenS = 32 - jax.random.randint(jax.random.fold_in(_rk, 7), (64,), 0, max(1, 32 // 4) + 1, jnp.int32)
        _lenS2 = 257 - jax.random.randint(jax.random.fold_in(_rk, 8), (64,), 0, max(1, 257 // 4) + 1, jnp.int32)
        _ctx_2048P = jax.random.normal(jax.random.fold_in(_rk, 11), (64, 16, 512), jnp.float32)
        _ctx_2048c = jax.random.dirichlet(jax.random.fold_in(_rk, 511), 0.3 * jnp.ones((16,), jnp.float32), (64, 257))
        _ctx_2048t = jnp.einsum('bsk,bkd->bsd', _ctx_2048c, _ctx_2048P)
        _ctx_2048t = _ctx_2048t * jax.lax.rsqrt(jnp.mean(jnp.square(_ctx_2048t)) + 1e-12) * 0.953939
        ctx_2048 = -1.39393e-06 + 0.999914 * (_ctx_2048t + 0.3 * jax.random.normal(jax.random.fold_in(_rk, 611), (64, 257, 512), jnp.float32))
        itok_BxS_0_1023 = jax.random.randint(jax.random.fold_in(_rk, 12), (64, 32), 0, 256, jnp.int32)
        return (x, ctx_2048, itok_BxS_0_1023)
    x, ctx_2048, itok_BxS_0_1023 = _rec_inputs()

    def _L0_xattn_setup():
        import jax, jax.numpy as jnp
        import numpy as np
        B, Lq, Lk = (2, 1024, 256)
        Q_DIM, KV_DIM = (512, 512)
        H, HD = (16, 128)
        KVC, QC, R = (128, 192, 64)
        LOOKBACK = 8
        NEG = -1e+30

        def _rope(x, L):
            half = x.shape[-1] // 2
            inv_freq = 1.0 / 10000.0 ** (jnp.arange(half, dtype=jnp.float32) / half)
            ang = jnp.arange(L, dtype=jnp.float32)[:, None] * inv_freq
            cos, sin = (jnp.cos(ang), jnp.sin(ang))
            x1, x2 = (x[..., :half], x[..., half:])
            return jnp.concatenate([x1 * cos - x2 * sin, x1 * sin + x2 * cos], axis=-1)
        key = jax.random.key(seed)
        ks = jax.random.split(key, 11)

        def w(k, shape, fan_in):
            return jax.random.normal(k, shape, jnp.float32) / np.sqrt(fan_in).astype(np.float32)
        return {'q': jax.random.normal(ks[0], (B, Lq, Q_DIM), jnp.float32), 'kv': jax.random.normal(ks[1], (B, Lk, KV_DIM), jnp.float32), 'seg_id': jnp.sort(jax.random.randint(ks[2], (B, Lq), 0, Lk), axis=-1), 'W_kvc': w(ks[3], (KV_DIM, KVC), KV_DIM), 'W_dq': w(ks[4], (Q_DIM, QC), Q_DIM), 'W_uq': w(ks[5], (QC, H * HD), QC), 'W_qr': w(ks[6], (QC, H * R), QC), 'W_uk': w(ks[7], (KVC, H * HD), KVC), 'W_kr': w(ks[8], (KVC, R), KVC), 'W_uv': w(ks[9], (KVC, H * HD), KVC), 'W_o': w(ks[10], (H * HD, Q_DIM), H * HD)}
    _L0_xattn_all = _L0_xattn_setup()
    _L0_xattn_in = {k: v for k, v in _L0_xattn_all.items() if k in ('W_kvc', 'W_dq', 'W_uq', 'W_qr', 'W_uk', 'W_kr', 'W_uv', 'W_o')}
    del _L0_xattn_all

    def _L0_attn_setup():
        import jax, jax.numpy as jnp
        import numpy as np
        import math
        D_MODEL = 512
        NUM_HEADS = 16
        D_K = D_MODEL // NUM_HEADS
        SEQ_LEN = 512
        THETA = 10000.0
        BATCH = 2

        def _rope(t):
            S = t.shape[-2]
            dk = t.shape[-1]
            inv_freq = jnp.exp(-math.log(THETA) * jnp.arange(0, dk, 2, dtype=jnp.float32) / dk)
            pos = jnp.arange(S, dtype=jnp.float32)
            freqs = pos[:, None] * inv_freq[None, :]
            cos = jnp.cos(freqs)
            sin = jnp.sin(freqs)
            t1 = t[..., ::2]
            t2 = t[..., 1::2]
            rot = jnp.stack([t1 * cos - t2 * sin, t1 * sin + t2 * cos], axis=-1)
            return rot.reshape(t.shape)
        key = jax.random.key(seed)
        ks = jax.random.split(key, 5)
        std = (2.0 / (D_MODEL + D_MODEL)) ** 0.5
        return {'x': jax.random.normal(ks[0], (BATCH, SEQ_LEN, D_MODEL), dtype=jnp.float32), 'Wq': jax.random.normal(ks[1], (D_MODEL, D_MODEL), dtype=jnp.float32) * std, 'Wk': jax.random.normal(ks[2], (D_MODEL, D_MODEL), dtype=jnp.float32) * std, 'Wv': jax.random.normal(ks[3], (D_MODEL, D_MODEL), dtype=jnp.float32) * std, 'Wo': jax.random.normal(ks[4], (D_MODEL, D_MODEL), dtype=jnp.float32) * std}
    _L0_attn_all = _L0_attn_setup()
    _L0_attn_in = {k: v for k, v in _L0_attn_all.items() if k in ('Wq', 'Wk', 'Wv', 'Wo')}
    del _L0_attn_all

    def _L0_ffn_setup():
        import jax, jax.numpy as jnp
        import numpy as np
        EPS = 1e-05

        def _weight_quant(w):
            scale = jnp.clip(jnp.mean(jnp.abs(w)), EPS, None)
            wq = jnp.clip(jnp.round(w / scale), -1.0, 1.0) * scale
            return w + jax.lax.stop_gradient(wq - w)

        def _act_quant(x):
            scale = 127.0 / jnp.clip(jnp.max(jnp.abs(x), axis=-1, keepdims=True), EPS, None)
            xq = jnp.clip(jnp.round(x * scale), -128.0, 127.0) / scale
            return x + jax.lax.stop_gradient(xq - x)

        def _bitlinear(x, w):
            return jnp.einsum('...i,oi->...o', _act_quant(x), _weight_quant(w))
        key = jax.random.key(seed)
        k1, k2, k3, k4 = jax.random.split(key, 4)
        d_model, d_ffn = (512, 2048)
        B, S = (4, 512)
        x = jax.random.normal(k1, (B, S, d_model), dtype=jnp.float32)
        w_gate = jax.random.normal(k2, (d_ffn, d_model), dtype=jnp.float32) * d_model ** (-0.5)
        w_up = jax.random.normal(k3, (d_ffn, d_model), dtype=jnp.float32) * d_model ** (-0.5)
        w_down = jax.random.normal(k4, (d_model, d_ffn), dtype=jnp.float32) * d_ffn ** (-0.5)
        return {'x': x, 'w_gate': w_gate, 'w_up': w_up, 'w_down': w_down}
    _L0_ffn_all = _L0_ffn_setup()
    _L0_ffn_in = {k: v for k, v in _L0_ffn_all.items() if k in ('w_gate', 'w_up', 'w_down')}
    del _L0_ffn_all
    return {'x': x, 'ctx_2048': ctx_2048, 'itok_BxS_0_1023': itok_BxS_0_1023, 'L0_xattn_W_kvc': _L0_xattn_in['W_kvc'], 'L0_xattn_W_dq': _L0_xattn_in['W_dq'], 'L0_xattn_W_uq': _L0_xattn_in['W_uq'], 'L0_xattn_W_qr': _L0_xattn_in['W_qr'], 'L0_xattn_W_uk': _L0_xattn_in['W_uk'], 'L0_xattn_W_kr': _L0_xattn_in['W_kr'], 'L0_xattn_W_uv': _L0_xattn_in['W_uv'], 'L0_xattn_W_o': _L0_xattn_in['W_o'], 'L0_attn_Wq': _L0_attn_in['Wq'], 'L0_attn_Wk': _L0_attn_in['Wk'], 'L0_attn_Wv': _L0_attn_in['Wv'], 'L0_attn_Wo': _L0_attn_in['Wo'], 'L0_ffn_w_gate': _L0_ffn_in['w_gate'], 'L0_ffn_w_up': _L0_ffn_in['w_up'], 'L0_ffn_w_down': _L0_ffn_in['w_down']}

def reference(x, ctx_2048, itok_BxS_0_1023, L0_xattn_W_kvc, L0_xattn_W_dq, L0_xattn_W_uq, L0_xattn_W_qr, L0_xattn_W_uk, L0_xattn_W_kr, L0_xattn_W_uv, L0_xattn_W_o, L0_attn_Wq, L0_attn_Wk, L0_attn_Wv, L0_attn_Wo, L0_ffn_w_gate, L0_ffn_w_up, L0_ffn_w_down):
    import jax
    import jax.numpy as jnp

    def _L0_xattn_ref(q, kv, seg_id, W_kvc, W_dq, W_uq, W_qr, W_uk, W_kr, W_uv, W_o):
        import jax, jax.numpy as jnp
        import numpy as np
        B, Lq, Lk = (2, 1024, 256)
        Q_DIM, KV_DIM = (512, 512)
        H, HD = (16, 128)
        KVC, QC, R = (128, 192, 64)
        LOOKBACK = 8
        NEG = -1e+30

        def _rope(x, L):
            half = x.shape[-1] // 2
            inv_freq = 1.0 / 10000.0 ** (jnp.arange(half, dtype=jnp.float32) / half)
            ang = jnp.arange(L, dtype=jnp.float32)[:, None] * inv_freq
            cos, sin = (jnp.cos(ang), jnp.sin(ang))
            x1, x2 = (x[..., :half], x[..., half:])
            return jnp.concatenate([x1 * cos - x2 * sin, x1 * sin + x2 * cos], axis=-1)
        b, lq, _ = q.shape
        lk = kv.shape[1]
        kv_c = kv @ W_kvc
        q_c = q @ W_dq
        q_nope = (q_c @ W_uq).reshape(b, lq, H, HD).transpose(0, 2, 1, 3)
        q_rope = (q_c @ W_qr).reshape(b, lq, H, R).transpose(0, 2, 1, 3)
        k_nope = (kv_c @ W_uk).reshape(b, lk, H, HD)
        v = (kv_c @ W_uv).reshape(b, lk, H, HD)
        k_rope = kv_c @ W_kr
        q_rope = _rope(q_rope, lq)
        k_rope = _rope(k_rope, lk)
        scale = 1.0 / np.sqrt(HD + R).astype(np.float32)
        scores = (jnp.einsum('bhqd,bkhd->bhqk', q_nope, k_nope) + jnp.einsum('bhqr,bkr->bhqk', q_rope, k_rope)) * scale
        k_ids = jnp.arange(lk)[None, None, :]
        qs = seg_id[:, :, None]
        good = (k_ids <= qs) & (k_ids >= qs - LOOKBACK)
        scores = jnp.where(good[:, None, :, :], scores, NEG)
        attn = jax.nn.softmax(scores, axis=-1)
        out = jnp.einsum('bhqk,bkhd->bqhd', attn, v).reshape(b, lq, H * HD)
        return out @ W_o

    def _L0_attn_ref(x, Wq, Wk, Wv, Wo):
        import jax, jax.numpy as jnp
        import numpy as np
        import math
        D_MODEL = 512
        NUM_HEADS = 16
        D_K = D_MODEL // NUM_HEADS
        SEQ_LEN = 512
        THETA = 10000.0
        BATCH = 2

        def _rope(t):
            S = t.shape[-2]
            dk = t.shape[-1]
            inv_freq = jnp.exp(-math.log(THETA) * jnp.arange(0, dk, 2, dtype=jnp.float32) / dk)
            pos = jnp.arange(S, dtype=jnp.float32)
            freqs = pos[:, None] * inv_freq[None, :]
            cos = jnp.cos(freqs)
            sin = jnp.sin(freqs)
            t1 = t[..., ::2]
            t2 = t[..., 1::2]
            rot = jnp.stack([t1 * cos - t2 * sin, t1 * sin + t2 * cos], axis=-1)
            return rot.reshape(t.shape)
        B, S, D = x.shape
        H, dk = (NUM_HEADS, D // NUM_HEADS)

        def split_heads(t):
            return t.reshape(B, S, H, dk).transpose(0, 2, 1, 3)
        q = split_heads(x @ Wq.T)
        k = split_heads(x @ Wk.T)
        v = split_heads(x @ Wv.T)
        q = _rope(q)
        k = _rope(k)
        scores = jnp.einsum('bhqd,bhkd->bhqk', q, k) / math.sqrt(dk)
        causal = jnp.tril(jnp.ones((S, S), dtype=bool))
        scores = jnp.where(causal[None, None], scores, -jnp.inf)
        attn = jax.nn.softmax(scores, axis=-1)
        ctx = jnp.einsum('bhqk,bhkd->bhqd', attn, v)
        ctx = ctx.transpose(0, 2, 1, 3).reshape(B, S, D)
        return ctx @ Wo.T

    def _L0_ffn_ref(x, w_gate, w_up, w_down):
        import jax, jax.numpy as jnp
        import numpy as np
        EPS = 1e-05

        def _weight_quant(w):
            scale = jnp.clip(jnp.mean(jnp.abs(w)), EPS, None)
            wq = jnp.clip(jnp.round(w / scale), -1.0, 1.0) * scale
            return w + jax.lax.stop_gradient(wq - w)

        def _act_quant(x):
            scale = 127.0 / jnp.clip(jnp.max(jnp.abs(x), axis=-1, keepdims=True), EPS, None)
            xq = jnp.clip(jnp.round(x * scale), -128.0, 127.0) / scale
            return x + jax.lax.stop_gradient(xq - x)

        def _bitlinear(x, w):
            return jnp.einsum('...i,oi->...o', _act_quant(x), _weight_quant(w))
        gate = _bitlinear(x, w_gate)
        up = _bitlinear(x, w_up)
        return _bitlinear(jax.nn.silu(gate) * up, w_down)
    x = x + _L0_xattn_ref(_layernorm(x, axis=-1), ctx_2048, itok_BxS_0_1023, L0_xattn_W_kvc, L0_xattn_W_dq, L0_xattn_W_uq, L0_xattn_W_qr, L0_xattn_W_uk, L0_xattn_W_kr, L0_xattn_W_uv, L0_xattn_W_o)
    x = x + _L0_attn_ref(_layernorm(x, axis=-1), L0_attn_Wq, L0_attn_Wk, L0_attn_Wv, L0_attn_Wo)
    x = x + _L0_ffn_ref(_layernorm(x, axis=-1), L0_ffn_w_gate, L0_ffn_w_up, L0_ffn_w_down)
    return x

_drawn_inputs = setup_inputs


def setup_inputs(seed=0):
    import zlib

    import numpy as np

    out = dict(_drawn_inputs(seed))
    spreads = {}
    factors = {}
    for name, (base, spread) in spreads.items():
        noise = np.random.default_rng([zlib.crc32(name.encode()), seed]).standard_normal(out[name].shape)
        drawn = base * np.exp(spread * noise) if base else spread * noise
        out[name] = jnp.asarray(drawn.astype(out[name].dtype))
    for name, factor in factors.items():
        out[name] = (out[name] * factor).astype(out[name].dtype)
    return out
```

```python
from contextlib import ExitStack

import concourse.bass as bass
from concourse import mybir

F32 = mybir.dt.float32
F32R = mybir.dt.float32r
BF16 = mybir.dt.bfloat16
I32 = mybir.dt.int32
ALU = mybir.AluOpType
ACT = mybir.ActivationFunctionType
AX = mybir.AxisListType

P = 128
D = 512
DC = D // P
B, LQ, LK = 64, 32, 257
TB = P // LQ
TILES = B // TB
PAIRS = TILES // 2
H, HD, QC, KVC, R = 16, 128, 192, 128, 64
QC1 = QC - P
LM = LK - 1
KT = LM // P
LOOKBACK = 8
XSCALE = float(1.0 / (HD + R) ** 0.5)
NEG = -float(2 ** 100)
EPS = 1e-5
SH, SD = 16, 32
SSCALE = float(1.0 / SD ** 0.5)
F = 2048
FCH = F // P
MAGIC = float(3 * 2 ** 22)


SPLIT = ((0, 0), (0, 1), (1, 0))


def after(eng, sem, count):
    if not isinstance(count, int) or count > 0:
        eng.wait_ge(sem, count)


def build(nc, x, ctxT, seg, Wkvc, Wkr2, Wdq, WuqT, WukT, WuvT, Wo, Wqr,
          Sq, Sk, Sv, So, Wffn, tab_k, tab_q, tab_s, tab_i, out):
    with ExitStack() as top:
        def sbt(ctx, name, shape, dt=F32):
            return ctx.enter_context(nc.sbuf_tensor(name, shape, dt))

        x_all = sbt(top, "x_all", [P, TILES, D])
        ident = sbt(top, "ident", [P, P])
        wsum = sbt(top, "wsum", [P, 4])
        wsc = sbt(top, "wsc", [P, 3])

        with ExitStack() as ctx:
            cross_attention(nc, ctx, x_all, ident, wsum, x, ctxT, seg, Wkvc, Wkr2, Wdq, WuqT, WukT,
                            WuvT, Wo, Wqr, Wffn, tab_k, tab_q, tab_i)
        wt = sbt(top, "wt", [P, 3, D * F // P], BF16)
        with ExitStack() as ctx:
            self_attention(nc, ctx, x_all, ident, wsum, wt, wsc, Sq, Sk, Sv, So, Wffn, tab_s)
        with ExitStack() as ctx:
            feed_forward(nc, ctx, x_all, ident, wt, wsc, out)


def cross_attention(nc, ctx, x_all, ident, wsum, x, ctxT, seg, Wkvc, Wkr2, Wdq, WuqT, WukT, WuvT,
                    Wo, Wqr, Wffn, tab_k, tab_q, tab_i):
    def sb(name, shape, dt=F32):
        return ctx.enter_context(nc.sbuf_tensor(name, shape, dt))

    def sem(name):
        return ctx.enter_context(nc.semaphore(name))

    wkvc = sb("wkvc", [P, DC, KVC])
    wkr = sb("wkr", [P, P])
    wdq = sb("wdq", [P, DC, QC])
    wqn0 = sb("wqn0", [P, H, KVC])
    wqn1 = sb("wqn1", [QC1, H, KVC])
    wqr0 = sb("wqr0", [P, H * R])
    wqr1 = sb("wqr1", [QC1, H * R])
    wvo = sb("wvo", [P, H, D])
    tk = sb("tk", [P, LK])
    tq = sb("tq", [P, 3, R // 2])
    iota = sb("iota", [P, LK])
    seg_i = sb("seg_i", [P, B], I32)
    qc0 = sb("qc0", [P, TILES * P])
    qc1 = sb("qc1", [QC1, TILES * P])
    qcur0 = sb("qcur0", [P, 2, P])
    qcur1 = sb("qcur1", [QC1, 2, P])
    rc = sb("rc", [P, 4, R])
    rs_ = sb("rs_", [P, 4, R])
    qr2 = sb("qr2", [P, 4, 2, R])
    cx = sb("cx", [P, 2, DC * LK])
    kvt = sb("kvt", [P, 2, LK])
    kvr = sb("kvr", [P, 2, KT, KVC])
    kp = sb("kp", [P, LM])
    kp_last = sb("kp_last", [P, 1])
    cseg = sb("cseg", [P, 8])
    dist = sb("dist", [P, LK])
    mask = sb("mask", [P, LK])
    smask = sb("smask", [P, 1])
    pr = sb("pr", [P, 2, 4, LM])
    mx = sb("mx", [P, 4])
    nb = sb("nb", [P, 4])
    rsum = sb("rsum", [P, 4])
    e_last = sb("e_last", [P, 4])
    tot = sb("tot", [P, 4])
    rinv = sb("rinv", [P, 4])
    wch = sb("wch", [P, 2, 3, P])
    wpart = sb("wpart", [P, 3, B])
    arena = sb("arena", [P, 15360])
    qn = arena[:, 0:4096].rearrange("p (u b g c) -> p u b g c", u=2, b=TB, g=4)
    qrt = arena[:, 4096:8192].rearrange("p (u b g c) -> p u b g c", u=2, b=TB, g=4)
    yt = arena[:, 8192:12288].rearrange("p (u h c) -> p u h c", u=2, h=H)
    pt = arena[:, 12288:13312].rearrange("p (k c) -> p k c", k=KT)
    wo_st = arena[:, 0:8192].rearrange("p (h n) -> p h n", h=H)
    wuv_st = arena[:, 8192:10240].rearrange("p (h c) -> p h c", h=H)
    wuk_st = arena[:, 10240:12288].rearrange("p (h c) -> p h c", h=H)
    wuq_st = arena[:, 12288:15360].rearrange("p (h c) -> p h c", h=H)
    xn = pr[:].rearrange("p u g k -> p u (g k)")[:, :, 0:D]
    xnt = cx[:, :, 0:D].rearrange("p u (c q) -> p u c q", c=DC)
    carrier = sb("carrier", [P, 1])
    stats = sb("stats", [P, 6])
    mv = sb("mv", [P, 2])
    veps = sb("veps", [P, 1])
    rstd = sb("rstd", [P, 1])
    power = sb("power", [P, 1])

    with ExitStack() as pctx:
        ps = pctx.enter_context(nc.psum_tensor("ps", [P, 8, 512], F32))

        x_in, x_in2 = sem("x_loaded"), sem("x_rest_loaded")
        w_in = [sem(f"weights_loaded{i}") for i in range(8)]
        k_in = sem("tables_loaded")
        pw_set = sem("power_set")
        id_set = sem("ident_set")
        bnd = sem("ln_stats")
        ve_s = sem("ln_var_eps")
        mv_s = sem("ln_mean_var")
        rstd_s = sem("ln_rstd")
        xn_s = sem("xn_ready")
        xt_s = sem("xn_transposed")
        xtc_s = sem("xn_transpose_copied")
        qc_s = sem("q_latent_done")
        qcc_s = sem("q_latent_copied")
        prep_s = sem("weight_product_done")
        prepa_s = sem("weight_product_copied_act")
        prepd_s = sem("weight_product_copied_dve")
        id0_s = sem("ident_zeroed")

        items = [("qn0", g) for g in range(4)] + [("qn1", g) for g in range(4)] + \
                [("vo", h) for h in range(H)]
        NBANK = 4

        def copy_product(copy, what, g, i):
            src = ps[:, i % NBANK, :]
            if what == "qn0":
                return copy(wqn0[:, 4 * g:4 * g + 4, :].rearrange("p h c -> p (h c)"), src)
            if what == "qn1":
                return copy(wqn1[:, 4 * g:4 * g + 4, :].rearrange("p h c -> p (h c)"), src[0:QC1, :])
            return copy(wvo[:, g, :], src)

        with nc.Block() as block:
            @block.sync
            def _(sp):
                sp.dma_start(x_all[:, 0:2, :], x[:, 0:2, :]).then_inc(x_in, 16)
                sp.dma_start(wdq[:], Wdq).then_inc(w_in[0], 16)
                sp.dma_start(x_all[:, 2:TILES, :], x[:, 2:TILES, :]).then_inc(x_in2, 16)
                sp.dma_start(wuq_st, WuqT).then_inc(w_in[1], 16)
                sp.dma_start(wuk_st, WukT).then_inc(w_in[2], 16)
                sp.dma_start(wuv_st, WuvT).then_inc(w_in[3], 16)
                sp.dma_start(wo_st, Wo).then_inc(w_in[4], 16)
                sp.dma_start(wkvc[:], Wkvc).then_inc(w_in[5], 16)
                sp.dma_start(wkr[:], Wkr2).then_inc(w_in[5], 16)
                sp.dma_start(wqr0[:], Wqr[0:P, :]).then_inc(w_in[6], 16)
                sp.dma_start(wqr1[:], Wqr[P:QC, :]).then_inc(w_in[6], 16)
                sp.dma_start(tk[:], tab_k).then_inc(k_in, 16)
                sp.dma_start(tq[:], tab_q).then_inc(k_in, 16)
                sp.dma_start(iota[:], tab_i).then_inc(k_in, 16)
                sp.dma_start(seg_i[:], seg).then_inc(k_in, 16)
                sp.wait_ge(k_in, 64)
                sp.wait_ge(w_in[5], 32)
                sp.wait_ge(w_in[6], 32)

            @block.gpsimd
            def _(pool):
                pool.memset(power[:], -0.5).then_inc(pw_set, 1)
                pool.memset(ident[:], 0.0).then_inc(id0_s, 1)
                pool.wait_ge(id0_s, 1)
                pool.affine_select(out=ident[:], in_=ident[:], compare_op=ALU.not_equal, fill=1.0,
                                   base=0, pattern=[[-1, P]], channel_multiplier=1).then_inc(id_set, 1)
                pool.wait_ge(pw_set, 1)
                with pool.Fori(0, TILES) as t:
                    pool.wait_ge(ve_s, t + 1)
                    pool.tensor_tensor(rstd[:], veps[:], power[:], ALU.pow).then_inc(rstd_s, 1)

            @block.vector
            def _(dve):
                dve.wait_ge(x_in, 16)

                def norm_tile(p, u):
                    t = 2 * p + u
                    dve.bn_stats(stats[:], x_all[:, bass.ds(t, 1), :]).then_inc(bnd, 1)
                    dve.wait_ge(bnd, t + 1)
                    dve.memset(carrier[:], 0.0)
                    dve.bn_aggr(mv[:], stats[:]).then_inc(mv_s, 1)
                    dve.wait_ge(mv_s, t + 1)
                    dve.tensor_scalar(veps[:], mv[:, 1:2], EPS, None, ALU.add).then_inc(ve_s, 1)
                    if not isinstance(p, int):
                        dve.wait_ge(xt_s, t - 1)
                    dve.wait_ge(rstd_s, t + 1)
                    dve.tensor_scalar(xn[:, u, :], x_all[:, bass.ds(t, 1), :], mv[:, 0:1], rstd[:, 0:1],
                                      ALU.subtract, ALU.mult).then_inc(xn_s, 1)
                    if not isinstance(p, int):
                        latent_copy(t - 2, u)

                def latent_copy(t, u):
                    dve.wait_ge(qc_s, t + 1)
                    src = ps[:, 6 + u, :]
                    dve.tensor_copy(qc0[:, bass.ds(t * P, P)], src[:, 0:P])
                    dve.tensor_copy(qc1[:, bass.ds(t * P, P)], src[0:QC1, P:2 * P]).then_inc(qcc_s, 1)

                norm_tile(0, 0)
                norm_tile(0, 1)
                dve.wait_ge(x_in2, 16)
                with dve.Fori(1, PAIRS) as p:
                    norm_tile(p, 0)
                    norm_tile(p, 1)
                latent_copy(TILES - 2, 0)
                latent_copy(TILES - 1, 1)
                for i, (what, g) in enumerate(items):
                    if i % 2 == 1:
                        dve.wait_ge(prep_s, i + 1)
                        copy_product(dve.tensor_copy, what, g, i).then_inc(prepd_s, 1)

            @block.scalar
            def _(act):
                def turn_copy(p, u):
                    t = 2 * p + u
                    act.wait_ge(xt_s, t + 1)
                    if not isinstance(p, int):
                        act.wait_ge(qc_s, t - 1)
                    act.copy(xnt[:, u, :, :].rearrange("p c q -> p (c q)"), ps[:, 4 + u, :]).then_inc(xtc_s, 1)

                turn_copy(0, 0)
                turn_copy(0, 1)
                with act.Fori(1, PAIRS) as p:
                    turn_copy(p, 0)
                    turn_copy(p, 1)
                for i, (what, g) in enumerate(items):
                    if i % 2 == 0:
                        act.wait_ge(prep_s, i + 1)
                        copy_product(act.copy, what, g, i).then_inc(prepa_s, 1)

            @block.tensor
            def _(pe):
                pe.wait_ge(id_set, 1)

                def turn(p, u):
                    t = 2 * p + u
                    pe.wait_ge(xn_s, t + 1)
                    if not isinstance(p, int):
                        pe.wait_ge(xtc_s, t - 1)
                    for c in range(DC):
                        last = pe.transpose(ps[:, 4 + u, c * P:(c + 1) * P], xn[:, u, c * P:(c + 1) * P], ident[:])
                    last.then_inc(xt_s, 1)

                def latent(t, u):
                    pe.wait_ge(xtc_s, t + 1)
                    after(pe, qcc_s, t - 1)
                    for c in range(DC):
                        pe.matmul(ps[:, 6 + u, 0:P], wdq[:, c, 0:P], xnt[:, u, c, :], start=(c == 0), stop=(c == DC - 1))
                    for c in range(DC):
                        last = pe.matmul(ps[0:QC1, 6 + u, P:2 * P], wdq[:, c, P:QC], xnt[:, u, c, :],
                                         start=(c == 0), stop=(c == DC - 1))
                    last.then_inc(qc_s, 1)

                turn(0, 0)
                pe.wait_ge(w_in[0], 16)
                turn(0, 1)
                latent(0, 0)
                with pe.Fori(1, PAIRS) as p:
                    turn(p, 0)
                    latent(2 * p - 1, 1)
                    turn(p, 1)
                    latent(2 * p, 0)
                latent(TILES - 1, 1)
                pe.wait_ge(w_in[1], 16)
                pe.wait_ge(w_in[2], 16)
                for i, (what, g) in enumerate(items):
                    if what == "vo" and g == 0:
                        pe.wait_ge(w_in[3], 16)
                        pe.wait_ge(w_in[4], 16)
                    if i >= NBANK:
                        pe.wait_ge(prepd_s if i % 2 else prepa_s, (i - NBANK) // 2 + 1)
                    if what == "vo":
                        last = pe.matmul(ps[:, i % NBANK, :], wuv_st[:, g, :], wo_st[:, g, :], start=True, stop=True)
                    else:
                        m0, m = (0, P) if what == "qn0" else (P, QC1)
                        for k in range(4):
                            last = pe.matmul(ps[0:m, i % NBANK, k * P:(k + 1) * P], wuq_st[:, 4 * g + k, m0:m0 + m],
                                             wuk_st[:, 4 * g + k, :], start=True, stop=True)
                    last.then_inc(prep_s, 1)

        cx_in = [sem("context_loaded0"), sem("context_loaded1")]
        wc_in = [sem("ffn_chunk_loaded0"), sem("ffn_chunk_loaded1")]
        qcur_s = sem("latent_tile_ready")
        qn_done, qn_cp = sem("qn_done"), sem("qn_copied")
        qr_done, qr_read = sem("qr_done"), sem("qr_read")
        qr_sum = sem("qr_added")
        qrt_done, qrt_cp = sem("qrt_done"), sem("qrt_copied")
        kv_done, kvt_s = sem("kv_done"), sem("kvt_ready")
        kr_done, kr_read = sem("kr_done"), sem("kr_read")
        kp_s = sem("kp_ready")
        kvr_done, kvr_cp = sem("kvr_done"), sem("kvr_copied")
        s_done, s_read = sem("scores_done"), sem("scores_read")
        cseg_s, dist_s, mask_s = sem("cseg_ready"), sem("dist_ready"), sem("mask_ready")
        nb_s = sem("bias_ready")
        exp_s = sem("exp_done")
        tot_s, rinv_s = sem("total_ready"), sem("rinv_ready")
        pr_s = sem("probs_ready")
        t0_done, t1_done = sem("probs_turned0"), sem("probs_turned1")
        t0_cp, t1_cp = sem("probs_turned0_copied"), sem("probs_turned1_copied")
        o_done, o_cp = sem("o_done"), sem("o_copied")
        c_done, c_add = sem("out_done"), sem("out_added")
        wpart_s = sem("ffn_chunk_summed")
        wsum_s = sem("ffn_sum_zeroed")

        S = ps[:, 0:2, :].rearrange("p a (g k) -> p (a g) k", g=2)
        R0, R1, R2, R3, R4, CB = (ps[:, 2 + i, :] for i in range(6))

        def slots(p):
            for s in range(8):
                yield s, 8 * p + s, 2 * p + s // 4, s % 4

        HEADS = {1: (0, 6), 2: (6, 11), 3: (11, 16)}

        with nc.Block() as block:
            @block.sync
            def _(sp):
                def load(p):
                    for s, n, t, j in slots(p):
                        if not (isinstance(p, int) and p == 0 and s < 2):
                            sp.wait_ge(kv_done, n - 1)
                        sp.dma_start(cx[:, s % 2, :], ctxT[bass.ds(n, 1), :, :].rearrange("a p n -> (a p) n")).then_inc(cx_in[s % 2], 16)
                        if not (isinstance(p, int) and p == 0 and s < 2):
                            sp.wait_ge(wpart_s, n - 1)
                        sp.dma_start(wch[:, s % 2, :, :], Wffn[:, :, bass.ds(n * P, P)]).then_inc(wc_in[s % 2], 16)
                load(0)
                with sp.Fori(1, PAIRS) as p:
                    load(p)

            @block.gpsimd
            def _(pool):
                def take(t, u):
                    pool.tensor_copy(qcur0[:, u, :], qc0[:, bass.ds(t * P, P)])
                    pool.tensor_copy(qcur1[:, u, :], qc1[:, bass.ds(t * P, P)]).then_inc(qcur_s, 1)

                def add_rope(a):
                    pool.wait_ge(qr_read, a + 1)
                    after(pool, qrt_done, a)
                    pool.tensor_tensor(qr2[:, :, 0, :], rc[:], rs_[:], ALU.add)
                    pool.tensor_tensor(qr2[:, :, 1, :], rc[:], rs_[:], ALU.add).then_inc(qr_sum, 1)

                def pair(p):
                    for s, n, t, j in slots(p):
                        if j == 0 and not (isinstance(p, int) and p == PAIRS - 1):
                            pool.wait_ge(qr_done, 4 * t + 4)
                            take(t + 2, s // 4)
                        if not (isinstance(p, int) and p == PAIRS - 1 and s >= 4):
                            add_rope(n + 4)
                take(0, 0)
                take(1, 1)
                for a in range(4):
                    add_rope(a)
                pair(0)
                with pool.Fori(1, PAIRS - 1) as p:
                    pair(p)
                pair(PAIRS - 1)

            @block.vector
            def _(dve):
                def rope(a):
                    dve.wait_ge(qr_done, a + 1)
                    after(dve, qr_sum, a)
                    q = R4[:, 0:256].rearrange("p (g f) -> p g f", f=R // 2)
                    qh = R4[:, 0:256].rearrange("p (h a f) -> p h a f", h=4, a=2)
                    rsh = rs_[:].rearrange("p h (a f) -> p h a f", a=2)
                    dve.tensor_tensor(rc[:].rearrange("p h (a f) -> p (h a) f", a=2), q,
                                      tq[:, 0:1, :].to_broadcast([P, 8, R // 2]), ALU.mult)
                    dve.tensor_tensor(rsh[:, :, 0, :], qh[:, :, 1, :], tq[:, 1:2, :].to_broadcast([P, 4, R // 2]), ALU.mult)
                    dve.tensor_tensor(rsh[:, :, 1, :], qh[:, :, 0, :], tq[:, 2:3, :].to_broadcast([P, 4, R // 2]),
                                      ALU.mult).then_inc(qr_read, 1)

                def total(m):
                    dve.wait_ge(exp_s, m + 1)
                    dve.tensor_tensor(tot[:], rsum[:], e_last[:], ALU.add).then_inc(tot_s, 1)
                    dve.wait_ge(tot_s, m + 1)
                    dve.reciprocal(rinv[:], tot[:]).then_inc(rinv_s, 1)

                def scale_probs(m, u):
                    dve.wait_ge(rinv_s, m + 1)
                    for g in range(4):
                        last = dve.tensor_scalar(pr[:, u, g, :], pr[:, u, g, :], rinv[:, g:g + 1], None, ALU.mult)
                    last.then_inc(pr_s, 1)

                def copy_t1(m):
                    dve.wait_ge(t1_done, m + 1)
                    after(dve, o_done, m)
                    dve.tensor_copy(pt[:, 1, :], R2).then_inc(t1_cp, 1)

                def residual(t):
                    dve.wait_ge(c_done, t + 1)
                    dve.tensor_tensor(x_all[:, bass.ds(t, 1), :], CB, x_all[:, bass.ds(t, 1), :], ALU.add).then_inc(c_add, 1)

                def pair(p):
                    first = isinstance(p, int) and p == 0
                    lastp = isinstance(p, int) and p == PAIRS - 1
                    dve.tensor_scalar(cseg[:], seg_i[:, bass.ds(8 * p, 8)], -1.0, float(LOOKBACK // 2), ALU.mult, ALU.add).then_inc(cseg_s, 1)
                    for s, n, t, j in slots(p):
                        u = s % 2
                        dve.wait_ge(kv_done, n + 1)
                        after(dve, o_cp, n - 1)
                        dve.tensor_copy(kvt[:, u, LM:LK], R0[:, LM:LK])
                        dve.tensor_scalar(kvt[:, u, 0:LM], R0[:, 0:LM], R0[:, LM:LK], None, ALU.subtract).then_inc(kvt_s, 1)
                        if not (first and s == 0):
                            total(n - 1)
                            scale_probs(n - 1, 1 - u)
                        dve.wait_ge(kr_done, n + 1)
                        after(dve, s_done, n)
                        dve.scalar_tensor_tensor(kp[:], R1[:, 0:LM], R1[:, LM:LK], tk[:, 0:LM], ALU.add, ALU.mult)
                        dve.tensor_tensor(kp_last[:], R1[:, LM:LK], tk[:, LM:LK], ALU.mult).then_inc(kr_read, 1)
                        dve.wait_ge(kr_read, n + 1)
                        dve.tensor_scalar(kp[:], kp[:], kp_last[:, 0:1], None, ALU.subtract).then_inc(kp_s, 1)
                        if not (lastp and s >= 4):
                            rope(n + 4)
                        dve.wait_ge(dist_s, n + 1)
                        dve.tensor_scalar(mask[:], dist[:], LOOKBACK ** 2 / 4 + 0.5, NEG, ALU.is_gt, ALU.mult).then_inc(mask_s, 1)
                        if not (first and s == 0):
                            copy_t1(n - 1)
                        dve.wait_ge(mask_s, n + 1)
                        dve.wait_ge(s_done, n + 1)
                        after(dve, t1_done, n - 1)
                        dve.tensor_scalar(smask[:], mask[:, LM:LK], XSCALE, None, ALU.mult)
                        for g in range(4):
                            last = dve.tensor_tensor_reduce(pr[:, u, g, :], S[:, g, :], mask[:, 0:LM], 1.0, 2 * NEG,
                                                            ALU.add, ALU.max, mx[:, g:g + 1])
                        last.then_inc(s_read, 1)
                        dve.wait_ge(s_read, n + 1)
                        dve.tensor_scalar(nb[:], mx[:], mask[:, LM:LK], -XSCALE, ALU.max, ALU.mult).then_inc(nb_s, 1)
                        if j == 0 and not (first and s <= 4):
                            residual(t - 2)
                        dve.wait_ge(wc_in[u], 64 * p + 16 * (s // 2) + 16)
                        dve.tensor_reduce(wpart[:, :, bass.ds(n, 1)], wch[:, u, :, :], AX.X, ALU.add, apply_absolute_value=True).then_inc(wpart_s, 1)

                for a in range(4):
                    rope(a)
                pair(0)
                with dve.Fori(1, PAIRS - 1) as p:
                    pair(p)
                pair(PAIRS - 1)
                total(B - 1)
                scale_probs(B - 1, 1)
                copy_t1(B - 1)
                residual(TILES - 2)
                residual(TILES - 1)
                dve.memset(wsum[:], 0.0).then_inc(wsum_s, 1)
                dve.wait_ge(wsum_s, 1)
                dve.wait_ge(wpart_s, B)
                dve.tensor_reduce(wsum[:, 0:3], wpart[:], AX.X, ALU.add)

            @block.scalar
            def _(act):
                def copy_qn(a, u, j):
                    act.wait_ge(qn_done, a + 1)
                    act.copy(qn[:, u, :, j, :].rearrange("p b (h q) -> p h b q", h=4),
                             R3.rearrange("p (h b q) -> p h b q", h=4, b=TB)).then_inc(qn_cp, 1)

                def copy_qrt(a, u, j):
                    act.wait_ge(qrt_done, a + 1)
                    act.copy(qrt[:, u, :, j, :].rearrange("p b (h q) -> p h b q", h=4),
                             R0.rearrange("p (h b q) -> p h b q", h=4, b=TB)).then_inc(qrt_cp, 1)

                def copy_t0(m):
                    act.wait_ge(t0_done, m + 1)
                    after(act, o_done, m)
                    act.copy(pt[:, 0, :], R1).then_inc(t0_cp, 1)

                def copy_o(m, tile, ty, j, u):
                    act.wait_ge(o_done, m + 1)
                    if j == 0:
                        after(act, c_done, tile - 1)
                    act.activation(yt[:, ty, :, j * LQ:(j + 1) * LQ], R4.rearrange("p (h q) -> p h q", h=H),
                                   ACT.Identity, bias=kvt[:, u, LM:LK]).then_inc(o_cp, 1)

                def pair(p):
                    first = isinstance(p, int) and p == 0
                    lastp = isinstance(p, int) and p == PAIRS - 1
                    for s, n, t, j in slots(p):
                        u = s % 2
                        if s == 0:
                            act.wait_ge(cseg_s, p + 1)
                        after(act, mask_s, n)
                        act.activation(dist[:], iota[:], ACT.Square, bias=cseg[:, s:s + 1]).then_inc(dist_s, 1)
                        if not (lastp and s >= 4):
                            if j == 0:
                                after(act, s_done, 4 * t)
                            copy_qn(n + 4, 1 - s // 4, j)
                        act.wait_ge(kvr_done, n + 1)
                        after(act, o_done, n - 1)
                        act.copy(kvr[:, u, :, :].rearrange("p k c -> p (k c)"), R2[:, 0:KT * KVC]).then_inc(kvr_cp, 1)
                        if not (first and s == 0):
                            copy_t0(n - 1)
                        if not (lastp and s >= 4):
                            copy_qrt(n + 4, 1 - s // 4, j)
                        act.wait_ge(nb_s, n + 1)
                        for g in range(4):
                            if g == 2 and j == 0 and not (first and s == 0):
                                copy_o(n - 1, t - 1, 1 - s // 4, 3, 1 - u)
                            act.activation(pr[:, u, g, :], pr[:, u, g, :], ACT.Exp, bias=nb[:, g:g + 1],
                                           scale=XSCALE, accum_out=rsum[:, g:g + 1])
                        act.activation(e_last[:], nb[:], ACT.Exp, bias=smask[:, 0:1]).then_inc(exp_s, 1)
                        if j:
                            copy_o(n - 1, t, s // 4, j - 1, 1 - u)

                for a in range(4):
                    copy_qn(a, 0, a)
                    copy_qrt(a, 0, a)
                pair(0)
                with act.Fori(1, PAIRS - 1) as p:
                    pair(p)
                pair(PAIRS - 1)
                copy_t0(B - 1)
                copy_o(B - 1, TILES - 1, 1, 3, 1)

            @block.tensor
            def _(pe):
                def qn_product(u, j):
                    for k in range(4):
                        h = 4 * j + k
                        pe.matmul(R3[:, k * P:(k + 1) * P], wqn0[:, h, :], qcur0[:, u, :], start=True, stop=False)
                        last = pe.matmul(R3[:, k * P:(k + 1) * P], wqn1[:, h, :], qcur1[:, u, :], start=False, stop=True)
                    last.then_inc(qn_done, 1)

                def qr_product(u, j):
                    pe.matmul(R4[:, 0:256], qcur0[:, u, :], wqr0[:, 256 * j:256 * j + 256], start=True, stop=False)
                    pe.matmul(R4[:, 0:256], qcur1[:, u, :], wqr1[:, 256 * j:256 * j + 256], start=False, stop=True).then_inc(qr_done, 1)

                def qr_turn(a):
                    pe.wait_ge(qr_sum, a + 1)
                    for k in range(4):
                        last = pe.transpose(R0[:, k * P:(k + 1) * P], qr2[:, k, :, :].rearrange("p a r -> p (a r)"), ident[:])
                    last.then_inc(qrt_done, 1)

                def probs_turn(m, u):
                    pe.wait_ge(pr_s, m + 1)
                    for k, (bank, done) in enumerate(((R1, t0_done), (R2, t1_done))):
                        for g in range(4):
                            last = pe.transpose(bank[:, g * P:(g + 1) * P], pr[:, u, g, k * P:(k + 1) * P], ident[:])
                        last.then_inc(done, 1)

                def out_product(ty, h0, h1):
                    for h in range(h0, h1):
                        last = pe.matmul(CB, yt[:, ty, h, :], wvo[:, h, :], start=(h == 0), stop=(h == H - 1))
                    if h1 == H:
                        last.then_inc(c_done, 1)

                def o_product(m, u):
                    pe.wait_ge(t0_cp, m + 1)
                    pe.wait_ge(t1_cp, m + 1)
                    for k in range(KT):
                        last = pe.matmul(R4, kvr[:, u, k, :], pt[:, k, :], start=(k == 0), stop=(k == KT - 1))
                    last.then_inc(o_done, 1)

                def pair(p):
                    first = isinstance(p, int) and p == 0
                    lastp = isinstance(p, int) and p == PAIRS - 1
                    for s, n, t, j in slots(p):
                        u = s % 2
                        more = not (lastp and s >= 4)
                        nt = 1 - s // 4
                        back = not (first and s == 0)
                        pe.wait_ge(cx_in[u], 64 * p + 16 * (s // 2) + 16)
                        pe.wait_ge(qrt_cp, n + 4 if more else B)
                        after(pe, kvt_s, n)
                        for c in range(DC):
                            last = pe.matmul(R0[:, 0:LK], wkvc[:, c, :], cx[:, u, c * LK:(c + 1) * LK],
                                             start=(c == 0), stop=(c == DC - 1))
                        last.then_inc(kv_done, 1)
                        if more:
                            if j == 0:
                                pe.wait_ge(qcur_s, t + 2)
                            pe.wait_ge(qn_cp, n + 4)
                            qn_product(nt, j)
                        pe.wait_ge(kvt_s, n + 1)
                        after(pe, kr_read, n)
                        after(pe, t0_cp, n - 1)
                        pe.matmul(R1[:, 0:LK], wkr[:], kvt[:, u, :], start=True, stop=True).then_inc(kr_done, 1)
                        after(pe, kvr_cp, n)
                        after(pe, t1_cp, n - 1)
                        for k in range(KT):
                            last = pe.transpose(R2[:, k * KVC:(k + 1) * KVC], kvt[:, u, k * P:(k + 1) * P], ident[:])
                        last.then_inc(kvr_done, 1)
                        if more:
                            pe.wait_ge(qr_read, n + 4)
                            after(pe, o_cp, n - 1)
                            qr_product(nt, j)
                        pe.wait_ge(kp_s, n + 1)
                        after(pe, s_read, n)
                        pe.wait_ge(qn_cp, 4 * t + 4)
                        pe.wait_ge(qrt_cp, 4 * t + 4)
                        for g in range(4):
                            pe.matmul(S[:, g, :], qn[:, s // 4, j, g, :], kvt[:, u, 0:LM], start=True, stop=False)
                            last = pe.matmul(S[:, g, :], qrt[:, s // 4, j, g, :], kp[:], start=False, stop=True)
                        last.then_inc(s_done, 1)
                        if back:
                            pe.wait_ge(kr_read, n + 1)
                            pe.wait_ge(kvr_cp, n + 1)
                            probs_turn(n - 1, 1 - u)
                        if more:
                            qr_turn(n + 4)
                        if j in HEADS and not (first and s < 4):
                            if j == 1:
                                pe.wait_ge(o_cp, 4 * t)
                                after(pe, c_add, t - 1)
                            out_product(1 - s // 4, *HEADS[j])
                        if back:
                            pe.wait_ge(qr_read, n + 5 if more else B)
                            after(pe, o_cp, n - 1)
                            o_product(n - 1, 1 - u)

                for a in range(4):
                    if a == 0:
                        pe.wait_ge(qcur_s, 1)
                    after(pe, qn_cp, a)
                    qn_product(0, a)
                    after(pe, qr_read, a)
                    qr_product(0, a)
                    after(pe, qrt_cp, a)
                    qr_turn(a)
                pair(0)
                with pe.Fori(1, PAIRS - 1) as p:
                    pair(p)
                pair(PAIRS - 1)
                pe.wait_ge(kr_read, B)
                probs_turn(B - 1, 1)
                pe.wait_ge(o_cp, B - 1)
                o_product(B - 1, 1)
                pe.wait_ge(o_cp, B)
                pe.wait_ge(c_add, TILES - 1)
                out_product(1, 0, H)


def self_attention(nc, ctx, x_all, ident, wsum, wt, wsc, Sq, Sk, Sv, So, Wffn, tab_s):
    def sb(name, shape, dt=F32):
        return ctx.enter_context(nc.sbuf_tensor(name, shape, dt))

    def sem(name):
        return ctx.enter_context(nc.semaphore(name))

    G = SH // 4
    wqkv = sb("self_wqkv", [P, 2, 3, DC, D], F32R)
    raw = wt[:, :, D * F // P // 2:].bitcast(F32)
    wo = sb("self_wo", [P, DC, D])
    ts = sb("ts", [P, 3 * SD // 2 + LQ])
    ones = sb("ones", [P, P])
    half = sb("half", [P, 2, 3])
    wmean = sb("wmean", [P, 3])
    wraw = sb("wraw", [P, 2, 3, D])
    wneg = sb("wneg", [P, 3, D], BF16)
    xn = sb("s_xn", [P, 2, D])
    xnt = sb("s_xnt", [P, 2, DC, P], F32R)
    rc = sb("s_rc", [P, 2, D])
    rs_ = sb("s_rs", [P, 2, D])
    qk = sb("s_qk", [P, 2, D])
    qbd = sb("s_qbd", [P, G * TB, P])
    kt = sb("s_kt", [P, G, P])
    vb = sb("s_v", [P, 2, D])
    pr = sb("s_pr", [P, G * TB, LQ])
    mx = sb("s_mx", [P, G * TB])
    tot = sb("s_tot", [P, G * TB])
    rinv = sb("s_rinv", [P, G * TB])
    pt = sb("s_pt", [P, G, P])
    ot = sb("s_ot", [P, G, TB, LQ])
    stats = sb("s_stats", [P, 6])
    mv = sb("s_mv", [P, 2])
    veps = sb("s_veps", [P, 1])
    rstd = sb("s_rstd", [P, 1])
    power = sb("s_power", [P, 1])
    carrier = sb("s_carrier", [P, 1])

    w_in = [sem(f"self_weights_loaded{i}") for i in range(3)]
    t_in = sem("self_tables_loaded")
    wh_s, wl_s = sem("self_weights_high"), sem("self_weights_low")
    xl_s = sem("s_xn_low")
    o_in = sem("self_out_weights_loaded")
    wr_in = [sem("ffn_raw_loaded0"), sem("ffn_raw_loaded1")]
    set_s = sem("self_constants_set")
    mean_done, mean_cp, mean_c2, mean_s = sem("mean_done"), sem("mean_copied"), sem("mean_clipped"), sem("mean_ready")
    wneg_s, wt_s = sem("ffn_negative_ready"), sem("ffn_ternary_ready")
    bn_s, mv_s, ve_s, rstd_s, xn_s = (sem("s_" + k) for k in ("bn", "mean_var", "var_eps", "rstd", "xn_ready"))
    xt_done, xt_cp = sem("s_xn_turned"), sem("s_xn_turned_copied")
    qk_done, qk_read, qk_sum = sem("s_qk_done"), sem("s_qk_read"), sem("s_qk_added")
    v_done, v_cp = sem("s_v_done"), sem("s_v_copied")
    qt_done, qbd_d, qbd_a = sem("s_q_turned"), sem("s_qbd_dve"), sem("s_qbd_act")
    kt_done, kt_cp = sem("s_k_turned"), sem("s_k_turned_copied")
    sc_done, sc_read, mx_s, sub_s = sem("s_scores_done"), sem("s_scores_read"), sem("s_max_ready"), sem("s_shifted")
    exp_s, tot_s, rinv_s, pr_s = sem("s_exp_done"), sem("s_total"), sem("s_rinv"), sem("s_probs_ready")
    pt_done, pt_cp = sem("s_probs_turned"), sem("s_probs_turned_copied")
    av_done, ot_d, ot_a = sem("s_values_done"), sem("s_values_dve"), sem("s_values_act")
    y_done, res_s = sem("s_out_done"), sem("s_out_added")

    with ExitStack() as pctx:
        ps = pctx.enter_context(nc.psum_tensor("s_ps", [P, 8, 512], F32))
        XT, QT = ps[:, 7, :], ps[:, 0, :]
        QK = ps[:, 1:3, :]
        AV = ps[:, 3:7, :].rearrange("p b (g h q) -> p b g h q", g=G, h=4)
        KTB, YB, SB = ps[:, 2, :], ps[:, 4, :], ps[:, 5, :]
        PT, V = ps[:, 7, :], ps[:, 1, :]

        def steps(p):
            for u in range(2):
                yield u, 2 * p + u

        with nc.Block() as block:
            @block.sync
            def _(sp):
                for i, src in enumerate((Sq, Sk, Sv)):
                    sp.dma_start(raw[:, i, :], src.rearrange("p c n -> p (c n)")).then_inc(w_in[i], 16)
                sp.dma_start(ts[:], tab_s).then_inc(t_in, 16)
                sp.dma_start(wo[:], So).then_inc(o_in, 16)

                def load(p):
                    for u, n in steps(p):
                        if not isinstance(p, int):
                            sp.wait_ge(wt_s, n - 1)
                        sp.dma_start(wraw[:, u, :, :], Wffn[:, :, bass.ds(n * D, D)]).then_inc(wr_in[u], 16)
                load(0)
                with sp.Fori(1, PAIRS) as p:
                    load(p)

            @block.gpsimd
            def _(pool):
                pool.memset(power[:], -0.5)
                pool.memset(ones[:], 1.0).then_inc(set_s, 1)
                pool.memset(qbd[:], 0.0).then_inc(set_s, 1)
                pool.wait_ge(set_s, 2)

                def rsqrt(n):
                    pool.wait_ge(ve_s, n + 1)
                    pool.tensor_tensor(rstd[:], veps[:], power[:], ALU.pow).then_inc(rstd_s, 1)

                def scale_probs(n):
                    pool.wait_ge(rinv_s, n + 1)
                    pool.tensor_tensor(pr[:], pr[:], rinv[:].rearrange("p (a b) -> p a b", b=1).to_broadcast([P, G * TB, LQ]),
                                       ALU.mult).then_inc(pr_s, 1)

                def add_rope(n):
                    after(pool, qt_done, n)
                    after(pool, kt_done, n)
                    for i in range(2):
                        pool.wait_ge(qk_read, 2 * n + 1 + i)
                        pool.tensor_tensor(qk[:, i, :], rc[:, i, :], rs_[:, i, :], ALU.add).then_inc(qk_sum, 1)

                def pair(p):
                    for u, n in steps(p):
                        if not (isinstance(p, int) and n == 0):
                            scale_probs(n - 1)
                        add_rope(n)
                        if not (isinstance(p, int) and n == TILES - 1):
                            rsqrt(n + 1)
                rsqrt(0)
                pair(0)
                with pool.Fori(1, PAIRS - 1) as p:
                    pair(p)
                pair(PAIRS - 1)
                scale_probs(TILES - 1)

            @block.vector
            def _(dve):
                def norm_stats(n):
                    dve.bn_stats(stats[:], x_all[:, bass.ds(n, 1), :]).then_inc(bn_s, 1)
                    dve.wait_ge(bn_s, n + 1)
                    dve.memset(carrier[:], 0.0)
                    dve.bn_aggr(mv[:], stats[:]).then_inc(mv_s, 1)
                    dve.wait_ge(mv_s, n + 1)
                    dve.tensor_scalar(veps[:], mv[:, 1:2], EPS, None, ALU.add).then_inc(ve_s, 1)

                def norm(n, u):
                    after(dve, xt_done, n - 1)
                    dve.wait_ge(rstd_s, n + 1)
                    dve.tensor_scalar(xn[:, u, :], x_all[:, bass.ds(n, 1), :], mv[:, 0:1], rstd[:, 0:1],
                                      ALU.subtract, ALU.mult).then_inc(xn_s, 1)

                def low_tokens(n):
                    dve.wait_ge(xt_cp, n + 1)
                    dve.tensor_tensor(xnt[:, 1, :, :].rearrange("p c q -> p (c q)"), XT,
                                      xnt[:, 0, :, :].rearrange("p c q -> p (c q)").bitcast(F32), ALU.subtract).then_inc(xl_s, 1)

                def rope(n):
                    for i in range(2):
                        dve.wait_ge(qk_done, 2 * n + 1 + i)
                        after(dve, qk_sum, 2 * n - 1 + i)
                        q = QK[:, i, :].rearrange("p (g f) -> p g f", f=SD // 2)
                        qh = QK[:, i, :].rearrange("p (h a f) -> p h a f", a=2, f=SD // 2)
                        sh = rs_[:, i, :].rearrange("p (h a f) -> p h a f", a=2, f=SD // 2)
                        tab = lambda k, m: ts[:, k * SD // 2:(k + 1) * SD // 2].rearrange("p (a f) -> p a f", a=1).to_broadcast([P, m, SD // 2])
                        dve.tensor_tensor(rc[:, i, :].rearrange("p (g f) -> p g f", f=SD // 2), q, tab(0, 2 * SH), ALU.mult)
                        dve.tensor_tensor(sh[:, :, 0, :], qh[:, :, 1, :], tab(1, SH), ALU.mult)
                        dve.tensor_tensor(sh[:, :, 1, :], qh[:, :, 0, :], tab(2, SH), ALU.mult).then_inc(qk_read, 1)

                def softmax_front(n):
                    dve.wait_ge(sc_done, n + 1)
                    after(dve, pt_done, n)
                    dve.tensor_tensor(pr[:], SB.rearrange("p (a k) -> p a k", k=LQ),
                                      ts[:, 3 * SD // 2:].rearrange("p (a k) -> p a k", a=1).to_broadcast([P, G * TB, LQ]),
                                      ALU.add).then_inc(sc_read, 1)
                    dve.wait_ge(sc_read, n + 1)
                    dve.tensor_reduce(mx[:], pr[:], AX.X, ALU.max).then_inc(mx_s, 1)
                    dve.wait_ge(mx_s, n + 1)
                    dve.tensor_tensor(pr[:], pr[:], mx[:].rearrange("p (a b) -> p a b", b=1).to_broadcast([P, G * TB, LQ]),
                                      ALU.subtract).then_inc(sub_s, 1)

                def softmax_back(n):
                    dve.wait_ge(exp_s, n + 1)
                    dve.tensor_reduce(tot[:], pr[:], AX.X, ALU.add).then_inc(tot_s, 1)
                    dve.wait_ge(tot_s, n + 1)
                    dve.reciprocal(rinv[:], tot[:]).then_inc(rinv_s, 1)

                def values(n):
                    dve.wait_ge(av_done, n + 1)
                    after(dve, y_done, n)
                    for h in (0, 1):
                        r = slice(32 * h, 32 * h + 32)
                        last = dve.tensor_copy(ot[r, :, :, :], AV[r, :, :, h, :].rearrange("p b g q -> p g b q"))
                    last.then_inc(ot_d, 1)

                def queries(n):
                    dve.wait_ge(qt_done, n + 1)
                    after(dve, sc_done, n)
                    for h in (0, 1):
                        r = slice(32 * h, 32 * h + 32)
                        last = dve.tensor_copy(qbd[r, :, 32 * h:32 * h + 32], QT[r, :].rearrange("p (a q) -> p a q", q=LQ))
                    last.then_inc(qbd_d, 1)

                def residual(n):
                    dve.wait_ge(y_done, n + 1)
                    dve.tensor_tensor(x_all[:, bass.ds(n, 1), :], YB, x_all[:, bass.ds(n, 1), :], ALU.add).then_inc(res_s, 1)

                def ternary(p, u, n):
                    dve.wait_ge(wr_in[u], 16 * p + 16)
                    for i in range(3):
                        last = dve.tensor_scalar(wneg[:, i, :], wraw[:, u, i, :], half[:, 1, i:i + 1], None, ALU.is_lt)
                    last.then_inc(wneg_s, 1)
                    dve.wait_ge(wneg_s, n + 1)
                    for i in range(3):
                        last = dve.scalar_tensor_tensor(wt[:, i, bass.ds(n * D, D)], wraw[:, u, i, :], half[:, 0, i:i + 1],
                                                        wneg[:, i, :], ALU.is_gt, ALU.subtract)
                    last.then_inc(wt_s, 1)

                def pair(p):
                    for u, n in steps(p):
                        more = not (isinstance(p, int) and n == TILES - 1)
                        back = not (isinstance(p, int) and n == 0)
                        if back:
                            softmax_back(n - 1)
                        if more:
                            norm_stats(n + 1)
                        rope(n)
                        if more:
                            norm(n + 1, 1 - u)
                        if back:
                            values(n - 1)
                        queries(n)
                        if more:
                            low_tokens(n + 1)
                        ternary(p, u, n)
                        if back:
                            residual(n - 1)
                        softmax_front(n)

                norm_stats(0)
                norm(0, 0)
                dve.wait_ge(mean_done, 1)
                dve.tensor_scalar(wmean[:], ps[:, 7, 0:3], 1.0 / (D * F), EPS, ALU.mult, ALU.max).then_inc(mean_cp, 1)
                dve.wait_ge(mean_cp, 1)
                dve.tensor_scalar(half[:, 0, :], wmean[:], 0.5, None, ALU.mult)
                dve.tensor_scalar(half[:, 1, :], wmean[:], -0.5, None, ALU.mult)
                dve.tensor_scalar(wsc[:], wmean[:], 1.0 / 127.0, None, ALU.mult).then_inc(mean_s, 1)
                dve.wait_ge(mean_s, 1)
                for i in range(3):
                    dve.wait_ge(wh_s, i + 1)
                    if i == 1:
                        low_tokens(0)
                    dve.tensor_tensor(wqkv[:, 1, i, :, :].rearrange("p c n -> p (c n)"), raw[:, i, :],
                                      wqkv[:, 0, i, :, :].rearrange("p c n -> p (c n)").bitcast(F32), ALU.subtract).then_inc(wl_s, 1)
                dve.wait_ge(t_in, 16)
                dve.wait_ge(wl_s, 3)
                pair(0)
                with dve.Fori(1, PAIRS - 1) as p:
                    pair(p)
                pair(PAIRS - 1)
                softmax_back(TILES - 1)
                values(TILES - 1)
                residual(TILES - 1)

            @block.scalar
            def _(act):
                def tokens(n):
                    act.wait_ge(xt_done, n + 1)
                    after(act, v_done, n)
                    act.copy(xnt[:, 0, :, :].rearrange("p c q -> p (c q)"), XT).then_inc(xt_cp, 1)

                def probs(n):
                    act.wait_ge(pt_done, n + 1)
                    after(act, av_done, n)
                    act.copy(pt[:].rearrange("p g q -> p (g q)"), PT).then_inc(pt_cp, 1)

                def values(n):
                    act.wait_ge(av_done, n + 1)
                    after(act, y_done, n)
                    for h in (2, 3):
                        r = slice(32 * h, 32 * h + 32)
                        last = act.copy(ot[r, :, :, :], AV[r, :, :, h, :].rearrange("p b g q -> p g b q"))
                    last.then_inc(ot_a, 1)

                def pair(p):
                    for u, n in steps(p):
                        back = not (isinstance(p, int) and n == 0)
                        if back:
                            probs(n - 1)
                        act.wait_ge(v_done, n + 1)
                        after(act, av_done, n - 1)
                        act.copy(vb[:, u, :], V).then_inc(v_cp, 1)
                        if back:
                            values(n - 1)
                        act.wait_ge(qt_done, n + 1)
                        after(act, sc_done, n)
                        for h in (2, 3):
                            r = slice(32 * h, 32 * h + 32)
                            last = act.copy(qbd[r, :, 32 * h:32 * h + 32], QT[r, :].rearrange("p (a q) -> p a q", q=LQ))
                        last.then_inc(qbd_a, 1)
                        act.wait_ge(kt_done, n + 1)
                        act.copy(kt[:].rearrange("p g q -> p (g q)"), KTB).then_inc(kt_cp, 1)
                        if not (isinstance(p, int) and n == TILES - 1):
                            tokens(n + 1)
                        act.wait_ge(sub_s, n + 1)
                        act.activation(pr[:], pr[:], ACT.Exp, scale=SSCALE).then_inc(exp_s, 1)
                act.wait_ge(set_s, 2)
                for i in range(3):
                    act.wait_ge(w_in[i], 16)
                    act.copy(wqkv[:, 0, i, :, :].rearrange("p c n -> p (c n)"), raw[:, i, :]).then_inc(wh_s, 1)
                    if i == 0:
                        tokens(0)
                pair(0)
                with act.Fori(1, PAIRS - 1) as p:
                    pair(p)
                pair(PAIRS - 1)
                probs(TILES - 1)
                values(TILES - 1)

            @block.tensor
            def _(pe):
                def project(bank, i):
                    for k, (a, b) in enumerate(SPLIT):
                        for c in range(DC):
                            last = pe.matmul(bank, xnt[:, a, c, :], wqkv[:, b, i, c, :], start=(k + c == 0), stop=(k + c == 2 + DC - 1))
                    return last

                def tokens_turn(n, u):
                    pe.wait_ge(xn_s, n + 1)
                    after(pe, pt_cp, n - 1)
                    for c in range(DC):
                        last = pe.transpose(XT[:, c * P:(c + 1) * P], xn[:, u, c * P:(c + 1) * P], ident[:])
                    last.then_inc(xt_done, 1)

                def probs_turn(n):
                    pe.wait_ge(pr_s, n + 1)
                    if not (isinstance(n, int) and n == TILES - 1):
                        pe.wait_ge(xl_s, n + 2)
                    for g in range(G):
                        last = pe.transpose(PT[:, g * P:(g + 1) * P], pr[:, TB * g:TB * g + TB, :].rearrange("p b k -> p (b k)"), ident[:])
                    last.then_inc(pt_done, 1)

                def value_product(n, u):
                    pe.wait_ge(pt_cp, n + 1)
                    pe.wait_ge(v_cp, n + 1)
                    after(pe, res_s, n)
                    pe.wait_ge(sc_read, n + 1)
                    after(pe, ot_d, n)
                    after(pe, ot_a, n)
                    for g in range(G):
                        for b in range(TB):
                            r = slice(32 * b, 32 * b + 32)
                            last = pe.matmul(ps[:, 3 + b, g * P:(g + 1) * P], vb[r, u, g * P:(g + 1) * P], pt[r, g, :],
                                             start=True, stop=True)
                    last.then_inc(av_done, 1)

                def out_product(n):
                    pe.wait_ge(ot_d, n + 1)
                    pe.wait_ge(ot_a, n + 1)
                    for g in range(G):
                        last = pe.matmul(YB, ot[:, g, :, :].rearrange("p b q -> p (b q)"), wo[:, g, :], start=(g == 0), stop=(g == G - 1))
                    last.then_inc(y_done, 1)

                def pair(p):
                    for u, n in steps(p):
                        back = not (isinstance(p, int) and n == 0)
                        pe.wait_ge(xl_s, n + 1)
                        for i in range(2):
                            if isinstance(p, int) and n == 0:
                                pe.wait_ge(wl_s, i + 1)
                            after(pe, qk_read, 2 * n - 1 + i)
                            after(pe, v_cp if i == 0 else kt_cp, n)
                            project(QK[:, i, :], i).then_inc(qk_done, 1)
                        if back:
                            probs_turn(n - 1)
                        pe.wait_ge(qk_read, 2 * n + 1)
                        if isinstance(p, int) and n == 0:
                            pe.wait_ge(wl_s, 3)
                        project(V, 2).then_inc(v_done, 1)
                        if back:
                            value_product(n - 1, 1 - u)
                        pe.wait_ge(qk_sum, 2 * n + 2)
                        after(pe, qbd_d, n)
                        after(pe, qbd_a, n)
                        for g in range(G):
                            last = pe.transpose(QT[:, g * P:(g + 1) * P], qk[:, 0, g * P:(g + 1) * P], ident[:])
                        last.then_inc(qt_done, 1)
                        for g in range(G):
                            last = pe.transpose(KTB[:, g * P:(g + 1) * P], qk[:, 1, g * P:(g + 1) * P], ident[:])
                        last.then_inc(kt_done, 1)
                        if not (isinstance(p, int) and n == TILES - 1):
                            tokens_turn(n + 1, 1 - u)
                        if back:
                            if isinstance(p, int) and n == 1:
                                pe.wait_ge(o_in, 16)
                            out_product(n - 1)
                        pe.wait_ge(qbd_d, n + 1)
                        pe.wait_ge(qbd_a, n + 1)
                        pe.wait_ge(kt_cp, n + 1)
                        for a in range(G * TB):
                            g, b = a // TB, a % TB
                            last = pe.matmul(SB[:, a * LQ:(a + 1) * LQ], qbd[:, a, :], kt[:, g, b * LQ:(b + 1) * LQ],
                                             start=True, stop=True)
                        last.then_inc(sc_done, 1)
                pe.wait_ge(set_s, 2)
                pe.matmul(ps[:, 7, 0:4], ones[:], wsum[:, 0:4], start=True, stop=True).then_inc(mean_done, 1)
                pe.wait_ge(mean_cp, 1)
                tokens_turn(0, 0)
                pair(0)
                with pe.Fori(1, PAIRS - 1) as p:
                    pair(p)
                pair(PAIRS - 1)
                probs_turn(TILES - 1)
                value_product(TILES - 1, 1)
                out_product(TILES - 1)


def feed_forward(nc, ctx, x_all, ident, wt, wsc, out):
    def sb(name, shape, dt=F32):
        return ctx.enter_context(nc.sbuf_tensor(name, shape, dt))

    def sem(name):
        return ctx.enter_context(nc.semaphore(name))

    NCH = F // D
    identb = sb("identb", [P, P], BF16)
    magic = sb("magic", [P, 1])
    negmagic = sb("negmagic", [P, 1])
    xn = sb("f_xn", [P, D])
    xr = sb("f_xr", [P, D])
    xq = sb("f_xq", [P, D], BF16)
    xqt = sb("f_xqt", [P, DC, P], BF16)
    sg = sb("f_sg", [P, 2, D])
    hb = sb("f_h", [P, F])
    hq = sb("f_hq", [P, F], BF16)
    hqt = sb("f_hqt", [P, FCH, P], BF16)
    xm, xm2, xinv, x127 = (sb("f_" + k, [P, 1]) for k in ("xm", "xm2", "xinv", "x127"))
    gu = sb("f_gu", [P, 2, 2])
    hm4 = sb("f_hm4", [P, NCH])
    hm, hm2, hinv, h127 = (sb("f_" + k, [P, 1]) for k in ("hm", "hm2", "hinv", "h127"))
    ysc = sb("f_ysc", [P, 2])
    stats = sb("f_stats", [P, 6])
    mv = sb("f_mv", [P, 2])
    veps = sb("f_veps", [P, 1])
    rstd = sb("f_rstd", [P, 1])
    power = sb("f_power", [P, 1])
    carrier = sb("f_carrier", [P, 1])

    set_s = sem("f_constants_set")
    idb_s = sem("f_ident_ready")
    bn_s, mv_s, ve_s, rstd_s, xn_s = (sem("f_" + k) for k in ("bn", "mean_var", "var_eps", "rstd", "xn_ready"))
    xm_s, xm2_s, xinv_s, x127_s, xr_s, xq_s = (sem("f_" + k) for k in ("xmax", "xclip", "xinv", "x127", "xrounded", "xq"))
    xt_done, xt_cp = sem("f_x_turned"), sem("f_x_turned_copied")
    g_done, u_done, sg_s, h_s = sem("f_gate_done"), sem("f_up_done"), sem("f_silu_ready"), sem("f_h_ready")
    hm4_s, hm_s, hm2_s, hinv_s, h127_s, hr_s, hq_s = (sem("f_" + k) for k in ("hmax4", "hmax", "hclip", "hinv", "h127", "hrounded", "hq"))
    ht_done, ht_d, ht_a = sem("f_h_turned"), sem("f_h_turned_dve"), sem("f_h_turned_act")
    y_done, res_s, out_s = sem("f_down_done"), sem("f_added"), sem("out_stored")

    with ExitStack() as pctx:
        GB = pctx.enter_context(nc.psum_tensor("f_g", [P, 2, D], F32))
        UB = pctx.enter_context(nc.psum_tensor("f_u", [P, 2, D], F32))
        YB = pctx.enter_context(nc.psum_tensor("f_y", [P, D], F32))
        XT = pctx.enter_context(nc.psum_tensor("f_xt", [P, 2 * D], BF16))
        HT = pctx.enter_context(nc.psum_tensor("f_ht", [P, F], BF16))

        def steps(p):
            for u in range(2):
                yield u, 2 * p + u

        with nc.Block() as block:
            @block.sync
            def _(sp):
                with sp.Fori(0, TILES) as n:
                    sp.wait_ge(res_s, n + 1)
                    sp.dma_start(out[bass.ds(n * P, P), :], x_all[:, bass.ds(n, 1), :].rearrange("p a d -> p (a d)")).then_inc(out_s, 16)
                sp.wait_ge(out_s, 16 * TILES)

            @block.gpsimd
            def _(pool):
                pool.tensor_copy(identb[:], ident[:]).then_inc(idb_s, 1)
                pool.memset(magic[:], MAGIC).then_inc(set_s, 1)
                pool.memset(negmagic[:], -MAGIC).then_inc(set_s, 1)
                pool.memset(power[:], -0.5).then_inc(set_s, 1)
                pool.wait_ge(set_s, 3)

                def row(n):
                    pool.wait_ge(ve_s, n + 1)
                    pool.tensor_tensor(rstd[:], veps[:], power[:], ALU.pow).then_inc(rstd_s, 1)
                    pool.wait_ge(xr_s, n + 1)
                    after(pool, xt_done, n)
                    pool.tensor_tensor(xq[:], xr[:], negmagic[:].to_broadcast([P, D]), ALU.add).then_inc(xq_s, 1)
                row(0)
                with pool.Fori(1, TILES) as n:
                    row(n)

            @block.vector
            def _(dve):
                def norm_stats(n):
                    dve.bn_stats(stats[:], x_all[:, bass.ds(n, 1), :]).then_inc(bn_s, 1)
                    dve.wait_ge(bn_s, n + 1)
                    dve.memset(carrier[:], 0.0)
                    dve.bn_aggr(mv[:], stats[:]).then_inc(mv_s, 1)
                    dve.wait_ge(mv_s, n + 1)
                    dve.tensor_scalar(veps[:], mv[:, 1:2], EPS, None, ALU.add).then_inc(ve_s, 1)

                def norm(n):
                    dve.wait_ge(rstd_s, n + 1)
                    after(dve, xr_s, n)
                    dve.tensor_scalar(xn[:], x_all[:, bass.ds(n, 1), :], mv[:, 0:1], rstd[:, 0:1],
                                      ALU.subtract, ALU.mult).then_inc(xn_s, 1)
                    dve.wait_ge(xn_s, n + 1)
                    dve.tensor_reduce(xm[:], xn[:], AX.X, ALU.max, apply_absolute_value=True).then_inc(xm_s, 1)

                def scale_x(n, u):
                    dve.wait_ge(xm_s, n + 1)
                    dve.tensor_scalar(xm2[:], xm[:], EPS, None, ALU.max).then_inc(xm2_s, 1)
                    dve.wait_ge(xm2_s, n + 1)
                    dve.tensor_scalar(gu[:, u, :], wsc[:, 0:2], xm2[:, 0:1], None, ALU.mult)
                    dve.reciprocal(xinv[:], xm2[:]).then_inc(xinv_s, 1)
                    dve.wait_ge(xinv_s, n + 1)
                    dve.tensor_scalar(x127[:], xinv[:], 127.0, None, ALU.mult).then_inc(x127_s, 1)

                def hidden(n, c, u):
                    dve.wait_ge(sg_s, 4 * n + c + 1)
                    dve.wait_ge(u_done, 4 * n + c + 1)
                    if c == 0:
                        after(dve, hq_s, n)
                    dve.scalar_tensor_tensor(hb[:, c * D:(c + 1) * D], UB[:, c % 2, :], gu[:, u, 1:2], sg[:, c % 2, :],
                                             ALU.mult, ALU.mult).then_inc(h_s, 1)
                    dve.wait_ge(h_s, 4 * n + c + 1)
                    dve.tensor_reduce(hm4[:, c:c + 1], hb[:, c * D:(c + 1) * D], AX.X, ALU.max, apply_absolute_value=True).then_inc(hm4_s, 1)

                def scale_h(n, u):
                    dve.wait_ge(hm4_s, 4 * n + 4)
                    dve.tensor_reduce(hm[:], hm4[:], AX.X, ALU.max).then_inc(hm_s, 1)
                    dve.wait_ge(hm_s, n + 1)
                    dve.tensor_scalar(hm2[:], hm[:], EPS, None, ALU.max).then_inc(hm2_s, 1)
                    dve.wait_ge(hm2_s, n + 1)
                    dve.tensor_scalar(ysc[:, u:u + 1], wsc[:, 2:3], hm2[:, 0:1], None, ALU.mult)
                    dve.reciprocal(hinv[:], hm2[:]).then_inc(hinv_s, 1)
                    dve.wait_ge(hinv_s, n + 1)
                    dve.tensor_scalar(h127[:], hinv[:], 127.0, None, ALU.mult).then_inc(h127_s, 1)

                def quantise_h(n):
                    dve.wait_ge(hr_s, n + 1)
                    after(dve, ht_done, n)
                    dve.tensor_scalar(hq[:], hb[:], MAGIC, None, ALU.subtract).then_inc(hq_s, 1)

                def copy_turned(n):
                    dve.wait_ge(ht_done, n + 1)
                    after(dve, y_done, n)
                    dve.tensor_copy(hqt[:, 0:8, :].rearrange("p c q -> p (c q)"), HT[:, 0:8 * P]).then_inc(ht_d, 1)

                def residual(n, u):
                    dve.wait_ge(y_done, n + 1)
                    dve.scalar_tensor_tensor(x_all[:, bass.ds(n, 1), :].rearrange("p a d -> p (a d)"), YB[:], ysc[:, u:u + 1],
                                             x_all[:, bass.ds(n, 1), :].rearrange("p a d -> p (a d)"), ALU.mult, ALU.add).then_inc(res_s, 1)

                def pair(p):
                    for u, n in steps(p):
                        back = not (isinstance(p, int) and n == 0)
                        if back:
                            quantise_h(n - 1)
                        hidden(n, 0, u)
                        hidden(n, 1, u)
                        hidden(n, 2, u)
                        if back:
                            copy_turned(n - 1)
                        hidden(n, 3, u)
                        scale_h(n, u)
                        if not (isinstance(p, int) and p == PAIRS - 1):
                            norm_stats(n + 2)
                            norm(n + 2)
                            scale_x(n + 2, u)
                        if back:
                            residual(n - 1, 1 - u)

                for n in range(2):
                    norm_stats(n)
                    norm(n)
                    scale_x(n, n)
                pair(0)
                with dve.Fori(1, PAIRS - 1) as p:
                    pair(p)
                pair(PAIRS - 1)
                quantise_h(TILES - 1)
                copy_turned(TILES - 1)
                residual(TILES - 1, 1)

            @block.scalar
            def _(act):
                def round_x(n):
                    act.wait_ge(x127_s, n + 1)
                    after(act, xq_s, n)
                    act.activation(xr[:], xn[:], ACT.Identity, bias=magic[:, 0:1], scale=x127[:, 0:1]).then_inc(xr_s, 1)

                def copy_x(n):
                    act.wait_ge(xt_done, n + 1)
                    after(act, u_done, 4 * n)
                    act.copy(xqt[:].rearrange("p c q -> p (c q)"), XT[:, 0:D]).then_inc(xt_cp, 1)

                def copy_turned(n):
                    act.wait_ge(ht_done, n + 1)
                    after(act, y_done, n)
                    act.copy(hqt[:, 8:16, :].rearrange("p c q -> p (c q)"), HT[:, 8 * P:16 * P]).then_inc(ht_a, 1)

                def pair(p):
                    for u, n in steps(p):
                        for c in range(NCH):
                            if c == 3 and not (isinstance(p, int) and n == 0):
                                copy_turned(n - 1)
                            act.wait_ge(g_done, 4 * n + c + 1)
                            after(act, h_s, 4 * n + c - 1)
                            act.activation(sg[:, c % 2, :], GB[:, c % 2, :], ACT.Silu, scale=gu[:, u, 0:1]).then_inc(sg_s, 1)
                        if not (isinstance(p, int) and n == TILES - 1):
                            copy_x(n + 1)
                        act.wait_ge(h127_s, n + 1)
                        act.activation(hb[:], hb[:], ACT.Identity, bias=magic[:, 0:1], scale=h127[:, 0:1]).then_inc(hr_s, 1)
                        if not (isinstance(p, int) and p == PAIRS - 1):
                            round_x(n + 2)
                act.wait_ge(set_s, 3)
                round_x(0)
                round_x(1)
                copy_x(0)
                pair(0)
                with act.Fori(1, PAIRS - 1) as p:
                    pair(p)
                pair(PAIRS - 1)
                copy_turned(TILES - 1)

            @block.tensor
            def _(pe):
                def turn_x(n):
                    pe.wait_ge(xq_s, n + 1)
                    after(pe, xt_cp, n)
                    for c in range(DC):
                        last = pe.transpose(XT[:, c * P:(c + 1) * P], xq[:, c * P:(c + 1) * P], identb[:])
                    last.then_inc(xt_done, 1)

                def turn_h(n):
                    pe.wait_ge(hq_s, n + 1)
                    after(pe, ht_d, n)
                    after(pe, ht_a, n)
                    for c in range(FCH):
                        last = pe.transpose(HT[:, c * P:(c + 1) * P], hq[:, c * P:(c + 1) * P], identb[:])
                    last.then_inc(ht_done, 1)

                def down(n):
                    pe.wait_ge(ht_d, n + 1)
                    pe.wait_ge(ht_a, n + 1)
                    after(pe, res_s, n)
                    for c in range(FCH):
                        last = pe.matmul(YB[:], hqt[:, c, :], wt[:, 2, c * D:(c + 1) * D], start=(c == 0), stop=(c == FCH - 1))
                    last.then_inc(y_done, 1)

                def pair(p):
                    for u, n in steps(p):
                        pe.wait_ge(xt_cp, n + 1)
                        for c in range(NCH):
                            if c == 3 and not (isinstance(p, int) and n == 0):
                                turn_h(n - 1)
                            after(pe, sg_s, 4 * n + c - 1)
                            for k in range(DC):
                                last = pe.matmul(GB[:, c % 2, :], xqt[:, k, :], wt[:, 0, k * F + c * D:k * F + (c + 1) * D],
                                                 start=(k == 0), stop=(k == DC - 1))
                            last.then_inc(g_done, 1)
                            after(pe, h_s, 4 * n + c - 1)
                            for k in range(DC):
                                last = pe.matmul(UB[:, c % 2, :], xqt[:, k, :], wt[:, 1, k * F + c * D:k * F + (c + 1) * D],
                                                 start=(k == 0), stop=(k == DC - 1))
                            last.then_inc(u_done, 1)
                        if not (isinstance(p, int) and n == TILES - 1):
                            turn_x(n + 1)
                        if not (isinstance(p, int) and n == 0):
                            down(n - 1)
                pe.wait_ge(idb_s, 1)
                turn_x(0)
                pair(0)
                with pe.Fori(1, PAIRS - 1) as p:
                    pair(p)
                pair(PAIRS - 1)
                turn_h(TILES - 1)
                down(TILES - 1)


def kernel(**inputs):
    import numpy as np
    import concourse.bacc as bacc
    from concourse.bass_utils import run_bass_kernel_spmd

    f32 = np.float32
    a = {k: np.asarray(v) for k, v in inputs.items()}
    g = lambda name: a["L0_" + name]
    rows = lambda w: np.ascontiguousarray(w.reshape(-1, P, w.shape[1]).transpose(1, 0, 2))
    heads_T = lambda w: np.ascontiguousarray(w.reshape(w.shape[0], H, HD).transpose(2, 1, 0))
    inv = (f32(1.0) / f32(10000.0) ** (np.arange(R // 2, dtype=f32) / f32(R // 2))).astype(f32)
    ang = np.arange(LK, dtype=f32)[None, :] * inv[:, None]
    tab_k = np.concatenate([np.cos(ang), np.cos(ang), -np.sin(ang), np.sin(ang)], 0).astype(f32)
    angq = (np.arange(P) % LQ).astype(f32)[:, None] * inv
    tab_q = np.stack([np.cos(angq), -np.sin(angq), np.sin(angq)], 1).astype(f32)
    invs = np.exp(f32(-np.log(10000.0)) * np.arange(0, SD, 2, dtype=f32) / f32(SD)).astype(f32)
    angs = (np.arange(P) % LQ).astype(f32)[:, None] * invs
    causal = np.where(np.arange(LQ)[None, :] <= (np.arange(P) % LQ)[:, None], 0.0, -1e30)
    tab_s = np.concatenate([np.cos(angs), -np.sin(angs), np.sin(angs), causal], 1).astype(f32)
    tab_i = np.ascontiguousarray(np.broadcast_to(np.arange(LK, dtype=f32), (P, LK)))
    swap = (np.arange(R) + R // 2) % R
    wkr = g("xattn_W_kr")
    halves = np.concatenate([np.arange(0, SD, 2), np.arange(1, SD, 2)])
    order = (np.arange(SH)[:, None] * SD + halves).ravel()
    ffn = [g("ffn_w_gate").T, g("ffn_w_up").T, g("ffn_w_down").T]
    arrays = {
        "x": rows(a["x"].reshape(B * LQ, D)),
        "ctxT": np.ascontiguousarray(a["ctx_2048"].transpose(0, 2, 1).reshape(B, DC, P, LK)
                                     .transpose(0, 2, 1, 3)).reshape(B, P, DC * LK),
        "seg": np.ascontiguousarray(np.tile(a["itok_BxS_0_1023"].T, (TB, 1))),
        "Wkvc": rows(g("xattn_W_kvc")),
        "Wkr2": np.concatenate([wkr, wkr[:, swap]], 1),
        "Wdq": rows(g("xattn_W_dq")),
        "WuqT": heads_T(g("xattn_W_uq")),
        "WukT": heads_T(g("xattn_W_uk")),
        "WuvT": heads_T(g("xattn_W_uv")),
        "Wo": rows(g("xattn_W_o")),
        "Wqr": g("xattn_W_qr"),
        "Sq": rows(g("attn_Wq").T[:, order]),
        "Sk": rows(g("attn_Wk").T[:, order]),
        "Sv": rows(g("attn_Wv").T),
        "So": rows(g("attn_Wo").T),
        "Wffn": np.ascontiguousarray(np.stack([rows(w).reshape(P, -1) for w in ffn], 1)),
        "tab_k": tab_k, "tab_q": tab_q, "tab_s": tab_s, "tab_i": tab_i,
    }
    nc = bacc.Bacc("TRN2", target_bir_lowering=False, num_devices=1)
    aps = [nc.dram_tensor(f"in_{k}", v.shape, mybir.dt.from_np(v.dtype), kind="ExternalInput").ap()
           for k, v in arrays.items()]
    out = nc.dram_tensor("out", (B * LQ, D), F32, kind="ExternalOutput").ap()
    build(nc, *aps, out)
    r = run_bass_kernel_spmd(nc, [{f"in_{k}": np.ascontiguousarray(v) for k, v in arrays.items()}], core_ids=[0])
    return r.results[0]["out"].reshape(B, LQ, D)
```

```python
from contextlib import ExitStack

import concourse.bass as bass
from concourse import mybir

F32 = mybir.dt.float32
F32R = mybir.dt.float32r
BF16 = mybir.dt.bfloat16
I32 = mybir.dt.int32
ALU = mybir.AluOpType
ACT = mybir.ActivationFunctionType
AX = mybir.AxisListType

P = 128
D = 512
DC = D // P
B, LQ, LK = 64, 32, 257
TB = P // LQ
TILES = B // TB
PAIRS = TILES // 2
H, HD, QC, KVC, R = 16, 128, 192, 128, 64
QC1 = QC - P
LM = LK - 1
KT = LM // P
LOOKBACK = 8
XSCALE = float(1.0 / (HD + R) ** 0.5)
NEG = -float(2 ** 100)
EPS = 1e-5
SH, SD = 16, 32
SSCALE = float(1.0 / SD ** 0.5)
F = 2048
FCH = F // P
MAGIC = float(3 * 2 ** 22)


SPLIT = ((0, 0), (0, 1), (1, 0))


def after(eng, sem, count):
    if not isinstance(count, int) or count > 0:
        eng.wait_ge(sem, count)


def build(nc, x, ctxT, seg, Wkvc, Wkr2, Wdq, WuqT, WukT, WuvT, Wo, Wqr,
          Sq, Sk, Sv, So, Wffn, tab_k, tab_q, tab_s, tab_i, x_mid, out):
    with ExitStack() as top:
        def sbt(ctx, name, shape, dt=F32):
            return ctx.enter_context(nc.sbuf_tensor(name, shape, dt))

        ident = sbt(top, "ident", [P, P])
        wsum = sbt(top, "wsum", [P, 4])
        wsc = sbt(top, "wsc", [P, 3])

        with ExitStack() as ctx:
            cross_attention(nc, ctx, x_mid, ident, wsum, x, ctxT, seg, Wkvc, Wkr2, Wdq, WuqT, WukT,
                            WuvT, Wo, Wqr, Wffn, tab_k, tab_q, tab_i)
        x_all = sbt(top, "x_all", [P, TILES, D])
        wt = sbt(top, "wt", [P, 3, D * F // P], BF16)
        with ExitStack() as ctx:
            self_attention(nc, ctx, x_all, ident, wsum, wt, wsc, x_mid, Sq, Sk, Sv, So, Wffn, tab_s)
        with ExitStack() as ctx:
            feed_forward(nc, ctx, x_all, ident, wt, wsc, out)


def cross_attention(nc, ctx, x_mid, ident, wsum, x, ctxT, seg, Wkvc, Wkr2, Wdq, WuqT, WukT, WuvT,
                    Wo, Wqr, Wffn, tab_k, tab_q, tab_i):
    def sb(name, shape, dt=F32):
        return ctx.enter_context(nc.sbuf_tensor(name, shape, dt))

    def sem(name):
        return ctx.enter_context(nc.semaphore(name))

    wkvc = sb("wkvc", [P, 2, DC, KVC], F32R)
    wkr = sb("wkr", [P, 2, P], F32R)
    wqn0 = sb("wqn0", [P, H, KVC])
    wqn1 = sb("wqn1", [QC1, H, KVC])
    wqr0 = sb("wqr0", [P, 2, H * R], F32R)
    wqr1 = sb("wqr1", [P, H * R], F32R)
    wvo = sb("wvo", [P, H, D])
    tk = sb("tk", [P, LK])
    tq = sb("tq", [P, 3, R // 2])
    iota = sb("iota", [P, LK])
    seg_i = sb("seg_i", [P, B], I32)
    identr = sb("identr", [P, P], F32R)
    qc0 = sb("qc0", [P, TILES * P])
    qc1 = sb("qc1", [P, TILES * P])
    qcur0 = sb("qcur0", [P, 2, 2, P], F32R)
    qcur1 = sb("qcur1", [P, 2, P], F32R)
    qcur1l = sb("qcur1l", [P, 2, P], F32R)
    rc = sb("rc", [P, 4, R])
    rs_ = sb("rs_", [P, 4, R])
    qr2 = sb("qr2", [P, 4, 2, R])
    qn = sb("qn", [P, 2, 2, TB, 4, P], F32R)
    cx = sb("cx", [P, 2, DC * LK])
    cxs = sb("cxs", [P, 2, DC, LK + 1], F32R)
    kvt = sb("kvt", [P, 2, 2, LK + 1], F32R)
    kv_last = sb("kv_last", [P, 4])
    kvr = sb("kvr", [P, 2, 2, KT, KVC], F32R)
    kp = sb("kp", [P, LM])
    kp_last = sb("kp_last", [P, 1])
    cseg = sb("cseg", [P, 8])
    dist = sb("dist", [P, LK])
    mask = sb("mask", [P, LK])
    smask = sb("smask", [P, 1])
    pr = sb("pr", [P, 2, 4, LM])
    mx = sb("mx", [P, 4])
    nb = sb("nb", [P, 4])
    rsum = sb("rsum", [P, 4])
    e_last = sb("e_last", [P, 4])
    tot = sb("tot", [P, 4])
    rinv = sb("rinv", [P, 4])
    pt = sb("pt", [P, 2, KT, D], F32R)
    wch = sb("wch", [P, 2, 3, P])
    wpart = sb("wpart", [P, 3, B])
    xres = sb("xres", [P, D])
    arena = sb("arena", [P, 8192])
    qrt = arena[:, 0:4096].rearrange("p (u b g c) -> p u b g c", u=2, b=TB, g=4)
    yt = arena[:, 4096:8192].rearrange("p (u h c) -> p u h c", u=2, h=H)
    wo_st = arena[:].rearrange("p (h n) -> p h n", h=H)
    vo_flat = wvo[:].rearrange("p h n -> p (h n)")
    wuq_st = vo_flat[:, 0:H * QC].rearrange("p (h c) -> p h c", h=H)
    wuk_st = vo_flat[:, 4096:6144].rearrange("p (h c) -> p h c", h=H)
    wqr0_st, wqr1_st = vo_flat[:, 6144:7168], vo_flat[:, 7168:8192]
    pr_flat = pr[:].rearrange("p u g k -> p (u g k)")
    wkr_st = dist[:, 0:P]
    wkvc_st = qr2[:].rearrange("p k a r -> p (k a r)")
    xt_in = cx[:, 0, 0:2 * D].rearrange("p (u n) -> p u n", u=2)
    wdq = cx[:, 1, 0:DC * 2 * P].rearrange("p (c n) -> p c n", c=DC)
    xn = pr_flat[:, 0:2 * D].rearrange("p (u n) -> p u n", u=2)
    xnt = pr_flat[:, 2 * D:4 * D].rearrange("p (u c q) -> p u c q", u=2, c=DC)
    wuv_st = pr_flat.rearrange("p (h c) -> p h c", h=H)
    x_tail = cx[:, 0, 0:D]
    carrier = sb("carrier", [P, 1])
    carrier_p = sb("carrier_p", [P, 1])
    stats = sb("stats", [P, 6])
    mv = sb("mv", [P, 2])
    veps = sb("veps", [P, 1])
    rstd = sb("rstd", [P, 1])
    power = sb("power", [P, 1])

    with ExitStack() as pctx:
        ps = pctx.enter_context(nc.psum_tensor("ps", [P, 8, 512], F32))

        x_in = [sem("x_loaded0"), sem("x_loaded1")]
        w_in = [sem(f"weights_loaded{i}") for i in range(6)]
        k_in = sem("tables_loaded")
        pw_set = sem("power_set")
        id_set = sem("ident_set")
        bnd = sem("ln_stats")
        ve_s = sem("ln_var_eps")
        mv_s = sem("ln_mean_var")
        rstd_s = sem("ln_rstd")
        xn_s = sem("xn_ready")
        xt_s = sem("xn_transposed")
        xtc_s = sem("xn_transpose_copied")
        qc_s = sem("q_latent_done")
        qcc_s = sem("q_latent_copied")
        prep_s = sem("weight_product_done")
        prepa_s = sem("weight_product_copied_act")
        prepd_s = sem("weight_product_copied_dve")
        id0_s = sem("ident_zeroed")
        wqh_s, wql_s = sem("rotary_weights_high"), sem("rotary_weights_low")

        items = [("qn0", g) for g in range(4)] + [("qn1", g) for g in range(4)] + \
                [("vo", h) for h in range(H)]
        FIRST_VO = 8
        NBANK = 4

        def copy_product(copy, what, g, i):
            src = ps[:, i % NBANK, :]
            if what == "qn0":
                return copy(wqn0[:, 4 * g:4 * g + 4, :].rearrange("p h c -> p (h c)"), src)
            if what == "qn1":
                return copy(wqn1[:, 4 * g:4 * g + 4, :].rearrange("p h c -> p (h c)"), src[0:QC1, :])
            return copy(wvo[:, g, :], src)

        with nc.Block() as block:
            @block.sync
            def _(sp):
                def load_x(p):
                    for u in range(2):
                        if p > 0:
                            sp.wait_ge(xn_s, 2 * p + u - 1)
                        sp.dma_start(xt_in[:, u, :], x[:, 2 * p + u, :]).then_inc(x_in[u], 16)
                quarter = lambda i: (wo_st[:, 4 * i:4 * i + 4, :], Wo[:, 4 * i:4 * i + 4, :], w_in[4])
                between = {
                    0: [(wdq[:, :, 0:QC], Wdq, w_in[0]), (wdq[:, :, QC:2 * P], Wdq[:, :, P:QC], w_in[0])],
                    1: [(wkvc_st, Wkvc.rearrange("p c n -> p (c n)"), w_in[5]), (wqr0_st, Wqr[0:P, :], w_in[5]), (wqr1_st[0:QC1, :], Wqr[P:QC, :], w_in[5]),
                        (wqr1_st[QC1:P, :], Wqr[P:QC, :], w_in[5]), (wkr_st, Wkr2, w_in[5])],
                    2: [(wuq_st, WuqT, w_in[1])],
                    3: [(wuk_st, WukT, w_in[2])],
                    4: [quarter(0)], 5: [quarter(1)], 6: [quarter(2)],
                    7: [quarter(3), (tk[:], tab_k, k_in), (tq[:], tab_q, k_in),
                        (iota[:], tab_i, k_in), (seg_i[:], seg, k_in)],
                }
                for p in range(PAIRS):
                    load_x(p)
                    for dst, src, done in between[p]:
                        sp.dma_start(dst, src).then_inc(done, 16)
                sp.wait_ge(qc_s, TILES)
                sp.dma_start(wuv_st, WuvT).then_inc(w_in[3], 16)
                sp.wait_ge(k_in, 64)

            @block.gpsimd
            def _(pool):
                pool.memset(power[:], -0.5).then_inc(pw_set, 1)
                pool.memset(ident[:], 0.0).then_inc(id0_s, 1)
                pool.wait_ge(id0_s, 1)
                pool.affine_select(out=ident[:], in_=ident[:], compare_op=ALU.not_equal, fill=1.0,
                                   base=0, pattern=[[-1, P]], channel_multiplier=1).then_inc(id_set, 1)
                pool.wait_ge(pw_set, 1)
                with pool.Fori(0, TILES) as t:
                    pool.wait_ge(ve_s, t + 1)
                    pool.tensor_tensor(rstd[:], veps[:], power[:], ALU.pow).then_inc(rstd_s, 1)
                pool.tensor_copy(identr[:], ident[:])
                pool.tensor_copy(cxs[:, :, :, LK:LK + 1], ident[:, 0:2 * DC].rearrange("p (a c n) -> p a c n", a=2, n=1))

            @block.vector
            def _(dve):
                def norm_tile(p, u):
                    t = 2 * p + u
                    dve.wait_ge(x_in[u], 16 * p + 16)
                    dve.bn_stats(stats[:], xt_in[:, u, :]).then_inc(bnd, 1)
                    dve.wait_ge(bnd, t + 1)
                    dve.memset(carrier[:], 0.0)
                    dve.bn_aggr(mv[:], stats[:]).then_inc(mv_s, 1)
                    dve.wait_ge(mv_s, t + 1)
                    dve.tensor_scalar(veps[:], mv[:, 1:2], EPS, None, ALU.add).then_inc(ve_s, 1)
                    if not isinstance(p, int):
                        dve.wait_ge(xt_s, t - 1)
                    dve.wait_ge(rstd_s, t + 1)
                    dve.tensor_scalar(xn[:, u, :], xt_in[:, u, :], mv[:, 0:1], rstd[:, 0:1],
                                      ALU.subtract, ALU.mult).then_inc(xn_s, 1)
                    if not isinstance(p, int):
                        latent_copy(t - 2, u)

                def latent_copy(t, u):
                    dve.wait_ge(qc_s, t + 1)
                    src = ps[:, 6 + u, :]
                    dve.tensor_copy(qc0[:, bass.ds(t * P, P)], src[:, 0:P])
                    dve.tensor_copy(qc1[:, bass.ds(t * P, P)], src[:, P:2 * P]).then_inc(qcc_s, 1)

                norm_tile(0, 0)
                norm_tile(0, 1)
                with dve.Fori(1, PAIRS) as p:
                    norm_tile(p, 0)
                    norm_tile(p, 1)
                latent_copy(TILES - 2, 0)
                latent_copy(TILES - 1, 1)
                dve.wait_ge(wqh_s, 1)
                dve.tensor_tensor(wkvc[:, 1].rearrange("p c n -> p (c n)"), wkvc_st,
                                  wkvc[:, 0].rearrange("p c n -> p (c n)").bitcast(F32), ALU.subtract)
                dve.tensor_tensor(wqr0[:, 1, :], wqr0_st, wqr0[:, 0, :].bitcast(F32), ALU.subtract)
                dve.tensor_tensor(wkr[:, 1, :], wkr_st, wkr[:, 0, :].bitcast(F32), ALU.subtract)
                dve.tensor_tensor(wqr1[QC1:P, :], wqr1_st[QC1:P, :], wqr1[QC1:P, :].bitcast(F32),
                                  ALU.subtract).then_inc(wql_s, 1)
                for i, (what, g) in enumerate(items):
                    if i % 2 == 1:
                        dve.wait_ge(prep_s, i + 1)
                        if i == FIRST_VO + 1:
                            dve.wait_ge(wql_s, 1)
                        copy_product(dve.tensor_copy, what, g, i).then_inc(prepd_s, 1)

            @block.scalar
            def _(act):
                def turn_copy(p, u):
                    t = 2 * p + u
                    act.wait_ge(xt_s, t + 1)
                    if not isinstance(p, int):
                        act.wait_ge(qc_s, t - 1)
                    act.copy(xnt[:, u, :, :].rearrange("p c q -> p (c q)"), ps[:, 4 + u, :]).then_inc(xtc_s, 1)

                turn_copy(0, 0)
                turn_copy(0, 1)
                with act.Fori(1, PAIRS) as p:
                    turn_copy(p, 0)
                    turn_copy(p, 1)
                act.wait_ge(w_in[5], 80)
                act.copy(wkvc[:, 0].rearrange("p c n -> p (c n)"), wkvc_st)
                act.copy(wqr0[:, 0, :], wqr0_st)
                act.copy(wkr[:, 0, :], wkr_st)
                act.copy(wqr1[:], wqr1_st).then_inc(wqh_s, 1)
                for i, (what, g) in enumerate(items):
                    if i % 2 == 0:
                        act.wait_ge(prep_s, i + 1)
                        if i == FIRST_VO:
                            act.wait_ge(wql_s, 1)
                        copy_product(act.copy, what, g, i).then_inc(prepa_s, 1)

            @block.tensor
            def _(pe):
                pe.wait_ge(id_set, 1)

                def turn(p, u):
                    t = 2 * p + u
                    pe.wait_ge(xn_s, t + 1)
                    if not isinstance(p, int):
                        pe.wait_ge(xtc_s, t - 1)
                    for c in range(DC):
                        last = pe.transpose(ps[:, 4 + u, c * P:(c + 1) * P], xn[:, u, c * P:(c + 1) * P], ident[:])
                    last.then_inc(xt_s, 1)

                def latent(t, u):
                    pe.wait_ge(xtc_s, t + 1)
                    after(pe, qcc_s, t - 1)
                    for c in range(DC):
                        pe.matmul(ps[:, 6 + u, 0:P], wdq[:, c, 0:P], xnt[:, u, c, :], start=(c == 0), stop=(c == DC - 1))
                    for c in range(DC):
                        last = pe.matmul(ps[:, 6 + u, P:2 * P], wdq[:, c, P:2 * P], xnt[:, u, c, :],
                                         start=(c == 0), stop=(c == DC - 1))
                    last.then_inc(qc_s, 1)

                turn(0, 0)
                pe.wait_ge(w_in[0], 32)
                turn(0, 1)
                latent(0, 0)
                with pe.Fori(1, PAIRS) as p:
                    turn(p, 0)
                    latent(2 * p - 1, 1)
                    turn(p, 1)
                    latent(2 * p, 0)
                latent(TILES - 1, 1)
                pe.wait_ge(w_in[1], 16)
                pe.wait_ge(w_in[2], 16)
                for i, (what, g) in enumerate(items):
                    if what == "vo" and g == 0:
                        pe.wait_ge(w_in[3], 16)
                        pe.wait_ge(w_in[4], 64)
                    if i >= NBANK:
                        pe.wait_ge(prepd_s if i % 2 else prepa_s, (i - NBANK) // 2 + 1)
                    if what == "vo":
                        last = pe.matmul(ps[:, i % NBANK, :], wuv_st[:, g, :], wo_st[:, g, :], start=True, stop=True)
                    else:
                        m0, m = (0, P) if what == "qn0" else (P, QC1)
                        for k in range(4):
                            last = pe.matmul(ps[0:m, i % NBANK, k * P:(k + 1) * P], wuq_st[:, 4 * g + k, m0:m0 + m],
                                             wuk_st[:, 4 * g + k, :], start=True, stop=True)
                    last.then_inc(prep_s, 1)

        cx_in = [sem("context_loaded0"), sem("context_loaded1")]
        wc_in = [sem("ffn_chunk_loaded0"), sem("ffn_chunk_loaded1")]
        qcur_s = sem("latent_tile_ready")
        qn_done, qn_cp = sem("qn_done"), sem("qn_copied")
        qr_done, qr_read = sem("qr_done"), sem("qr_read")
        qr_sum = sem("qr_added")
        qrt_done, qrt_cp = sem("qrt_done"), sem("qrt_copied")
        kv_done, kvt_s = sem("kv_done"), sem("kvt_ready")
        kr_done, kr_read = sem("kr_done"), sem("kr_read")
        kp_s = sem("kp_ready")
        kvr_done, kvr_cp = sem("kvr_done"), sem("kvr_copied")
        s_done, s_read = sem("scores_done"), sem("scores_read")
        cseg_s, dist_s, mask_s = sem("cseg_ready"), sem("dist_ready"), sem("mask_ready")
        nb_s = sem("bias_ready")
        exp_s = sem("exp_done")
        tot_s, rinv_s = sem("total_ready"), sem("rinv_ready")
        pr_s = sem("probs_ready")
        t0_done, t1_done = sem("probs_turned0"), sem("probs_turned1")
        t0_cp, t1_cp = sem("probs_turned0_copied"), sem("probs_turned1_copied")
        o_done, o_cp = sem("o_done"), sem("o_copied")
        c_done, c_add = sem("out_done"), sem("out_added")
        pt_lo = sem("probs_turned_low")
        qcurh_s = sem("latent_tile_high")
        qn_lo = sem("qn_low")
        cxh_s, cxl_s = sem("context_high"), sem("context_low")
        kvh_s = sem("kvt_high")
        xr_in, tail_in = sem("residual_loaded"), sem("residual_tail_loaded")
        xm_out = sem("x_mid_stored")
        wpart_s = sem("ffn_chunk_summed")
        wsum_s = sem("ffn_sum_zeroed")

        S = ps[:, 0:2, :].rearrange("p a (g k) -> p (a g) k", g=2)
        R0, R1, R2, R3, R4, CB = (ps[:, 2 + i, :] for i in range(6))

        FIRST_QN = (R3, R1, R2, CB)

        def slots(p):
            for s in range(8):
                yield s, 8 * p + s, 2 * p + s // 4, s % 4

        HEADS = {1: (0, 6), 2: (6, 11), 3: (11, 16)}
        LAST_HEADS = {1: (0, 2, 3, 6), 2: (6, 8, 9, 11), 3: (11, 13, 14, 16)}

        with nc.Block() as block:
            @block.sync
            def _(sp):
                def load(p):
                    for s, n, t, j in slots(p):
                        if not (isinstance(p, int) and p == 0 and s < 2):
                            sp.wait_ge(cxl_s, n - 1)
                        sp.dma_start(cx[:, s % 2, :], ctxT[bass.ds(n, 1), :, :].rearrange("a p n -> (a p) n")).then_inc(cx_in[s % 2], 16)
                        if not (isinstance(p, int) and p == 0 and s < 2):
                            sp.wait_ge(wpart_s, n - 1)
                        sp.dma_start(wch[:, s % 2, :, :], Wffn[:, :, bass.ds(n * P, P)]).then_inc(wc_in[s % 2], 16)
                        if j == 2 and not (isinstance(p, int) and p == 0):
                            store_mid(t - 2, xres[:])
                        if j == 3 and not (isinstance(p, int) and t == 0):
                            after(sp, xm_out, 16 * (t - 1))
                            sp.dma_start(xres[:], x[:, bass.ds(t - 1, 1), :].rearrange("p a d -> p (a d)")).then_inc(xr_in, 16)

                def store_mid(t, src):
                    sp.wait_ge(c_add, t + 1)
                    sp.dma_start(x_mid[:, bass.ds(t, 1), :].rearrange("p a d -> p (a d)"), src).then_inc(xm_out, 16)

                load(0)
                with sp.Fori(1, PAIRS) as p:
                    load(p)
                sp.wait_ge(cxl_s, B - 1)
                sp.dma_start(x_tail, x[:, TILES - 1, :]).then_inc(tail_in, 16)
                store_mid(TILES - 2, xres[:])
                store_mid(TILES - 1, x_tail)
                sp.wait_ge(xm_out, 16 * TILES)

            @block.gpsimd
            def _(pool):
                def take(t, u):
                    pool.tensor_copy(qcur0[:, u, 0, :], qc0[:, bass.ds(t * P, P)])
                    pool.tensor_copy(qcur1[:, u, :], qc1[:, bass.ds(t * P, P)]).then_inc(qcurh_s, 1)
                    pool.wait_ge(qcurh_s, t + 1)
                    pool.tensor_tensor(carrier_p[:], power[:], power[:], ALU.add)
                    pool.tensor_tensor(qcur0[:, u, 1, :], qc0[:, bass.ds(t * P, P)], qcur0[:, u, 0, :].bitcast(F32),
                                       ALU.subtract)
                    pool.tensor_tensor(qcur1l[:, u, :], qc1[:, bass.ds(t * P, P)], qcur1[:, u, :].bitcast(F32),
                                       ALU.subtract).then_inc(qcur_s, 1)

                def add_rope(a):
                    pool.wait_ge(qr_read, a + 1)
                    after(pool, qrt_done, a)
                    pool.tensor_tensor(qr2[:, :, 0, :], rc[:], rs_[:], ALU.add)
                    pool.tensor_tensor(qr2[:, :, 1, :], rc[:], rs_[:], ALU.add).then_inc(qr_sum, 1)

                def context_low(m, u):
                    pool.wait_ge(cxh_s, m + 1)
                    pool.tensor_tensor(cxs[:, 1, :, 0:LK], cx[:, u, :].rearrange("p (c n) -> p c n", c=DC),
                                       cxs[:, 0, :, 0:LK].bitcast(F32), ALU.subtract).then_inc(cxl_s, 1)

                def pair(p):
                    for s, n, t, j in slots(p):
                        if j == 0 and not (isinstance(p, int) and p == PAIRS - 1):
                            pool.wait_ge(qr_done, 4 * t + 4)
                            take(t + 2, s // 4)
                        if not (isinstance(p, int) and p == PAIRS - 1 and s >= 4):
                            add_rope(n + 4)
                        if not (isinstance(p, int) and n == B - 1):
                            context_low(n + 1, (s + 1) % 2)
                take(0, 0)
                add_rope(0)
                add_rope(1)
                context_low(0, 0)
                add_rope(2)
                add_rope(3)
                take(1, 1)
                pair(0)
                with pool.Fori(1, PAIRS - 1) as p:
                    pair(p)
                pair(PAIRS - 1)

            @block.vector
            def _(dve):
                def rope(a):
                    dve.wait_ge(qr_done, a + 1)
                    after(dve, qr_sum, a)
                    q = R4[:, 0:256].rearrange("p (g f) -> p g f", f=R // 2)
                    qh = R4[:, 0:256].rearrange("p (h a f) -> p h a f", h=4, a=2)
                    rsh = rs_[:].rearrange("p h (a f) -> p h a f", a=2)
                    dve.tensor_tensor(rc[:].rearrange("p h (a f) -> p (h a) f", a=2), q,
                                      tq[:, 0:1, :].to_broadcast([P, 8, R // 2]), ALU.mult)
                    dve.tensor_tensor(rsh[:, :, 0, :], qh[:, :, 1, :], tq[:, 1:2, :].to_broadcast([P, 4, R // 2]), ALU.mult)
                    dve.tensor_tensor(rsh[:, :, 1, :], qh[:, :, 0, :], tq[:, 2:3, :].to_broadcast([P, 4, R // 2]),
                                      ALU.mult).then_inc(qr_read, 1)

                def total(m):
                    dve.wait_ge(exp_s, m + 1)
                    dve.tensor_tensor(tot[:], rsum[:], e_last[:], ALU.add).then_inc(tot_s, 1)
                    dve.wait_ge(tot_s, m + 1)
                    dve.reciprocal(rinv[:], tot[:]).then_inc(rinv_s, 1)

                def scale_probs(m, u, g0):
                    if g0 == 0:
                        dve.wait_ge(rinv_s, m + 1)
                    for g in (g0, g0 + 1):
                        last = dve.tensor_scalar(pr[:, u, g, :], pr[:, u, g, :], rinv[:, g:g + 1], None, ALU.mult)
                    last.then_inc(pr_s, 1)

                def probs_low(m):
                    for k, (bank, copied) in enumerate(((R1, t0_cp), (R2, t1_cp))):
                        dve.wait_ge(copied, m + 1)
                        last = dve.tensor_tensor(pt[:, 1, k, :], bank, pt[:, 0, k, :].bitcast(F32), ALU.subtract)
                    last.then_inc(pt_lo, 1)

                def queries_low(a, u, j, bank=R3):
                    dve.wait_ge(qn_cp, a + 1)
                    hi, lo = (qn[:, u, i, :, j, :].rearrange("p b (h q) -> p h b q", h=4) for i in range(2))
                    dve.tensor_tensor(lo, bank.rearrange("p (h b q) -> p h b q", h=4, b=TB), hi.bitcast(F32),
                                      ALU.subtract).then_inc(qn_lo, 1)

                def residual(t):
                    dve.wait_ge(c_done, t + 1)
                    dve.wait_ge(xr_in, 16 * t + 16)
                    dve.tensor_tensor(xres[:], CB, xres[:], ALU.add).then_inc(c_add, 1)

                def pair(p):
                    first = isinstance(p, int) and p == 0
                    lastp = isinstance(p, int) and p == PAIRS - 1
                    dve.tensor_scalar(cseg[:], seg_i[:, bass.ds(8 * p, 8)], -1.0, float(LOOKBACK // 2), ALU.mult, ALU.add).then_inc(cseg_s, 1)
                    for s, n, t, j in slots(p):
                        u = s % 2
                        dve.wait_ge(kv_done, n + 1)
                        after(dve, o_cp, n - 3)
                        dve.tensor_copy(kv_last[:, j:j + 1], R0[:, LM:LK])
                        dve.tensor_scalar(kvt[:, u, 0, 0:LM], R0[:, 0:LM], R0[:, LM:LK], None, ALU.subtract)
                        dve.tensor_copy(kvt[:, u, 0, LM:LK + 1], R0[:, LM:LK].to_broadcast([P, 2])).then_inc(kvh_s, 1)
                        dve.wait_ge(kvh_s, n + 1)
                        dve.scalar_tensor_tensor(kvt[:, u, 1, 0:LM], R0[:, 0:LM], R0[:, LM:LK], kvt[:, u, 0, 0:LM].bitcast(F32),
                                                 ALU.subtract, ALU.subtract)
                        dve.tensor_tensor(kvt[:, u, 1, LM:LK + 1], R0[:, LM:LK].to_broadcast([P, 2]),
                                          kvt[:, u, 0, LM:LK + 1].bitcast(F32), ALU.subtract).then_inc(kvt_s, 1)
                        if not (first and s == 0):
                            total(n - 1)
                            scale_probs(n - 1, 1 - u, 0)
                        dve.wait_ge(kr_done, n + 1)
                        after(dve, s_done, n)
                        dve.scalar_tensor_tensor(kp[:], R1[:, 0:LM], R1[:, LM:LK], tk[:, 0:LM], ALU.add, ALU.mult)
                        dve.tensor_tensor(kp_last[:], R1[:, LM:LK], tk[:, LM:LK], ALU.mult).then_inc(kr_read, 1)
                        dve.wait_ge(kr_read, n + 1)
                        dve.tensor_scalar(kp[:], kp[:], kp_last[:, 0:1], None, ALU.subtract).then_inc(kp_s, 1)
                        if not (first and s == 0):
                            scale_probs(n - 1, 1 - u, 2)
                        if not (lastp and s >= 4):
                            queries_low(n + 4, 1 - s // 4, j)
                            rope(n + 4)
                        dve.wait_ge(dist_s, n + 1)
                        dve.tensor_scalar(mask[:], dist[:], LOOKBACK ** 2 / 4 + 0.5, NEG, ALU.is_gt, ALU.mult).then_inc(mask_s, 1)
                        if not (first and s == 0):
                            probs_low(n - 1)
                        dve.wait_ge(mask_s, n + 1)
                        dve.wait_ge(s_done, n + 1)
                        after(dve, t1_done, n - 1)
                        dve.tensor_scalar(smask[:], mask[:, LM:LK], XSCALE, None, ALU.mult)
                        for g in range(4):
                            last = dve.tensor_tensor_reduce(pr[:, u, g, :], S[:, g, :], mask[:, 0:LM], 1.0, 2 * NEG,
                                                            ALU.add, ALU.max, mx[:, g:g + 1])
                        last.then_inc(s_read, 1)
                        dve.wait_ge(s_read, n + 1)
                        dve.tensor_scalar(nb[:], mx[:], mask[:, LM:LK], -XSCALE, ALU.max, ALU.mult).then_inc(nb_s, 1)
                        if j == 0 and not (first and s <= 4):
                            residual(t - 2)
                        dve.wait_ge(wc_in[u], 64 * p + 16 * (s // 2) + 16)
                        dve.tensor_reduce(wpart[:, :, bass.ds(n, 1)], wch[:, u, :, :], AX.X, ALU.add, apply_absolute_value=True).then_inc(wpart_s, 1)

                for a in range(4):
                    rope(a)
                    queries_low(a, 0, a, FIRST_QN[a])
                pair(0)
                with dve.Fori(1, PAIRS - 1) as p:
                    pair(p)
                pair(PAIRS - 1)
                total(B - 1)
                scale_probs(B - 1, 1, 0)
                scale_probs(B - 1, 1, 2)
                probs_low(B - 1)
                residual(TILES - 2)
                dve.wait_ge(c_done, TILES)
                dve.wait_ge(tail_in, 16)
                dve.tensor_tensor(x_tail, CB, x_tail, ALU.add).then_inc(c_add, 1)
                dve.memset(wsum[:], 0.0).then_inc(wsum_s, 1)
                dve.wait_ge(wsum_s, 1)
                dve.wait_ge(wpart_s, B)
                dve.tensor_reduce(wsum[:, 0:3], wpart[:], AX.X, ALU.add)

            @block.scalar
            def _(act):
                def context_high(m, loads, u):
                    act.wait_ge(cx_in[u], loads)
                    after(act, kv_done, m)
                    act.copy(cxs[:, 0, :, 0:LK], cx[:, u, :].rearrange("p (c n) -> p c n", c=DC)).then_inc(cxh_s, 1)

                def copy_qn(a, u, j, bank=R3):
                    act.wait_ge(qn_done, a + 1)
                    act.copy(qn[:, u, 0, :, j, :].rearrange("p b (h q) -> p h b q", h=4),
                             bank.rearrange("p (h b q) -> p h b q", h=4, b=TB)).then_inc(qn_cp, 1)

                def copy_qrt(a, u, j):
                    act.wait_ge(qrt_done, a + 1)
                    act.copy(qrt[:, u, :, j, :].rearrange("p b (h q) -> p h b q", h=4),
                             R0.rearrange("p (h b q) -> p h b q", h=4, b=TB)).then_inc(qrt_cp, 1)

                def copy_probs(m):
                    act.wait_ge(t0_done, m + 1)
                    after(act, o_done, m)
                    act.copy(pt[:, 0, 0, :], R1).then_inc(t0_cp, 1)
                    act.wait_ge(t1_done, m + 1)
                    act.copy(pt[:, 0, 1, :], R2).then_inc(t1_cp, 1)

                def copy_o(m, tile, ty, j):
                    act.wait_ge(o_done, m + 1)
                    if j == 0:
                        after(act, c_done, tile - 1)
                    act.activation(yt[:, ty, :, j * LQ:(j + 1) * LQ], R4.rearrange("p (h q) -> p h q", h=H),
                                   ACT.Identity, bias=kv_last[:, j:j + 1]).then_inc(o_cp, 1)

                def pair(p):
                    first = isinstance(p, int) and p == 0
                    lastp = isinstance(p, int) and p == PAIRS - 1
                    for s, n, t, j in slots(p):
                        u = s % 2
                        if s == 0:
                            act.wait_ge(cseg_s, p + 1)
                        after(act, mask_s, n)
                        act.activation(dist[:], iota[:], ACT.Square, bias=cseg[:, s:s + 1]).then_inc(dist_s, 1)
                        if not (lastp and s >= 4):
                            if j == 0:
                                after(act, s_done, 4 * t)
                            copy_qn(n + 4, 1 - s // 4, j)
                        act.wait_ge(kvr_done, n + 1)
                        after(act, o_done, n - 1)
                        act.copy(kvr[:, u].rearrange("p a k c -> p (a k c)"), R2).then_inc(kvr_cp, 1)
                        if not (lastp and s == 7):
                            context_high(n + 1, 64 * p + 16 * ((s + 1) // 2) + 16, (s + 1) % 2)
                        if not (first and s == 0):
                            copy_probs(n - 1)
                        if not (lastp and s >= 4):
                            copy_qrt(n + 4, 1 - s // 4, j)
                        if j == 0 and not (first and s == 0):
                            copy_o(n - 1, t - 1, 1 - s // 4, 3)
                        act.wait_ge(nb_s, n + 1)
                        for g in range(4):
                            act.activation(pr[:, u, g, :], pr[:, u, g, :], ACT.Exp, bias=nb[:, g:g + 1],
                                           scale=XSCALE, accum_out=rsum[:, g:g + 1])
                        act.activation(e_last[:], nb[:], ACT.Exp, bias=smask[:, 0:1]).then_inc(exp_s, 1)
                        if j:
                            copy_o(n - 1, t, s // 4, j - 1)

                for a in range(4):
                    copy_qn(a, 0, a, FIRST_QN[a])
                    if a == 0:
                        context_high(0, 16, 0)
                    if a > 0:
                        copy_qrt(a - 1, 0, a - 1)
                copy_qrt(3, 0, 3)
                pair(0)
                with act.Fori(1, PAIRS - 1) as p:
                    pair(p)
                pair(PAIRS - 1)
                copy_probs(B - 1)
                copy_o(B - 1, TILES - 1, 1, 3)

            @block.tensor
            def _(pe):
                def qn_product(t, j, out=R3):
                    for k in range(4):
                        h = 4 * j + k
                        bank = out[:, k * P:(k + 1) * P]
                        pe.matmul(bank, wqn0[:, h, :], qc0[:, bass.ds(t * P, P)], start=True, stop=False)
                        last = pe.matmul(bank, wqn1[:, h, :], qc1[0:QC1, bass.ds(t * P, P)], start=False, stop=True)
                    last.then_inc(qn_done, 1)

                def qr_product(u, j):
                    cols = slice(256 * j, 256 * j + 256)
                    for i, (a, b) in enumerate(SPLIT):
                        pe.matmul(R4[:, 0:256], qcur0[:, u, a, :], wqr0[:, b, cols], start=(i == 0), stop=False)
                    pe.matmul(R4[:, 0:256], qcur1[:, u, :], wqr1[:, cols], start=False, stop=False)
                    pe.matmul(R4[:, 0:256], qcur1l[0:QC1, u, :], wqr1[0:QC1, cols], start=False, stop=True).then_inc(qr_done, 1)

                def qr_turn(a):
                    pe.wait_ge(qr_sum, a + 1)
                    for k in range(4):
                        last = pe.transpose(R0[:, k * P:(k + 1) * P], qr2[:, k, :, :].rearrange("p a r -> p (a r)"), ident[:])
                    last.then_inc(qrt_done, 1)

                def probs_turn(m, u):
                    pe.wait_ge(pr_s, 2 * m + 2)
                    for k, (bank, done) in enumerate(((R1, t0_done), (R2, t1_done))):
                        for g in range(4):
                            last = pe.transpose(bank[:, g * P:(g + 1) * P], pr[:, u, g, k * P:(k + 1) * P], ident[:])
                        last.then_inc(done, 1)

                def out_product(ty, h0, h1):
                    for h in range(h0, h1):
                        last = pe.matmul(CB, yt[:, ty, h, :], wvo[:, h, :], start=(h == 0), stop=(h == H - 1))
                    if h1 == H:
                        last.then_inc(c_done, 1)

                def o_product(m, u):
                    order = [(k, a, 0) for k in range(KT) for a in range(2)] + [(k, 0, 1) for k in range(KT)]
                    for i, (k, a, b) in enumerate(order):
                        if i == 0:
                            pe.wait_ge(t0_cp, m + 1)
                        if i == 2:
                            pe.wait_ge(t1_cp, m + 1)
                        if i == 4:
                            pe.wait_ge(pt_lo, m + 1)
                        last = pe.matmul(R4, kvr[:, u, a, k, :], pt[:, b, k, :], start=(i == 0), stop=(i == 5))
                    last.then_inc(o_done, 1)

                def pair(p):
                    first = isinstance(p, int) and p == 0
                    lastp = isinstance(p, int) and p == PAIRS - 1
                    for s, n, t, j in slots(p):
                        u = s % 2
                        more = not (lastp and s >= 4)
                        nt = 1 - s // 4
                        back = not (first and s == 0)
                        pe.wait_ge(cxl_s, n + 1)
                        pe.wait_ge(qrt_cp, n + 4 if more else B)
                        after(pe, kvt_s, n)
                        for i, (a, b) in enumerate(SPLIT):
                            for c in range(DC):
                                last = pe.matmul(R0[:, 0:LK + 1], wkvc[:, a, c, :], cxs[:, b, c, :],
                                                 start=(i + c == 0), stop=(i == 2 and c == DC - 1))
                        last.then_inc(kv_done, 1)
                        spread = not more and j in LAST_HEADS
                        if spread:
                            if j == 1:
                                pe.wait_ge(o_cp, 4 * t)
                                pe.wait_ge(c_add, t - 1)
                            out_product(1 - s // 4, *LAST_HEADS[j][0:2])
                        if more:
                            pe.wait_ge(qn_lo, n + 4)
                            qn_product(t + 1, j)
                        pe.wait_ge(kvt_s, n + 1)
                        after(pe, kr_read, n)
                        after(pe, pt_lo, n - 1)
                        for i, (a, b) in enumerate(SPLIT):
                            last = pe.matmul(R1[:, 0:LK + 1], wkr[:, a, :], kvt[:, u, b, :], start=(i == 0), stop=(i == 2))
                        last.then_inc(kr_done, 1)
                        after(pe, kvr_cp, n)
                        for i in range(2):
                            for k in range(KT):
                                m = (i * KT + k) * KVC
                                last = pe.transpose(R2[:, m:m + KVC].bitcast(F32R), kvt[:, u, i, k * P:(k + 1) * P], identr[:])
                        last.then_inc(kvr_done, 1)
                        if more:
                            pe.wait_ge(qr_read, n + 4)
                            after(pe, o_cp, n - 1)
                            if j == 0:
                                pe.wait_ge(qcur_s, t + 2)
                            qr_product(nt, j)
                        if spread:
                            out_product(1 - s // 4, *LAST_HEADS[j][1:3])
                        pe.wait_ge(kp_s, n + 1)
                        after(pe, s_read, n)
                        pe.wait_ge(qn_lo, 4 * t + 4)
                        pe.wait_ge(qrt_cp, 4 * t + 4)
                        for g in range(4):
                            for i, (a, b) in enumerate(SPLIT):
                                pe.matmul(S[:, g, :], qn[:, s // 4, a, j, g, :], kvt[:, u, b, 0:LM], start=(i == 0), stop=False)
                            last = pe.matmul(S[:, g, :], qrt[:, s // 4, j, g, :], kp[:], start=False, stop=True)
                        last.then_inc(s_done, 1)
                        if back:
                            pe.wait_ge(kr_read, n + 1)
                            pe.wait_ge(kvr_cp, n + 1)
                            probs_turn(n - 1, 1 - u)
                        if more:
                            qr_turn(n + 4)
                        if spread:
                            out_product(1 - s // 4, *LAST_HEADS[j][2:4])
                        elif j in HEADS and not (first and s < 4):
                            if j == 1:
                                pe.wait_ge(o_cp, 4 * t)
                                after(pe, c_add, t - 1)
                            out_product(1 - s // 4, *HEADS[j])
                        if back:
                            pe.wait_ge(qr_read, n + 5 if more else B)
                            after(pe, o_cp, n - 1)
                            o_product(n - 1, 1 - u)

                for a in range(5):
                    if a < 4:
                        after(pe, qr_read, a)
                        if a == 0:
                            pe.wait_ge(qcur_s, 1)
                        qr_product(0, a)
                        qn_product(0, a, FIRST_QN[a])
                    if a > 0:
                        after(pe, qrt_cp, a - 1)
                        qr_turn(a - 1)
                pair(0)
                with pe.Fori(1, PAIRS - 1) as p:
                    pair(p)
                pair(PAIRS - 1)
                pe.wait_ge(kr_read, B)
                probs_turn(B - 1, 1)
                pe.wait_ge(o_cp, B - 1)
                o_product(B - 1, 1)
                pe.wait_ge(o_cp, B)
                pe.wait_ge(c_add, TILES - 1)
                out_product(1, 0, H)


def self_attention(nc, ctx, x_all, ident, wsum, wt, wsc, x_mid, Sq, Sk, Sv, So, Wffn, tab_s):
    def sb(name, shape, dt=F32):
        return ctx.enter_context(nc.sbuf_tensor(name, shape, dt))

    def sem(name):
        return ctx.enter_context(nc.semaphore(name))

    G = SH // 4
    wqkv = sb("self_wqkv", [P, 2, 3, DC, D], F32R)
    raw = wt[:, :, D * F // P // 2:].bitcast(F32)
    wo = sb("self_wo", [P, DC, D])
    ts = sb("ts", [P, 3 * SD // 2 + LQ])
    ones = sb("ones", [P, P])
    half = sb("half", [P, 2, 3])
    wmean = sb("wmean", [P, 3])
    wraw = sb("wraw", [P, 2, 3, D])
    wneg = sb("wneg", [P, 3, D], BF16)
    xn = sb("s_xn", [P, 2, D])
    xnt = sb("s_xnt", [P, 2, DC, P], F32R)
    rc = sb("s_rc", [P, 2, D])
    rs_ = sb("s_rs", [P, 2, D])
    qk = sb("s_qk", [P, 2, D])
    qbd = sb("s_qbd", [P, G * TB, P])
    kt = sb("s_kt", [P, G, P])
    vb = sb("s_v", [P, 2, D])
    pr = sb("s_pr", [P, G * TB, LQ])
    mx = sb("s_mx", [P, G * TB])
    tot = sb("s_tot", [P, G * TB])
    rinv = sb("s_rinv", [P, G * TB])
    pt = sb("s_pt", [P, G, P])
    ot = sb("s_ot", [P, G, TB, LQ])
    stats = sb("s_stats", [P, 6])
    mv = sb("s_mv", [P, 2])
    veps = sb("s_veps", [P, 1])
    rstd = sb("s_rstd", [P, 1])
    power = sb("s_power", [P, 1])
    carrier = sb("s_carrier", [P, 1])

    w_in = [sem(f"self_weights_loaded{i}") for i in range(3)]
    t_in = sem("self_tables_loaded")
    x_in, x_rest_in = sem("s_x_loaded"), sem("s_x_rest_loaded")
    wh_s, wl_s = sem("self_weights_high"), sem("self_weights_low")
    xl_s = sem("s_xn_low")
    o_in = sem("self_out_weights_loaded")
    wr_in = [sem("ffn_raw_loaded0"), sem("ffn_raw_loaded1")]
    set_s = sem("self_constants_set")
    mean_done, mean_cp, mean_c2, mean_s = sem("mean_done"), sem("mean_copied"), sem("mean_clipped"), sem("mean_ready")
    wneg_s, wt_s = sem("ffn_negative_ready"), sem("ffn_ternary_ready")
    bn_s, mv_s, ve_s, rstd_s, xn_s = (sem("s_" + k) for k in ("bn", "mean_var", "var_eps", "rstd", "xn_ready"))
    xt_done, xt_cp = sem("s_xn_turned"), sem("s_xn_turned_copied")
    qk_done, qk_read, qk_sum = sem("s_qk_done"), sem("s_qk_read"), sem("s_qk_added")
    v_done, v_cp = sem("s_v_done"), sem("s_v_copied")
    qt_done, qbd_d, qbd_a = sem("s_q_turned"), sem("s_qbd_dve"), sem("s_qbd_act")
    kt_done, kt_cp = sem("s_k_turned"), sem("s_k_turned_copied")
    sc_done, sc_read, mx_s, sub_s = sem("s_scores_done"), sem("s_scores_read"), sem("s_max_ready"), sem("s_shifted")
    exp_s, tot_s, rinv_s, pr_s = sem("s_exp_done"), sem("s_total"), sem("s_rinv"), sem("s_probs_ready")
    pt_done, pt_cp = sem("s_probs_turned"), sem("s_probs_turned_copied")
    av_done, ot_d, ot_a = sem("s_values_done"), sem("s_values_dve"), sem("s_values_act")
    y_done, res_s = sem("s_out_done"), sem("s_out_added")

    with ExitStack() as pctx:
        ps = pctx.enter_context(nc.psum_tensor("s_ps", [P, 8, 512], F32))
        XT, QT = ps[:, 7, :], ps[:, 0, :]
        QK = ps[:, 1:3, :]
        AV = ps[:, 3:7, :].rearrange("p b (g h q) -> p b g h q", g=G, h=4)
        KTB, YB, SB = ps[:, 2, :], ps[:, 4, :], ps[:, 5, :]
        PT, V = ps[:, 7, :], ps[:, 1, :]

        def steps(p):
            for u in range(2):
                yield u, 2 * p + u

        with nc.Block() as block:
            @block.sync
            def _(sp):
                sp.dma_start(x_all[:, 0:2, :], x_mid[:, 0:2, :]).then_inc(x_in, 16)
                for i, src in enumerate((Sq, Sk, Sv)):
                    sp.dma_start(raw[:, i, :], src.rearrange("p c n -> p (c n)")).then_inc(w_in[i], 16)
                sp.dma_start(ts[:], tab_s).then_inc(t_in, 16)
                sp.dma_start(wo[:], So).then_inc(o_in, 16)
                sp.dma_start(x_all[:, 2:TILES, :], x_mid[:, 2:TILES, :]).then_inc(x_rest_in, 16)

                def load(p):
                    for u, n in steps(p):
                        if not isinstance(p, int):
                            sp.wait_ge(wt_s, n - 1)
                        sp.dma_start(wraw[:, u, :, :], Wffn[:, :, bass.ds(n * D, D)]).then_inc(wr_in[u], 16)
                load(0)
                with sp.Fori(1, PAIRS) as p:
                    load(p)

            @block.gpsimd
            def _(pool):
                pool.memset(power[:], -0.5)
                pool.memset(ones[:], 1.0).then_inc(set_s, 1)
                pool.memset(qbd[:], 0.0).then_inc(set_s, 1)
                pool.wait_ge(set_s, 2)

                def rsqrt(n):
                    pool.wait_ge(ve_s, n + 1)
                    pool.tensor_tensor(rstd[:], veps[:], power[:], ALU.pow).then_inc(rstd_s, 1)

                def scale_probs(n):
                    pool.wait_ge(rinv_s, n + 1)
                    pool.tensor_tensor(pr[:], pr[:], rinv[:].rearrange("p (a b) -> p a b", b=1).to_broadcast([P, G * TB, LQ]),
                                       ALU.mult).then_inc(pr_s, 1)

                def add_rope(n):
                    after(pool, qt_done, n)
                    after(pool, kt_done, n)
                    for i in range(2):
                        pool.wait_ge(qk_read, 2 * n + 1 + i)
                        pool.tensor_tensor(qk[:, i, :], rc[:, i, :], rs_[:, i, :], ALU.add).then_inc(qk_sum, 1)

                def pair(p):
                    for u, n in steps(p):
                        if not (isinstance(p, int) and n == 0):
                            scale_probs(n - 1)
                        add_rope(n)
                        if not (isinstance(p, int) and n == TILES - 1):
                            rsqrt(n + 1)
                rsqrt(0)
                pair(0)
                with pool.Fori(1, PAIRS - 1) as p:
                    pair(p)
                pair(PAIRS - 1)
                scale_probs(TILES - 1)

            @block.vector
            def _(dve):
                def norm_stats(n):
                    if isinstance(n, int) and n in (0, 2):
                        dve.wait_ge(x_rest_in if n else x_in, 16)
                    dve.bn_stats(stats[:], x_all[:, bass.ds(n, 1), :]).then_inc(bn_s, 1)
                    dve.wait_ge(bn_s, n + 1)
                    dve.memset(carrier[:], 0.0)
                    dve.bn_aggr(mv[:], stats[:]).then_inc(mv_s, 1)
                    dve.wait_ge(mv_s, n + 1)
                    dve.tensor_scalar(veps[:], mv[:, 1:2], EPS, None, ALU.add).then_inc(ve_s, 1)

                def norm(n, u):
                    after(dve, xt_done, n - 1)
                    dve.wait_ge(rstd_s, n + 1)
                    dve.tensor_scalar(xn[:, u, :], x_all[:, bass.ds(n, 1), :], mv[:, 0:1], rstd[:, 0:1],
                                      ALU.subtract, ALU.mult).then_inc(xn_s, 1)

                def low_tokens(n):
                    dve.wait_ge(xt_cp, n + 1)
                    dve.tensor_tensor(xnt[:, 1, :, :].rearrange("p c q -> p (c q)"), XT,
                                      xnt[:, 0, :, :].rearrange("p c q -> p (c q)").bitcast(F32), ALU.subtract).then_inc(xl_s, 1)

                def rope(n):
                    for i in range(2):
                        dve.wait_ge(qk_done, 2 * n + 1 + i)
                        after(dve, qk_sum, 2 * n - 1 + i)
                        q = QK[:, i, :].rearrange("p (g f) -> p g f", f=SD // 2)
                        qh = QK[:, i, :].rearrange("p (h a f) -> p h a f", a=2, f=SD // 2)
                        sh = rs_[:, i, :].rearrange("p (h a f) -> p h a f", a=2, f=SD // 2)
                        tab = lambda k, m: ts[:, k * SD // 2:(k + 1) * SD // 2].rearrange("p (a f) -> p a f", a=1).to_broadcast([P, m, SD // 2])
                        dve.tensor_tensor(rc[:, i, :].rearrange("p (g f) -> p g f", f=SD // 2), q, tab(0, 2 * SH), ALU.mult)
                        dve.tensor_tensor(sh[:, :, 0, :], qh[:, :, 1, :], tab(1, SH), ALU.mult)
                        dve.tensor_tensor(sh[:, :, 1, :], qh[:, :, 0, :], tab(2, SH), ALU.mult).then_inc(qk_read, 1)

                def softmax_front(n):
                    dve.wait_ge(sc_done, n + 1)
                    after(dve, pt_done, n)
                    dve.tensor_tensor(pr[:], SB.rearrange("p (a k) -> p a k", k=LQ),
                                      ts[:, 3 * SD // 2:].rearrange("p (a k) -> p a k", a=1).to_broadcast([P, G * TB, LQ]),
                                      ALU.add).then_inc(sc_read, 1)
                    dve.wait_ge(sc_read, n + 1)
                    dve.tensor_reduce(mx[:], pr[:], AX.X, ALU.max).then_inc(mx_s, 1)
                    dve.wait_ge(mx_s, n + 1)
                    dve.tensor_tensor(pr[:], pr[:], mx[:].rearrange("p (a b) -> p a b", b=1).to_broadcast([P, G * TB, LQ]),
                                      ALU.subtract).then_inc(sub_s, 1)

                def softmax_back(n):
                    dve.wait_ge(exp_s, n + 1)
                    dve.tensor_reduce(tot[:], pr[:], AX.X, ALU.add).then_inc(tot_s, 1)
                    dve.wait_ge(tot_s, n + 1)
                    dve.reciprocal(rinv[:], tot[:]).then_inc(rinv_s, 1)

                def values(n):
                    dve.wait_ge(av_done, n + 1)
                    after(dve, y_done, n)
                    for h in (0, 1):
                        r = slice(32 * h, 32 * h + 32)
                        last = dve.tensor_copy(ot[r, :, :, :], AV[r, :, :, h, :].rearrange("p b g q -> p g b q"))
                    last.then_inc(ot_d, 1)

                def queries(n):
                    dve.wait_ge(qt_done, n + 1)
                    after(dve, sc_done, n)
                    for h in (0, 1):
                        r = slice(32 * h, 32 * h + 32)
                        last = dve.tensor_copy(qbd[r, :, 32 * h:32 * h + 32], QT[r, :].rearrange("p (a q) -> p a q", q=LQ))
                    last.then_inc(qbd_d, 1)

                def residual(n):
                    dve.wait_ge(y_done, n + 1)
                    dve.tensor_tensor(x_all[:, bass.ds(n, 1), :], YB, x_all[:, bass.ds(n, 1), :], ALU.add).then_inc(res_s, 1)

                def ternary(p, u, n):
                    dve.wait_ge(wr_in[u], 16 * p + 16)
                    for i in range(3):
                        last = dve.tensor_scalar(wneg[:, i, :], wraw[:, u, i, :], half[:, 1, i:i + 1], None, ALU.is_lt)
                    last.then_inc(wneg_s, 1)
                    dve.wait_ge(wneg_s, n + 1)
                    for i in range(3):
                        last = dve.scalar_tensor_tensor(wt[:, i, bass.ds(n * D, D)], wraw[:, u, i, :], half[:, 0, i:i + 1],
                                                        wneg[:, i, :], ALU.is_gt, ALU.subtract)
                    last.then_inc(wt_s, 1)

                def pair(p):
                    for u, n in steps(p):
                        more = not (isinstance(p, int) and n == TILES - 1)
                        back = not (isinstance(p, int) and n == 0)
                        if back:
                            softmax_back(n - 1)
                        if more:
                            norm_stats(n + 1)
                        rope(n)
                        if more:
                            norm(n + 1, 1 - u)
                        if back:
                            values(n - 1)
                        queries(n)
                        if more:
                            low_tokens(n + 1)
                        ternary(p, u, n)
                        if back:
                            residual(n - 1)
                        softmax_front(n)

                norm_stats(0)
                norm(0, 0)
                dve.wait_ge(mean_done, 1)
                dve.tensor_scalar(wmean[:], ps[:, 7, 0:3], 1.0 / (D * F), EPS, ALU.mult, ALU.max).then_inc(mean_cp, 1)
                dve.wait_ge(mean_cp, 1)
                dve.tensor_scalar(half[:, 0, :], wmean[:], 0.5, None, ALU.mult)
                dve.tensor_scalar(half[:, 1, :], wmean[:], -0.5, None, ALU.mult)
                dve.tensor_scalar(wsc[:], wmean[:], 1.0 / 127.0, None, ALU.mult).then_inc(mean_s, 1)
                dve.wait_ge(mean_s, 1)
                for i in range(3):
                    dve.wait_ge(wh_s, i + 1)
                    if i == 1:
                        low_tokens(0)
                    dve.tensor_tensor(wqkv[:, 1, i, :, :].rearrange("p c n -> p (c n)"), raw[:, i, :],
                                      wqkv[:, 0, i, :, :].rearrange("p c n -> p (c n)").bitcast(F32), ALU.subtract).then_inc(wl_s, 1)
                dve.wait_ge(t_in, 16)
                dve.wait_ge(wl_s, 3)
                pair(0)
                with dve.Fori(1, PAIRS - 1) as p:
                    pair(p)
                pair(PAIRS - 1)
                softmax_back(TILES - 1)
                values(TILES - 1)
                residual(TILES - 1)

            @block.scalar
            def _(act):
                def tokens(n):
                    act.wait_ge(xt_done, n + 1)
                    after(act, v_done, n)
                    act.copy(xnt[:, 0, :, :].rearrange("p c q -> p (c q)"), XT).then_inc(xt_cp, 1)

                def probs(n):
                    act.wait_ge(pt_done, n + 1)
                    after(act, av_done, n)
                    act.copy(pt[:].rearrange("p g q -> p (g q)"), PT).then_inc(pt_cp, 1)

                def values(n):
                    act.wait_ge(av_done, n + 1)
                    after(act, y_done, n)
                    for h in (2, 3):
                        r = slice(32 * h, 32 * h + 32)
                        last = act.copy(ot[r, :, :, :], AV[r, :, :, h, :].rearrange("p b g q -> p g b q"))
                    last.then_inc(ot_a, 1)

                def pair(p):
                    for u, n in steps(p):
                        back = not (isinstance(p, int) and n == 0)
                        if back:
                            probs(n - 1)
                        act.wait_ge(v_done, n + 1)
                        after(act, av_done, n - 1)
                        act.copy(vb[:, u, :], V).then_inc(v_cp, 1)
                        if back:
                            values(n - 1)
                        act.wait_ge(qt_done, n + 1)
                        after(act, sc_done, n)
                        for h in (2, 3):
                            r = slice(32 * h, 32 * h + 32)
                            last = act.copy(qbd[r, :, 32 * h:32 * h + 32], QT[r, :].rearrange("p (a q) -> p a q", q=LQ))
                        last.then_inc(qbd_a, 1)
                        act.wait_ge(kt_done, n + 1)
                        act.copy(kt[:].rearrange("p g q -> p (g q)"), KTB).then_inc(kt_cp, 1)
                        if not (isinstance(p, int) and n == TILES - 1):
                            tokens(n + 1)
                        act.wait_ge(sub_s, n + 1)
                        act.activation(pr[:], pr[:], ACT.Exp, scale=SSCALE).then_inc(exp_s, 1)
                act.wait_ge(set_s, 2)
                for i in range(3):
                    act.wait_ge(w_in[i], 16)
                    act.copy(wqkv[:, 0, i, :, :].rearrange("p c n -> p (c n)"), raw[:, i, :]).then_inc(wh_s, 1)
                    if i == 0:
                        tokens(0)
                pair(0)
                with act.Fori(1, PAIRS - 1) as p:
                    pair(p)
                pair(PAIRS - 1)
                probs(TILES - 1)
                values(TILES - 1)

            @block.tensor
            def _(pe):
                def project(bank, i):
                    for k, (a, b) in enumerate(SPLIT):
                        for c in range(DC):
                            last = pe.matmul(bank, xnt[:, a, c, :], wqkv[:, b, i, c, :], start=(k + c == 0), stop=(k + c == 2 + DC - 1))
                    return last

                def tokens_turn(n, u):
                    pe.wait_ge(xn_s, n + 1)
                    after(pe, pt_cp, n - 1)
                    for c in range(DC):
                        last = pe.transpose(XT[:, c * P:(c + 1) * P], xn[:, u, c * P:(c + 1) * P], ident[:])
                    last.then_inc(xt_done, 1)

                def probs_turn(n):
                    pe.wait_ge(pr_s, n + 1)
                    if not (isinstance(n, int) and n == TILES - 1):
                        pe.wait_ge(xl_s, n + 2)
                    for g in range(G):
                        last = pe.transpose(PT[:, g * P:(g + 1) * P], pr[:, TB * g:TB * g + TB, :].rearrange("p b k -> p (b k)"), ident[:])
                    last.then_inc(pt_done, 1)

                def value_product(n, u):
                    pe.wait_ge(pt_cp, n + 1)
                    pe.wait_ge(v_cp, n + 1)
                    after(pe, res_s, n)
                    pe.wait_ge(sc_read, n + 1)
                    after(pe, ot_d, n)
                    after(pe, ot_a, n)
                    for g in range(G):
                        for b in range(TB):
                            r = slice(32 * b, 32 * b + 32)
                            last = pe.matmul(ps[:, 3 + b, g * P:(g + 1) * P], vb[r, u, g * P:(g + 1) * P], pt[r, g, :],
                                             start=True, stop=True)
                    last.then_inc(av_done, 1)

                def out_product(n):
                    pe.wait_ge(ot_d, n + 1)
                    pe.wait_ge(ot_a, n + 1)
                    for g in range(G):
                        last = pe.matmul(YB, ot[:, g, :, :].rearrange("p b q -> p (b q)"), wo[:, g, :], start=(g == 0), stop=(g == G - 1))
                    last.then_inc(y_done, 1)

                def pair(p):
                    for u, n in steps(p):
                        back = not (isinstance(p, int) and n == 0)
                        pe.wait_ge(xl_s, n + 1)
                        for i in range(2):
                            if isinstance(p, int) and n == 0:
                                pe.wait_ge(wl_s, i + 1)
                            after(pe, qk_read, 2 * n - 1 + i)
                            after(pe, v_cp if i == 0 else kt_cp, n)
                            project(QK[:, i, :], i).then_inc(qk_done, 1)
                        if back:
                            probs_turn(n - 1)
                        pe.wait_ge(qk_read, 2 * n + 1)
                        if isinstance(p, int) and n == 0:
                            pe.wait_ge(wl_s, 3)
                        project(V, 2).then_inc(v_done, 1)
                        if back:
                            value_product(n - 1, 1 - u)
                        pe.wait_ge(qk_sum, 2 * n + 2)
                        after(pe, qbd_d, n)
                        after(pe, qbd_a, n)
                        for g in range(G):
                            last = pe.transpose(QT[:, g * P:(g + 1) * P], qk[:, 0, g * P:(g + 1) * P], ident[:])
                        last.then_inc(qt_done, 1)
                        for g in range(G):
                            last = pe.transpose(KTB[:, g * P:(g + 1) * P], qk[:, 1, g * P:(g + 1) * P], ident[:])
                        last.then_inc(kt_done, 1)
                        if not (isinstance(p, int) and n == TILES - 1):
                            tokens_turn(n + 1, 1 - u)
                        if back:
                            if isinstance(p, int) and n == 1:
                                pe.wait_ge(o_in, 16)
                            out_product(n - 1)
                        pe.wait_ge(qbd_d, n + 1)
                        pe.wait_ge(qbd_a, n + 1)
                        pe.wait_ge(kt_cp, n + 1)
                        for a in range(G * TB):
                            g, b = a // TB, a % TB
                            last = pe.matmul(SB[:, a * LQ:(a + 1) * LQ], qbd[:, a, :], kt[:, g, b * LQ:(b + 1) * LQ],
                                             start=True, stop=True)
                        last.then_inc(sc_done, 1)
                pe.wait_ge(set_s, 2)
                pe.matmul(ps[:, 7, 0:4], ones[:], wsum[:, 0:4], start=True, stop=True).then_inc(mean_done, 1)
                pe.wait_ge(mean_cp, 1)
                tokens_turn(0, 0)
                pair(0)
                with pe.Fori(1, PAIRS - 1) as p:
                    pair(p)
                pair(PAIRS - 1)
                probs_turn(TILES - 1)
                value_product(TILES - 1, 1)
                out_product(TILES - 1)


def feed_forward(nc, ctx, x_all, ident, wt, wsc, out):
    def sb(name, shape, dt=F32):
        return ctx.enter_context(nc.sbuf_tensor(name, shape, dt))

    def sem(name):
        return ctx.enter_context(nc.semaphore(name))

    NCH = F // D
    identb = sb("identb", [P, P], BF16)
    magic = sb("magic", [P, 1])
    negmagic = sb("negmagic", [P, 1])
    xn = sb("f_xn", [P, D])
    xr = sb("f_xr", [P, D])
    xq = sb("f_xq", [P, D], BF16)
    xqt = sb("f_xqt", [P, DC, P], BF16)
    sg = sb("f_sg", [P, 2, D])
    hb = sb("f_h", [P, F])
    hq = sb("f_hq", [P, F], BF16)
    hqt = sb("f_hqt", [P, FCH, P], BF16)
    xm, xm2, xinv, x127 = (sb("f_" + k, [P, 1]) for k in ("xm", "xm2", "xinv", "x127"))
    gu = sb("f_gu", [P, 2, 2])
    hm4 = sb("f_hm4", [P, NCH])
    hm, hm2, hinv, h127 = (sb("f_" + k, [P, 1]) for k in ("hm", "hm2", "hinv", "h127"))
    ysc = sb("f_ysc", [P, 2])
    stats = sb("f_stats", [P, 6])
    mv = sb("f_mv", [P, 2])
    veps = sb("f_veps", [P, 1])
    rstd = sb("f_rstd", [P, 1])
    power = sb("f_power", [P, 1])
    carrier = sb("f_carrier", [P, 1])

    set_s = sem("f_constants_set")
    idb_s = sem("f_ident_ready")
    bn_s, mv_s, ve_s, rstd_s, xn_s = (sem("f_" + k) for k in ("bn", "mean_var", "var_eps", "rstd", "xn_ready"))
    xm_s, xm2_s, xinv_s, x127_s, xr_s, xq_s = (sem("f_" + k) for k in ("xmax", "xclip", "xinv", "x127", "xrounded", "xq"))
    xt_done, xt_cp = sem("f_x_turned"), sem("f_x_turned_copied")
    g_done, u_done, sg_s, h_s = sem("f_gate_done"), sem("f_up_done"), sem("f_silu_ready"), sem("f_h_ready")
    hm4_s, hm_s, hm2_s, hinv_s, h127_s, hr_s, hq_s = (sem("f_" + k) for k in ("hmax4", "hmax", "hclip", "hinv", "h127", "hrounded", "hq"))
    ht_done, ht_d, ht_a = sem("f_h_turned"), sem("f_h_turned_dve"), sem("f_h_turned_act")
    y_done, res_s, out_s = sem("f_down_done"), sem("f_added"), sem("out_stored")

    with ExitStack() as pctx:
        GB = pctx.enter_context(nc.psum_tensor("f_g", [P, 2, D], F32))
        UB = pctx.enter_context(nc.psum_tensor("f_u", [P, 2, D], F32))
        YB = pctx.enter_context(nc.psum_tensor("f_y", [P, D], F32))
        XT = pctx.enter_context(nc.psum_tensor("f_xt", [P, 2 * D], BF16))
        HT = pctx.enter_context(nc.psum_tensor("f_ht", [P, F], BF16))

        def steps(p):
            for u in range(2):
                yield u, 2 * p + u

        with nc.Block() as block:
            @block.sync
            def _(sp):
                with sp.Fori(0, TILES) as n:
                    sp.wait_ge(res_s, n + 1)
                    sp.dma_start(out[bass.ds(n * P, P), :], x_all[:, bass.ds(n, 1), :].rearrange("p a d -> p (a d)")).then_inc(out_s, 16)
                sp.wait_ge(out_s, 16 * TILES)

            @block.gpsimd
            def _(pool):
                pool.tensor_copy(identb[:], ident[:]).then_inc(idb_s, 1)
                pool.memset(magic[:], MAGIC).then_inc(set_s, 1)
                pool.memset(negmagic[:], -MAGIC).then_inc(set_s, 1)
                pool.memset(power[:], -0.5).then_inc(set_s, 1)
                pool.wait_ge(set_s, 3)

                def row(n):
                    pool.wait_ge(ve_s, n + 1)
                    pool.tensor_tensor(rstd[:], veps[:], power[:], ALU.pow).then_inc(rstd_s, 1)
                    pool.wait_ge(xr_s, n + 1)
                    after(pool, xt_done, n)
                    pool.tensor_tensor(xq[:], xr[:], negmagic[:].to_broadcast([P, D]), ALU.add).then_inc(xq_s, 1)
                row(0)
                with pool.Fori(1, TILES) as n:
                    row(n)

            @block.vector
            def _(dve):
                def norm_stats(n):
                    dve.bn_stats(stats[:], x_all[:, bass.ds(n, 1), :]).then_inc(bn_s, 1)
                    dve.wait_ge(bn_s, n + 1)
                    dve.memset(carrier[:], 0.0)
                    dve.bn_aggr(mv[:], stats[:]).then_inc(mv_s, 1)
                    dve.wait_ge(mv_s, n + 1)
                    dve.tensor_scalar(veps[:], mv[:, 1:2], EPS, None, ALU.add).then_inc(ve_s, 1)

                def norm(n):
                    dve.wait_ge(rstd_s, n + 1)
                    after(dve, xr_s, n)
                    dve.tensor_scalar(xn[:], x_all[:, bass.ds(n, 1), :], mv[:, 0:1], rstd[:, 0:1],
                                      ALU.subtract, ALU.mult).then_inc(xn_s, 1)
                    dve.wait_ge(xn_s, n + 1)
                    dve.tensor_reduce(xm[:], xn[:], AX.X, ALU.max, apply_absolute_value=True).then_inc(xm_s, 1)

                def scale_x(n, u):
                    dve.wait_ge(xm_s, n + 1)
                    dve.tensor_scalar(xm2[:], xm[:], EPS, None, ALU.max).then_inc(xm2_s, 1)
                    dve.wait_ge(xm2_s, n + 1)
                    dve.tensor_scalar(gu[:, u, :], wsc[:, 0:2], xm2[:, 0:1], None, ALU.mult)
                    dve.reciprocal(xinv[:], xm2[:]).then_inc(xinv_s, 1)
                    dve.wait_ge(xinv_s, n + 1)
                    dve.tensor_scalar(x127[:], xinv[:], 127.0, None, ALU.mult).then_inc(x127_s, 1)

                def hidden(n, c, u):
                    dve.wait_ge(sg_s, 4 * n + c + 1)
                    dve.wait_ge(u_done, 4 * n + c + 1)
                    if c == 0:
                        after(dve, hq_s, n)
                    dve.scalar_tensor_tensor(hb[:, c * D:(c + 1) * D], UB[:, c % 2, :], gu[:, u, 1:2], sg[:, c % 2, :],
                                             ALU.mult, ALU.mult).then_inc(h_s, 1)
                    dve.wait_ge(h_s, 4 * n + c + 1)
                    dve.tensor_reduce(hm4[:, c:c + 1], hb[:, c * D:(c + 1) * D], AX.X, ALU.max, apply_absolute_value=True).then_inc(hm4_s, 1)

                def scale_h(n, u):
                    dve.wait_ge(hm4_s, 4 * n + 4)
                    dve.tensor_reduce(hm[:], hm4[:], AX.X, ALU.max).then_inc(hm_s, 1)
                    dve.wait_ge(hm_s, n + 1)
                    dve.tensor_scalar(hm2[:], hm[:], EPS, None, ALU.max).then_inc(hm2_s, 1)
                    dve.wait_ge(hm2_s, n + 1)
                    dve.tensor_scalar(ysc[:, u:u + 1], wsc[:, 2:3], hm2[:, 0:1], None, ALU.mult)
                    dve.reciprocal(hinv[:], hm2[:]).then_inc(hinv_s, 1)
                    dve.wait_ge(hinv_s, n + 1)
                    dve.tensor_scalar(h127[:], hinv[:], 127.0, None, ALU.mult).then_inc(h127_s, 1)

                def quantise_h(n):
                    dve.wait_ge(hr_s, n + 1)
                    after(dve, ht_done, n)
                    dve.tensor_scalar(hq[:], hb[:], MAGIC, None, ALU.subtract).then_inc(hq_s, 1)

                def copy_turned(n):
                    dve.wait_ge(ht_done, n + 1)
                    after(dve, y_done, n)
                    dve.tensor_copy(hqt[:, 0:8, :].rearrange("p c q -> p (c q)"), HT[:, 0:8 * P]).then_inc(ht_d, 1)

                def residual(n, u):
                    dve.wait_ge(y_done, n + 1)
                    dve.scalar_tensor_tensor(x_all[:, bass.ds(n, 1), :].rearrange("p a d -> p (a d)"), YB[:], ysc[:, u:u + 1],
                                             x_all[:, bass.ds(n, 1), :].rearrange("p a d -> p (a d)"), ALU.mult, ALU.add).then_inc(res_s, 1)

                def pair(p):
                    for u, n in steps(p):
                        back = not (isinstance(p, int) and n == 0)
                        if back:
                            quantise_h(n - 1)
                        hidden(n, 0, u)
                        hidden(n, 1, u)
                        hidden(n, 2, u)
                        if back:
                            copy_turned(n - 1)
                        hidden(n, 3, u)
                        scale_h(n, u)
                        if not (isinstance(p, int) and p == PAIRS - 1):
                            norm_stats(n + 2)
                            norm(n + 2)
                            scale_x(n + 2, u)
                        if back:
                            residual(n - 1, 1 - u)

                for n in range(2):
                    norm_stats(n)
                    norm(n)
                    scale_x(n, n)
                pair(0)
                with dve.Fori(1, PAIRS - 1) as p:
                    pair(p)
                pair(PAIRS - 1)
                quantise_h(TILES - 1)
                copy_turned(TILES - 1)
                residual(TILES - 1, 1)

            @block.scalar
            def _(act):
                def round_x(n):
                    act.wait_ge(x127_s, n + 1)
                    after(act, xq_s, n)
                    act.activation(xr[:], xn[:], ACT.Identity, bias=magic[:, 0:1], scale=x127[:, 0:1]).then_inc(xr_s, 1)

                def copy_x(n):
                    act.wait_ge(xt_done, n + 1)
                    after(act, u_done, 4 * n)
                    act.copy(xqt[:].rearrange("p c q -> p (c q)"), XT[:, 0:D]).then_inc(xt_cp, 1)

                def copy_turned(n):
                    act.wait_ge(ht_done, n + 1)
                    after(act, y_done, n)
                    act.copy(hqt[:, 8:16, :].rearrange("p c q -> p (c q)"), HT[:, 8 * P:16 * P]).then_inc(ht_a, 1)

                def pair(p):
                    for u, n in steps(p):
                        for c in range(NCH):
                            if c == 3 and not (isinstance(p, int) and n == 0):
                                copy_turned(n - 1)
                            act.wait_ge(g_done, 4 * n + c + 1)
                            after(act, h_s, 4 * n + c - 1)
                            act.activation(sg[:, c % 2, :], GB[:, c % 2, :], ACT.Silu, scale=gu[:, u, 0:1]).then_inc(sg_s, 1)
                        if not (isinstance(p, int) and n == TILES - 1):
                            copy_x(n + 1)
                        act.wait_ge(h127_s, n + 1)
                        act.activation(hb[:], hb[:], ACT.Identity, bias=magic[:, 0:1], scale=h127[:, 0:1]).then_inc(hr_s, 1)
                        if not (isinstance(p, int) and p == PAIRS - 1):
                            round_x(n + 2)
                act.wait_ge(set_s, 3)
                round_x(0)
                round_x(1)
                copy_x(0)
                pair(0)
                with act.Fori(1, PAIRS - 1) as p:
                    pair(p)
                pair(PAIRS - 1)
                copy_turned(TILES - 1)

            @block.tensor
            def _(pe):
                def turn_x(n):
                    pe.wait_ge(xq_s, n + 1)
                    after(pe, xt_cp, n)
                    for c in range(DC):
                        last = pe.transpose(XT[:, c * P:(c + 1) * P], xq[:, c * P:(c + 1) * P], identb[:])
                    last.then_inc(xt_done, 1)

                def turn_h(n):
                    pe.wait_ge(hq_s, n + 1)
                    after(pe, ht_d, n)
                    after(pe, ht_a, n)
                    for c in range(FCH):
                        last = pe.transpose(HT[:, c * P:(c + 1) * P], hq[:, c * P:(c + 1) * P], identb[:])
                    last.then_inc(ht_done, 1)

                def down(n):
                    pe.wait_ge(ht_d, n + 1)
                    pe.wait_ge(ht_a, n + 1)
                    after(pe, res_s, n)
                    for c in range(FCH):
                        last = pe.matmul(YB[:], hqt[:, c, :], wt[:, 2, c * D:(c + 1) * D], start=(c == 0), stop=(c == FCH - 1))
                    last.then_inc(y_done, 1)

                def pair(p):
                    for u, n in steps(p):
                        pe.wait_ge(xt_cp, n + 1)
                        for c in range(NCH):
                            if c == 3 and not (isinstance(p, int) and n == 0):
                                turn_h(n - 1)
                            after(pe, sg_s, 4 * n + c - 1)
                            for k in range(DC):
                                last = pe.matmul(GB[:, c % 2, :], xqt[:, k, :], wt[:, 0, k * F + c * D:k * F + (c + 1) * D],
                                                 start=(k == 0), stop=(k == DC - 1))
                            last.then_inc(g_done, 1)
                            after(pe, h_s, 4 * n + c - 1)
                            for k in range(DC):
                                last = pe.matmul(UB[:, c % 2, :], xqt[:, k, :], wt[:, 1, k * F + c * D:k * F + (c + 1) * D],
                                                 start=(k == 0), stop=(k == DC - 1))
                            last.then_inc(u_done, 1)
                        if not (isinstance(p, int) and n == TILES - 1):
                            turn_x(n + 1)
                        if not (isinstance(p, int) and n == 0):
                            down(n - 1)
                pe.wait_ge(idb_s, 1)
                turn_x(0)
                pair(0)
                with pe.Fori(1, PAIRS - 1) as p:
                    pair(p)
                pair(PAIRS - 1)
                turn_h(TILES - 1)
                down(TILES - 1)


def kernel(**inputs):
    import numpy as np
    import concourse.bacc as bacc
    from concourse.bass_utils import run_bass_kernel_spmd

    f32 = np.float32
    a = {k: np.asarray(v) for k, v in inputs.items()}
    g = lambda name: a["L0_" + name]
    rows = lambda w: np.ascontiguousarray(w.reshape(-1, P, w.shape[1]).transpose(1, 0, 2))
    heads_T = lambda w: np.ascontiguousarray(w.reshape(w.shape[0], H, HD).transpose(2, 1, 0))
    inv = (f32(1.0) / f32(10000.0) ** (np.arange(R // 2, dtype=f32) / f32(R // 2))).astype(f32)
    ang = np.arange(LK, dtype=f32)[None, :] * inv[:, None]
    tab_k = np.concatenate([np.cos(ang), np.cos(ang), -np.sin(ang), np.sin(ang)], 0).astype(f32)
    angq = (np.arange(P) % LQ).astype(f32)[:, None] * inv
    tab_q = np.stack([np.cos(angq), -np.sin(angq), np.sin(angq)], 1).astype(f32)
    invs = np.exp(f32(-np.log(10000.0)) * np.arange(0, SD, 2, dtype=f32) / f32(SD)).astype(f32)
    angs = (np.arange(P) % LQ).astype(f32)[:, None] * invs
    causal = np.where(np.arange(LQ)[None, :] <= (np.arange(P) % LQ)[:, None], 0.0, -1e30)
    tab_s = np.concatenate([np.cos(angs), -np.sin(angs), np.sin(angs), causal], 1).astype(f32)
    tab_i = np.ascontiguousarray(np.broadcast_to(np.arange(LK, dtype=f32), (P, LK)))
    swap = (np.arange(R) + R // 2) % R
    wkr = g("xattn_W_kr")
    halves = np.concatenate([np.arange(0, SD, 2), np.arange(1, SD, 2)])
    order = (np.arange(SH)[:, None] * SD + halves).ravel()
    ffn = [g("ffn_w_gate").T, g("ffn_w_up").T, g("ffn_w_down").T]
    arrays = {
        "x": rows(a["x"].reshape(B * LQ, D)),
        "ctxT": np.ascontiguousarray(a["ctx_2048"].transpose(0, 2, 1).reshape(B, DC, P, LK)
                                     .transpose(0, 2, 1, 3)).reshape(B, P, DC * LK),
        "seg": np.ascontiguousarray(np.tile(a["itok_BxS_0_1023"].T, (TB, 1))),
        "Wkvc": rows(g("xattn_W_kvc")),
        "Wkr2": np.concatenate([wkr, wkr[:, swap]], 1),
        "Wdq": rows(g("xattn_W_dq")),
        "WuqT": heads_T(g("xattn_W_uq")),
        "WukT": heads_T(g("xattn_W_uk")),
        "WuvT": heads_T(g("xattn_W_uv")),
        "Wo": rows(g("xattn_W_o")),
        "Wqr": g("xattn_W_qr"),
        "Sq": rows(g("attn_Wq").T[:, order]),
        "Sk": rows(g("attn_Wk").T[:, order]),
        "Sv": rows(g("attn_Wv").T),
        "So": rows(g("attn_Wo").T),
        "Wffn": np.ascontiguousarray(np.stack([rows(w).reshape(P, -1) for w in ffn], 1)),
        "tab_k": tab_k, "tab_q": tab_q, "tab_s": tab_s, "tab_i": tab_i,
    }
    nc = bacc.Bacc("TRN2", target_bir_lowering=False, num_devices=1)
    aps = [nc.dram_tensor(f"in_{k}", v.shape, mybir.dt.from_np(v.dtype), kind="ExternalInput").ap()
           for k, v in arrays.items()]
    out = nc.dram_tensor("out", (B * LQ, D), F32, kind="ExternalOutput").ap()
    x_mid = nc.dram_tensor("x_mid", (P, TILES, D), F32).ap()
    build(nc, *aps, x_mid, out)
    r = run_bass_kernel_spmd(nc, [{f"in_{k}": np.ascontiguousarray(v) for k, v in arrays.items()}], core_ids=[0])
    return r.results[0]["out"].reshape(B, LQ, D)
```

```python
from contextlib import ExitStack

import concourse.bass as bass
from concourse import mybir

F32 = mybir.dt.float32
F32R = mybir.dt.float32r
BF16 = mybir.dt.bfloat16
I32 = mybir.dt.int32
ALU = mybir.AluOpType
ACT = mybir.ActivationFunctionType
AX = mybir.AxisListType

P = 128
D = 512
DC = D // P
B, LQ, LK = 64, 32, 257
TB = P // LQ
TILES = B // TB
PAIRS = TILES // 2
H, HD, QC, KVC, R = 16, 128, 192, 128, 64
QC1 = QC - P
LM = LK - 1
KT = LM // P
LOOKBACK = 8
XSCALE = float(1.0 / (HD + R) ** 0.5)
NEG = -float(2 ** 100)
EPS = 1e-5
SH, SD = 16, 32
SSCALE = float(1.0 / SD ** 0.5)
F = 2048
FCH = F // P
MAGIC = float(3 * 2 ** 22)


SPLIT = ((0, 0), (0, 1), (1, 0))


def after(eng, sem, count):
    if not isinstance(count, int) or count > 0:
        eng.wait_ge(sem, count)


def build(nc, x, ctxT, seg, Wkvc, Wkr2, Wdq, WuqT, WukT, WuvT, Wo, Wqr,
          Sq, Sk, Sv, So, Wffn, tab_k, tab_q, tab_s, tab_i, x_mid, out):
    with ExitStack() as top:
        def sbt(ctx, name, shape, dt=F32):
            return ctx.enter_context(nc.sbuf_tensor(name, shape, dt))

        ident = sbt(top, "ident", [P, P])
        wsum = sbt(top, "wsum", [P, 4])
        wsc = sbt(top, "wsc", [P, 3])

        with ExitStack() as ctx:
            cross_attention(nc, ctx, x_mid, ident, wsum, x, ctxT, seg, Wkvc, Wkr2, Wdq, WuqT, WukT,
                            WuvT, Wo, Wqr, Wffn, tab_k, tab_q, tab_i)
        x_all = sbt(top, "x_all", [P, TILES, D])
        wt = sbt(top, "wt", [P, 3, D * F // P], BF16)
        with ExitStack() as ctx:
            self_attention(nc, ctx, x_all, ident, wsum, wt, wsc, x_mid, Sq, Sk, Sv, So, Wffn, tab_s)
        with ExitStack() as ctx:
            feed_forward(nc, ctx, x_all, ident, wt, wsc, out)


def cross_attention(nc, ctx, x_mid, ident, wsum, x, ctxT, seg, Wkvc, Wkr2, Wdq, WuqT, WukT, WuvT,
                    Wo, Wqr, Wffn, tab_k, tab_q, tab_i):
    def sb(name, shape, dt=F32):
        return ctx.enter_context(nc.sbuf_tensor(name, shape, dt))

    def sem(name):
        return ctx.enter_context(nc.semaphore(name))

    wkvc = sb("wkvc", [P, 2, DC, KVC], F32R)
    wkr = sb("wkr", [P, 2, P], F32R)
    wqn0 = sb("wqn0", [P, H, KVC])
    wqn1 = sb("wqn1", [QC1, H, KVC])
    wqr0 = sb("wqr0", [P, 2, H * R], F32R)
    wqr1 = sb("wqr1", [P, H * R], F32R)
    wvo = sb("wvo", [P, H, D])
    tk = sb("tk", [P, LK])
    tq = sb("tq", [P, 3, R // 2])
    iota = sb("iota", [P, LK])
    seg_i = sb("seg_i", [P, B], I32)
    identr = sb("identr", [P, P], F32R)
    fold = sb("fold", [P, P], F32R)
    qc0 = sb("qc0", [P, TILES * P])
    qc1 = sb("qc1", [P, TILES * P])
    qcur0 = sb("qcur0", [P, 2, P], F32R)
    qcur1 = sb("qcur1", [P, P], F32R)
    qcur1l = sb("qcur1l", [P, P], F32R)
    rc = sb("rc", [P, 4, R])
    rs_ = sb("rs_", [P, 4, R])
    qr2 = sb("qr2", [P, 4, 2, R])
    qn = sb("qn", [P, 2, 2, TB, 4, P], F32R)
    cx = sb("cx", [P, 2, DC * LK])
    cxs = sb("cxs", [P, 2, DC, LK + 1], F32R)
    kvt = sb("kvt", [P, 2, 2, LK + 1], F32R)
    kv_last = sb("kv_last", [P, 4])
    kvr = sb("kvr", [P, 2, 2, KT, KVC], F32R)
    kp = sb("kp", [P, LM])
    kps = sb("kps", [P, 2, LM], F32R)
    krot = sb("krot", [P, LM], F32R)
    krot_lo = sb("krot_lo", [R, LM], F32R)
    qrt = sb("qrt", [P, 2, TB, 4, P], F32R)
    kp_last = sb("kp_last", [P, 1])
    cseg = sb("cseg", [P, 8])
    mask = sb("mask", [P, LK])
    smask = sb("smask", [P, 1])
    pr = sb("pr", [P, 2, 4, LM])
    mx = sb("mx", [P, 4])
    nb = sb("nb", [P, 4])
    rsum = sb("rsum", [P, 4])
    e_last = sb("e_last", [P, 4])
    tot = sb("tot", [P, 4])
    rinv = sb("rinv", [P, 4])
    pt = sb("pt", [P, 2, KT, D], F32R)
    wch = sb("wch", [P, 2, 3, P])
    wpart = sb("wpart", [P, 3, B])
    xres = sb("xres", [P, D])
    yt = sb("yt", [P, 2, H, P])
    vo_flat = wvo[:].rearrange("p h n -> p (h n)")
    wuq_st = vo_flat[:, 0:H * QC].rearrange("p (h c) -> p h c", h=H)
    wuk_st = vo_flat[:, 4096:6144].rearrange("p (h c) -> p h c", h=H)
    wqr0_st, wqr1_st = vo_flat[:, 6144:7168], vo_flat[:, 7168:8192]
    wkr_st = mask[:, 0:P]
    wkvc_st = qr2[:].rearrange("p k a r -> p (k a r)")

    def wo_st(h):
        if h < 8:
            return yt[:].rearrange("p u h c -> p (u h c)")[:, h * D:(h + 2) * D]
        if h < 12:
            return vo_flat[:, (h + 4) * D:(h + 6) * D]
        return cx[:, (h - 12) // 2, 0:2 * D]

    xt_in = [cx[:, 0, 0:D], cx[:, 0, D:2 * D], xres[:], wch[:].rearrange("p u i n -> p (u i n)")[:, 0:D]]
    wdq = cx[:, 1, 0:DC * 2 * P].rearrange("p (c n) -> p c n", c=DC)
    pr_flat = pr[:].rearrange("p u g k -> p (u g k)")
    xn = pr_flat[:, 0:2 * D].rearrange("p (u n) -> p u n", u=2)
    xnt = pr_flat[:, 2 * D:4 * D].rearrange("p (u c q) -> p u c q", u=2, c=DC)
    wuv_st = pr_flat.rearrange("p (h c) -> p h c", h=H)
    x_tail = cx[:, 0, 0:D]
    carrier = sb("carrier", [P, 1])
    carrier_p = sb("carrier_p", [P, 1])
    stats = sb("stats", [P, 6])
    mv = sb("mv", [P, 2])
    veps = sb("veps", [P, 1])
    rstd = sb("rstd", [P, 1])
    power = sb("power", [P, 1])

    with ExitStack() as pctx:
        ps = pctx.enter_context(nc.psum_tensor("ps", [P, 8, 512], F32))

        x_in = [sem(f"x_loaded{i}") for i in range(len(xt_in))]
        w_in = [sem(f"weights_loaded{i}") for i in range(4)]
        wo_in = [sem(f"out_weights_loaded{i}") for i in range(3)]
        k_in = sem("tables_loaded")
        set_s = sem("constants_set")
        id_set = sem("ident_set")
        bnd = sem("ln_mean_var")
        ve_s = sem("ln_var_eps")
        rstd_s = sem("ln_rstd")
        xn_s = sem("xn_ready")
        xt_s = sem("xn_transposed")
        xtc_s = sem("xn_transpose_copied")
        qc_s = sem("q_latent_done")
        qcc_s = sem("q_latent_copied")
        prep_s = sem("weight_product_done")
        prepa_s = sem("weight_product_copied_act")
        prepd_s = sem("weight_product_copied_dve")
        wqh_s, wql_s = sem("rotary_weights_high"), sem("rotary_weights_low")

        items = [("qn0", g) for g in range(4)] + [("qn1", g) for g in range(4)] + \
                [("vo", h) for h in range(H)]
        FIRST_VO = 8
        NBANK = 4

        def copy_product(copy, what, g, i):
            src = ps[:, i % NBANK, :]
            if what == "qn0":
                return copy(wqn0[:, 4 * g:4 * g + 4, :].rearrange("p h c -> p (h c)"), src)
            if what == "qn1":
                return copy(wqn1[:, 4 * g:4 * g + 4, :].rearrange("p h c -> p (h c)"), src[0:QC1, :])
            return copy(wvo[:, g, :], src)

        with nc.Block() as block:
            @block.sync
            def _(sp):
                def load_x(t):
                    i = t % len(xt_in)
                    after(sp, xn_s, t - len(xt_in) + 1)
                    sp.dma_start(xt_in[i], x[:, t, :]).then_inc(x_in[i], 16)

                two = lambda h: (wo_st(h), Wo[:, h:h + 2, :].rearrange("p h n -> p (h n)"), wo_in[max(0, h // 4 - 1)])
                between = {
                    0: [(wdq[:, :, 0:QC], Wdq, w_in[0]), (wdq[:, :, QC:2 * P], Wdq[:, :, P:QC], w_in[0])],
                    1: [(wkvc_st, Wkvc.rearrange("p c n -> p (c n)"), w_in[3]),
                        (wqr0_st, Wqr[0:P, :], w_in[3]), (wqr1_st[0:QC1, :], Wqr[P:QC, :], w_in[3]),
                        (wqr1_st[QC1:P, :], Wqr[P:QC, :], w_in[3]), (wkr_st, Wkr2, w_in[3])],
                    2: [(wuq_st, WuqT, w_in[1])],
                    3: [(wuk_st, WukT, w_in[1])],
                    4: [two(0)], 5: [two(2)], 6: [two(4), two(6)],
                    7: [(tk[:], tab_k, k_in), (tq[:], tab_q, k_in),
                        (iota[:], tab_i, k_in), (seg_i[:], seg, k_in)],
                }
                for p in range(PAIRS):
                    load_x(2 * p)
                    load_x(2 * p + 1)
                    for dst, src, done in between[p]:
                        sp.dma_start(dst, src).then_inc(done, 16)
                sp.wait_ge(qc_s, TILES)
                sp.dma_start(wuv_st, WuvT).then_inc(w_in[2], 16)
                for h in (8, 10, 12, 14):
                    if h == 8:
                        sp.wait_ge(wql_s, 1)
                    dst, src, done = two(h)
                    sp.dma_start(dst, src).then_inc(done, 16)
                sp.wait_ge(k_in, 64)

            @block.gpsimd
            def _(pool):
                pool.memset(power[:], -0.5).then_inc(set_s, 1)
                pool.memset(ident[:], 0.0).then_inc(set_s, 1)
                pool.wait_ge(set_s, 2)
                pool.affine_select(out=ident[:], in_=ident[:], compare_op=ALU.not_equal, fill=1.0,
                                   base=0, pattern=[[-1, P]], channel_multiplier=1).then_inc(id_set, 1)
                with pool.Fori(0, TILES) as t:
                    pool.wait_ge(ve_s, t + 1)
                    pool.tensor_tensor(rstd[:], veps[:], power[:], ALU.pow).then_inc(rstd_s, 1)
                pool.tensor_copy(identr[:], ident[:])
                for i in range(2):
                    pool.tensor_tensor(fold[:, i * R:(i + 1) * R], ident[:, 0:R], ident[:, R:P], ALU.add)
                pool.tensor_copy(cxs[:, :, :, LK:LK + 1], ident[:, 0:2 * DC].rearrange("p (a c n) -> p a c n", a=2, n=1))

            @block.vector
            def _(dve):
                def norm_stats(i, loads):
                    dve.wait_ge(x_in[i], loads)
                    dve.bn_stats(stats[:], xt_in[i]).then_inc(bnd, 1)

                def norm_var(t):
                    dve.wait_ge(bnd, 2 * t + 1)
                    dve.memset(carrier[:], 0.0)
                    dve.bn_aggr(mv[:], stats[:]).then_inc(bnd, 1)
                    dve.wait_ge(bnd, 2 * t + 2)
                    dve.tensor_scalar(veps[:], mv[:, 1:2], EPS, None, ALU.add).then_inc(ve_s, 1)

                def norm_tile(t, i):
                    after(dve, xt_s, t - 1)
                    dve.wait_ge(rstd_s, t + 1)
                    dve.tensor_scalar(xn[:, i % 2, :], xt_in[i], mv[:, 0:1], rstd[:, 0:1],
                                      ALU.subtract, ALU.mult).then_inc(xn_s, 1)

                def tiles(q):
                    for i in range(4):
                        t, more = 4 * q + i, not (isinstance(q, int) and 4 * q + i == TILES - 1)
                        if more:
                            norm_stats((i + 1) % 4, 16 * q + (16 if i < 3 else 32))
                        norm_tile(t, i)
                        if not (isinstance(q, int) and t < 2):
                            latent_copy(t - 2, i % 2)
                        if more:
                            dve.wait_ge(xn_s, t + 1)
                            norm_var(t + 1)

                def latent_copy(t, u):
                    dve.wait_ge(qc_s, t + 1)
                    src = ps[:, 6 + u, :]
                    dve.tensor_copy(qc0[:, bass.ds(t * P, P)], src[:, 0:P])
                    dve.tensor_copy(qc1[:, bass.ds(t * P, P)], src[:, P:2 * P]).then_inc(qcc_s, 1)

                norm_stats(0, 16)
                norm_var(0)
                tiles(0)
                with dve.Fori(1, TILES // 4 - 1) as q:
                    tiles(q)
                tiles(TILES // 4 - 1)
                latent_copy(TILES - 2, 0)
                latent_copy(TILES - 1, 1)
                dve.wait_ge(wqh_s, 1)
                dve.tensor_tensor(wkvc[:, 1].rearrange("p c n -> p (c n)"), wkvc_st,
                                  wkvc[:, 0].rearrange("p c n -> p (c n)").bitcast(F32), ALU.subtract)
                dve.tensor_tensor(wqr0[:, 1, :], wqr0_st, wqr0[:, 0, :].bitcast(F32), ALU.subtract)
                dve.tensor_tensor(wkr[:, 1, :], wkr_st, wkr[:, 0, :].bitcast(F32), ALU.subtract)
                dve.tensor_tensor(wqr1[QC1:P, :], wqr1_st[QC1:P, :], wqr1[QC1:P, :].bitcast(F32),
                                  ALU.subtract).then_inc(wql_s, 1)
                for i, (what, g) in enumerate(items):
                    if i % 2 == 1:
                        dve.wait_ge(prep_s, i + 1)
                        if i == FIRST_VO + 1:
                            dve.wait_ge(wql_s, 1)
                        copy_product(dve.tensor_copy, what, g, i).then_inc(prepd_s, 1)

            @block.scalar
            def _(act):
                def turn_copy(p, u):
                    t = 2 * p + u
                    act.wait_ge(xt_s, t + 1)
                    if not isinstance(p, int):
                        act.wait_ge(qc_s, t - 1)
                    act.copy(xnt[:, u, :, :].rearrange("p c q -> p (c q)"), ps[:, 4 + u, :]).then_inc(xtc_s, 1)

                turn_copy(0, 0)
                turn_copy(0, 1)
                with act.Fori(1, PAIRS) as p:
                    turn_copy(p, 0)
                    turn_copy(p, 1)
                act.wait_ge(w_in[3], 80)
                act.copy(wkvc[:, 0].rearrange("p c n -> p (c n)"), wkvc_st)
                act.copy(wqr0[:, 0, :], wqr0_st)
                act.copy(wkr[:, 0, :], wkr_st)
                act.copy(wqr1[:], wqr1_st).then_inc(wqh_s, 1)
                for i, (what, g) in enumerate(items):
                    if i % 2 == 0:
                        act.wait_ge(prep_s, i + 1)
                        if i == FIRST_VO:
                            act.wait_ge(wql_s, 1)
                        copy_product(act.copy, what, g, i).then_inc(prepa_s, 1)

            @block.tensor
            def _(pe):
                pe.wait_ge(id_set, 1)

                def turn(p, u):
                    t = 2 * p + u
                    pe.wait_ge(xn_s, t + 1)
                    if not isinstance(p, int):
                        pe.wait_ge(xtc_s, t - 1)
                    for c in range(DC):
                        last = pe.transpose(ps[:, 4 + u, c * P:(c + 1) * P], xn[:, u, c * P:(c + 1) * P], ident[:])
                    last.then_inc(xt_s, 1)

                def latent(t, u):
                    pe.wait_ge(xtc_s, t + 1)
                    after(pe, qcc_s, t - 1)
                    for c in range(DC):
                        pe.matmul(ps[:, 6 + u, 0:P], wdq[:, c, 0:P], xnt[:, u, c, :], start=(c == 0), stop=(c == DC - 1))
                    for c in range(DC):
                        last = pe.matmul(ps[:, 6 + u, P:2 * P], wdq[:, c, P:2 * P], xnt[:, u, c, :],
                                         start=(c == 0), stop=(c == DC - 1))
                    last.then_inc(qc_s, 1)

                turn(0, 0)
                pe.wait_ge(w_in[0], 32)
                turn(0, 1)
                latent(0, 0)
                with pe.Fori(1, PAIRS) as p:
                    turn(p, 0)
                    latent(2 * p - 1, 1)
                    turn(p, 1)
                    latent(2 * p, 0)
                latent(TILES - 1, 1)
                pe.wait_ge(w_in[1], 32)
                for i, (what, g) in enumerate(items):
                    if what == "vo" and g == 0:
                        pe.wait_ge(w_in[2], 16)
                        pe.wait_ge(wo_in[0], 64)
                    if what == "vo" and g in (8, 12):
                        pe.wait_ge(wo_in[g // 4 - 1], 32)
                    if i >= NBANK:
                        pe.wait_ge(prepd_s if i % 2 else prepa_s, (i - NBANK) // 2 + 1)
                    if what == "vo":
                        last = pe.matmul(ps[:, i % NBANK, :], wuv_st[:, g, :], wo_st(g - g % 2)[:, g % 2 * D:(g % 2 + 1) * D], start=True, stop=True)
                    else:
                        m0, m = (0, P) if what == "qn0" else (P, QC1)
                        for k in range(4):
                            last = pe.matmul(ps[0:m, i % NBANK, k * P:(k + 1) * P], wuq_st[:, 4 * g + k, m0:m0 + m],
                                             wuk_st[:, 4 * g + k, :], start=True, stop=True)
                    last.then_inc(prep_s, 1)

        cx_in = [sem("context_loaded0"), sem("context_loaded1")]
        wc_in = [sem("ffn_chunk_loaded0"), sem("ffn_chunk_loaded1")]
        qcur_s = sem("latent_tile_ready")
        qn_done, qn_cp = sem("qn_done"), sem("qn_copied")
        qr_done, qr_read = sem("qr_done"), sem("qr_read")
        qr_sum = sem("qr_added")
        qrt_done, qrt_cp = sem("qrt_done"), sem("qrt_copied")
        kv_done, kvt_s = sem("kv_done"), sem("kvt_ready")
        kr_done, kr_read = sem("kr_done"), sem("kr_read")
        kp_s = sem("kp_ready")
        kvr_done, kvr_cp = sem("kvr_done"), sem("kvr_copied")
        s_done, s_read = sem("scores_done"), sem("scores_read")
        cseg_s, dist_s, mask_s = sem("cseg_ready"), sem("dist_ready"), sem("mask_ready")
        nb_s = sem("bias_ready")
        exp_s = sem("exp_done")
        rinv_s = sem("total_and_inverse_ready")
        pr_s = sem("probs_ready")
        t0_done, t1_done = sem("probs_turned0"), sem("probs_turned1")
        t0_cp, t1_cp = sem("probs_turned0_copied"), sem("probs_turned1_copied")
        o_done, o_cp = sem("o_done"), sem("o_copied")
        c_done, c_add = sem("out_done"), sem("out_added")
        pt_lo = sem("probs_turned_low")
        qcurh_s = sem("latent_tile_high")
        qn_lo, qrt_lo = sem("qn_low"), sem("qrt_low")
        kph_s, fold_s = sem("kp_high"), sem("kp_folded")
        krh_s, krl_s = sem("rotary_keys_high"), sem("rotary_keys_low")
        cxh_s, cxl_s = sem("context_high"), sem("context_low")
        kvh_s = sem("kvt_high")
        xr_in, tail_in = sem("residual_loaded"), sem("residual_tail_loaded")
        xm_out = sem("x_mid_stored")
        wpart_s = sem("ffn_chunk_summed")
        wsum_s = sem("ffn_sum_zeroed")

        S = ps[:, 0:2, :].rearrange("p a (g k) -> p (a g) k", g=2)
        R0, R1, R2, R3, R4, CB = (ps[:, 2 + i, :] for i in range(6))

        FIRST_QN = (R3, R1, R2, CB)

        def slots(p):
            for s in range(8):
                yield s, 8 * p + s, 2 * p + s // 4, s % 4

        HEADS = {1: 0, 2: 4, 3: 8, 0: 12}

        with nc.Block() as block:
            @block.sync
            def _(sp):
                def load(p):
                    for s, n, t, j in slots(p):
                        if not (isinstance(p, int) and p == 0 and s < 2):
                            sp.wait_ge(cxl_s, n - 1)
                        sp.dma_start(cx[:, s % 2, :], ctxT[bass.ds(n, 1), :, :].rearrange("a p n -> (a p) n")).then_inc(cx_in[s % 2], 16)
                        if not (isinstance(p, int) and p == 0 and s < 2):
                            sp.wait_ge(wpart_s, n - 1)
                        sp.dma_start(wch[:, s % 2, :, :], Wffn[:, :, bass.ds(n * P, P)]).then_inc(wc_in[s % 2], 16)
                        if j == 2 and not (isinstance(p, int) and p == 0):
                            store_mid(t - 2, xres[:])
                        if j == 3 and not (isinstance(p, int) and t == 0):
                            after(sp, xm_out, 16 * (t - 1))
                            sp.dma_start(xres[:], x[:, bass.ds(t - 1, 1), :].rearrange("p a d -> p (a d)")).then_inc(xr_in, 16)

                def store_mid(t, src):
                    sp.wait_ge(c_add, t + 1)
                    sp.dma_start(x_mid[:, bass.ds(t, 1), :].rearrange("p a d -> p (a d)"), src).then_inc(xm_out, 16)

                load(0)
                with sp.Fori(1, PAIRS) as p:
                    load(p)
                sp.wait_ge(cxl_s, B - 1)
                sp.dma_start(x_tail, x[:, TILES - 1, :]).then_inc(tail_in, 16)
                store_mid(TILES - 2, xres[:])
                store_mid(TILES - 1, x_tail)
                sp.wait_ge(xm_out, 16 * TILES)

            @block.gpsimd
            def _(pool):
                def take(t):
                    pool.tensor_copy(qcur0[:, 0, :], qc0[:, bass.ds(t * P, P)])
                    pool.tensor_copy(qcur1[:], qc1[:, bass.ds(t * P, P)]).then_inc(qcurh_s, 1)
                    pool.wait_ge(qcurh_s, t + 1)
                    pool.tensor_tensor(carrier_p[:], power[:], power[:], ALU.add)
                    pool.tensor_tensor(qcur0[:, 1, :], qc0[:, bass.ds(t * P, P)], qcur0[:, 0, :].bitcast(F32),
                                       ALU.subtract)
                    pool.tensor_tensor(qcur1l[:], qc1[:, bass.ds(t * P, P)], qcur1[:].bitcast(F32),
                                       ALU.subtract).then_inc(qcur_s, 1)

                def add_rope(a):
                    pool.wait_ge(qr_read, a + 1)
                    after(pool, qrt_done, a)
                    pool.tensor_tensor(qr2[:, :, 0, :], rc[:], rs_[:], ALU.add)
                    pool.tensor_tensor(qr2[:, :, 1, :], rc[:], rs_[:], ALU.add).then_inc(qr_sum, 1)

                def context_low(m, u):
                    pool.wait_ge(cxh_s, m + 1)
                    pool.tensor_tensor(cxs[:, 1, :, 0:LK], cx[:, u, :].rearrange("p (c n) -> p c n", c=DC),
                                       cxs[:, 0, :, 0:LK].bitcast(F32), ALU.subtract).then_inc(cxl_s, 1)

                def pair(p):
                    for s, n, t, j in slots(p):
                        lastp = isinstance(p, int) and p == PAIRS - 1
                        if not (lastp and s >= 4):
                            add_rope(n + 4)
                        if not (isinstance(p, int) and n == B - 1):
                            context_low(n + 1, (s + 1) % 2)
                        if j == 3 and not (lastp and s >= 3):
                            pool.wait_ge(qr_done, 4 * t + 8)
                            take(t + 2)
                take(0)
                for a in range(4):
                    add_rope(a)
                pool.wait_ge(qr_done, 4)
                take(1)
                pair(0)
                with pool.Fori(1, PAIRS - 1) as p:
                    pair(p)
                pair(PAIRS - 1)

            @block.vector
            def _(dve):
                def rope(a):
                    dve.wait_ge(qr_done, a + 1)
                    after(dve, qr_sum, a)
                    q = R4[:, 0:256].rearrange("p (g f) -> p g f", f=R // 2)
                    qh = R4[:, 0:256].rearrange("p (h a f) -> p h a f", h=4, a=2)
                    rsh = rs_[:].rearrange("p h (a f) -> p h a f", a=2)
                    dve.tensor_tensor(rc[:].rearrange("p h (a f) -> p (h a) f", a=2), q,
                                      tq[:, 0:1, :].to_broadcast([P, 8, R // 2]), ALU.mult)
                    dve.tensor_tensor(rsh[:, :, 0, :], qh[:, :, 1, :], tq[:, 1:2, :].to_broadcast([P, 4, R // 2]), ALU.mult)
                    dve.tensor_tensor(rsh[:, :, 1, :], qh[:, :, 0, :], tq[:, 2:3, :].to_broadcast([P, 4, R // 2]),
                                      ALU.mult).then_inc(qr_read, 1)

                def total(m):
                    dve.wait_ge(exp_s, m + 1)
                    dve.tensor_tensor(tot[:], rsum[:], e_last[:], ALU.add).then_inc(rinv_s, 1)
                    dve.wait_ge(rinv_s, 2 * m + 1)
                    dve.reciprocal(rinv[:], tot[:]).then_inc(rinv_s, 1)

                def scale_probs(m, u):
                    dve.wait_ge(rinv_s, 2 * m + 2)
                    for g in range(4):
                        last = dve.tensor_scalar(pr[:, u, g, :], pr[:, u, g, :], rinv[:, g:g + 1], None, ALU.mult)
                    last.then_inc(pr_s, 1)

                def probs_low(m):
                    for k, (bank, copied) in enumerate(((R1, t0_cp), (R2, t1_cp))):
                        dve.wait_ge(copied, m + 1)
                        last = dve.tensor_tensor(pt[:, 1, k, :], bank, pt[:, 0, k, :].bitcast(F32), ALU.subtract)
                    last.then_inc(pt_lo, 1)

                def queries_low(a, u, j, bank=R3):
                    dve.wait_ge(qn_cp, a + 1)
                    hi, lo = (qn[:, u, i, :, j, :].rearrange("p b (h q) -> p h b q", h=4) for i in range(2))
                    dve.tensor_tensor(lo, bank.rearrange("p (h b q) -> p h b q", h=4, b=TB), hi.bitcast(F32),
                                      ALU.subtract).then_inc(qn_lo, 1)

                def turned_queries_low(a, u, j):
                    dve.wait_ge(qrt_cp, a + 1)
                    hi = qrt[R:P, u, :, j, :].rearrange("p b (h q) -> p h b q", h=4)
                    dve.tensor_tensor(hi, R0[R:P, :].rearrange("p (h b q) -> p h b q", h=4, b=TB), hi.bitcast(F32),
                                      ALU.subtract).then_inc(qrt_lo, 1)

                def residual(t):
                    dve.wait_ge(c_done, t + 1)
                    dve.wait_ge(xr_in, 16 * t + 16)
                    dve.tensor_tensor(xres[:], CB, xres[:], ALU.add).then_inc(c_add, 1)

                def pair(p):
                    first = isinstance(p, int) and p == 0
                    lastp = isinstance(p, int) and p == PAIRS - 1
                    dve.tensor_scalar(cseg[:], seg_i[:, bass.ds(8 * p, 8)], -1.0, float(LOOKBACK // 2), ALU.mult, ALU.add).then_inc(cseg_s, 1)
                    for s, n, t, j in slots(p):
                        u = s % 2
                        dve.wait_ge(kv_done, n + 1)
                        dve.tensor_scalar(kvt[:, u, 0, 0:LM], R0[:, 0:LM], R0[:, LM:LK], None, ALU.subtract)
                        dve.tensor_copy(kvt[:, u, 0, LM:LK + 1], R0[:, LM:LK].to_broadcast([P, 2])).then_inc(kvh_s, 1)
                        after(dve, o_cp, n - 3)
                        dve.tensor_copy(kv_last[:, j:j + 1], R0[:, LM:LK])
                        dve.wait_ge(kvh_s, n + 1)
                        dve.scalar_tensor_tensor(kvt[:, u, 1, 0:LM], R0[:, 0:LM], R0[:, LM:LK], kvt[:, u, 0, 0:LM].bitcast(F32),
                                                 ALU.subtract, ALU.subtract)
                        dve.tensor_tensor(kvt[:, u, 1, LM:LK + 1], R0[:, LM:LK].to_broadcast([P, 2]),
                                          kvt[:, u, 0, LM:LK + 1].bitcast(F32), ALU.subtract).then_inc(kvt_s, 1)
                        dve.wait_ge(kr_done, n + 1)
                        dve.scalar_tensor_tensor(kp[:], R1[:, 0:LM], R1[:, LM:LK], tk[:, 0:LM], ALU.add, ALU.mult)
                        dve.tensor_tensor(kp_last[:], R1[:, LM:LK], tk[:, LM:LK], ALU.mult).then_inc(kr_read, 1)
                        dve.wait_ge(kr_read, n + 1)
                        after(dve, fold_s, n)
                        dve.tensor_scalar(kps[:, 0, :], kp[:], kp_last[:, 0:1], None, ALU.subtract).then_inc(kph_s, 1)
                        dve.wait_ge(kph_s, n + 1)
                        dve.scalar_tensor_tensor(kps[:, 1, :], kp[:], kp_last[:, 0:1], kps[:, 0, :].bitcast(F32),
                                                 ALU.subtract, ALU.subtract).then_inc(kp_s, 1)
                        dve.wait_ge(krh_s, n + 1)
                        dve.tensor_tensor(krot_lo[:], R1[0:R, LM:2 * LM], krot[0:R, :].bitcast(F32), ALU.subtract).then_inc(krl_s, 1)
                        if not (lastp and s >= 4):
                            rope(n + 4)
                            queries_low(n + 4, 1 - s // 4, j)
                        dve.wait_ge(dist_s, n + 1)
                        dve.tensor_scalar(mask[:], mask[:], LOOKBACK ** 2 / 4 + 0.5, NEG, ALU.is_gt, ALU.mult).then_inc(mask_s, 1)
                        dve.wait_ge(mask_s, n + 1)
                        dve.wait_ge(s_done, n + 1)
                        after(dve, t1_done, n - 1)
                        dve.tensor_scalar(smask[:], mask[:, LM:LK], XSCALE, None, ALU.mult)
                        for g in range(4):
                            last = dve.tensor_tensor_reduce(pr[:, u, g, :], S[:, g, :], mask[:, 0:LM], 1.0, 2 * NEG,
                                                            ALU.add, ALU.max, mx[:, g:g + 1])
                        last.then_inc(s_read, 1)
                        dve.wait_ge(s_read, n + 1)
                        dve.tensor_scalar(nb[:], mx[:], mask[:, LM:LK], -XSCALE, ALU.max, ALU.mult).then_inc(nb_s, 1)
                        if not (first and s == 0):
                            probs_low(n - 1)
                        if not (lastp and s >= 4):
                            turned_queries_low(n + 4, 1 - s // 4, j)
                        if j == 0 and not (first and s <= 4):
                            residual(t - 2)
                        dve.wait_ge(wc_in[u], 64 * p + 16 * (s // 2) + 16)
                        dve.tensor_reduce(wpart[:, :, bass.ds(n, 1)], wch[:, u, :, :], AX.X, ALU.add, apply_absolute_value=True).then_inc(wpart_s, 1)
                        total(n)
                        scale_probs(n, u)

                for a in range(4):
                    rope(a)
                    if a == 0:
                        dve.wait_ge(cxh_s, 1)
                        dve.tensor_tensor(cxs[:, 1, :, 0:LK], cx[:, 0, :].rearrange("p (c n) -> p c n", c=DC),
                                          cxs[:, 0, :, 0:LK].bitcast(F32), ALU.subtract).then_inc(cxl_s, 1)
                    queries_low(a, 0, a, FIRST_QN[a])
                    if a > 0:
                        turned_queries_low(a - 1, 0, a - 1)
                turned_queries_low(3, 0, 3)
                pair(0)
                with dve.Fori(1, PAIRS - 1) as p:
                    pair(p)
                pair(PAIRS - 1)
                probs_low(B - 1)
                residual(TILES - 2)
                dve.wait_ge(c_done, TILES)
                dve.wait_ge(tail_in, 16)
                dve.tensor_tensor(x_tail, CB, x_tail, ALU.add).then_inc(c_add, 1)
                dve.memset(wsum[:], 0.0).then_inc(wsum_s, 1)
                dve.wait_ge(wsum_s, 1)
                dve.wait_ge(wpart_s, B)
                dve.tensor_reduce(wsum[:, 0:3], wpart[:], AX.X, ALU.add)

            @block.scalar
            def _(act):
                def context_high(m, loads, u):
                    act.wait_ge(cx_in[u], loads)
                    after(act, kv_done, m)
                    act.copy(cxs[:, 0, :, 0:LK], cx[:, u, :].rearrange("p (c n) -> p c n", c=DC)).then_inc(cxh_s, 1)

                def copy_qn(a, u, j, bank=R3):
                    act.wait_ge(qn_done, a + 1)
                    act.copy(qn[:, u, 0, :, j, :].rearrange("p b (h q) -> p h b q", h=4),
                             bank.rearrange("p (h b q) -> p h b q", h=4, b=TB)).then_inc(qn_cp, 1)

                def copy_qrt(a, u, j):
                    act.wait_ge(qrt_done, a + 1)
                    act.copy(qrt[:, u, :, j, :].rearrange("p b (h q) -> p h b q", h=4),
                             R0.rearrange("p (h b q) -> p h b q", h=4, b=TB)).then_inc(qrt_cp, 1)

                def copy_probs(m):
                    act.wait_ge(t0_done, m + 1)
                    after(act, o_done, m)
                    act.copy(pt[:, 0, 0, :], R1).then_inc(t0_cp, 1)
                    act.wait_ge(t1_done, m + 1)
                    act.copy(pt[:, 0, 1, :], R2).then_inc(t1_cp, 1)

                def copy_o(m, tile, ty, j):
                    act.wait_ge(o_done, m + 1)
                    if j == 0:
                        after(act, c_done, tile - 1)
                    act.activation(yt[:, ty, :, j * LQ:(j + 1) * LQ], R4.rearrange("p (h q) -> p h q", h=H),
                                   ACT.Identity, bias=kv_last[:, j:j + 1]).then_inc(o_cp, 1)

                def pair(p):
                    first = isinstance(p, int) and p == 0
                    lastp = isinstance(p, int) and p == PAIRS - 1
                    for s, n, t, j in slots(p):
                        u = s % 2
                        if s == 0:
                            act.wait_ge(cseg_s, p + 1)
                        after(act, nb_s, n)
                        act.activation(mask[:], iota[:], ACT.Square, bias=cseg[:, s:s + 1]).then_inc(dist_s, 1)
                        act.wait_ge(kvr_done, n + 1)
                        after(act, o_done, n - 1)
                        act.copy(kvr[:, u].rearrange("p a k c -> p (a k c)"), R2).then_inc(kvr_cp, 1)
                        act.wait_ge(fold_s, n + 1)
                        after(act, s_done, n)
                        act.copy(krot[:], R1[:, LM:2 * LM]).then_inc(krh_s, 1)
                        if not (lastp and s >= 4):
                            if j == 0:
                                after(act, s_done, 4 * t)
                            copy_qn(n + 4, 1 - s // 4, j)
                        if not (lastp and s == 7):
                            context_high(n + 1, 64 * p + 16 * ((s + 1) // 2) + 16, (s + 1) % 2)
                        if not (first and s == 0):
                            copy_probs(n - 1)
                        if not (lastp and s >= 4):
                            copy_qrt(n + 4, 1 - s // 4, j)
                        act.wait_ge(nb_s, n + 1)
                        for g in range(4):
                            act.activation(pr[:, u, g, :], pr[:, u, g, :], ACT.Exp, bias=nb[:, g:g + 1],
                                           scale=XSCALE, accum_out=rsum[:, g:g + 1])
                        act.activation(e_last[:], nb[:], ACT.Exp, bias=smask[:, 0:1]).then_inc(exp_s, 1)
                        if j:
                            copy_o(n - 1, t, s // 4, j - 1)
                        elif not (first and s == 0):
                            copy_o(n - 1, t - 1, 1 - s // 4, 3)

                context_high(0, 16, 0)
                for a in range(4):
                    copy_qn(a, 0, a, FIRST_QN[a])
                    if a > 0:
                        copy_qrt(a - 1, 0, a - 1)
                copy_qrt(3, 0, 3)
                pair(0)
                with act.Fori(1, PAIRS - 1) as p:
                    pair(p)
                pair(PAIRS - 1)
                copy_probs(B - 1)
                copy_o(B - 1, TILES - 1, 1, 3)

            @block.tensor
            def _(pe):
                def qn_product(t, j, heads=range(4), out=R3):
                    for k in heads:
                        h = 4 * j + k
                        bank = out[:, k * P:(k + 1) * P]
                        pe.matmul(bank, wqn0[:, h, :], qc0[:, bass.ds(t * P, P)], start=True, stop=False)
                        last = pe.matmul(bank, wqn1[:, h, :], qc1[0:QC1, bass.ds(t * P, P)], start=False, stop=True)
                    if k == 3:
                        last.then_inc(qn_done, 1)

                def qr_product(j):
                    cols = slice(256 * j, 256 * j + 256)
                    for i, (a, b) in enumerate(SPLIT):
                        pe.matmul(R4[:, 0:256], qcur0[:, a, :], wqr0[:, b, cols], start=(i == 0), stop=False)
                    pe.matmul(R4[:, 0:256], qcur1[:], wqr1[:, cols], start=False, stop=False)
                    pe.matmul(R4[:, 0:256], qcur1l[0:QC1, :], wqr1[0:QC1, cols], start=False, stop=True).then_inc(qr_done, 1)

                def qr_turn(a):
                    pe.wait_ge(qr_sum, a + 1)
                    for k in range(4):
                        last = pe.transpose(R0[:, k * P:(k + 1) * P], qr2[:, k, :, :].rearrange("p a r -> p (a r)"), ident[:])
                    last.then_inc(qrt_done, 1)

                def probs_turn(m, u):
                    pe.wait_ge(pr_s, m + 1)
                    for k, (bank, done) in enumerate(((R1, t0_done), (R2, t1_done))):
                        for g in range(4):
                            last = pe.transpose(bank[:, g * P:(g + 1) * P], pr[:, u, g, k * P:(k + 1) * P], ident[:])
                        last.then_inc(done, 1)

                def out_product(ty, h0, h1):
                    for h in range(h0, h1):
                        last = pe.matmul(CB, yt[:, ty, h, :], wvo[:, h, :], start=(h == 0), stop=(h == H - 1))
                    if h1 == H:
                        last.then_inc(c_done, 1)

                def latent_scores(g, ty, j, u):
                    for i, (a, b) in enumerate(SPLIT):
                        pe.matmul(S[:, g, :], qn[:, ty, a, j, g, :], kvt[:, u, b, 0:LM], start=(i == 0), stop=False)

                def rotary_scores(g, ty, j, low):
                    if low:
                        return pe.matmul(S[:, g, :], qrt[0:R, ty, j, g, :], krot_lo[:], start=False, stop=True)
                    return pe.matmul(S[:, g, :], qrt[:, ty, j, g, :], krot[:], start=False, stop=False)

                def output_wait(t):
                    pe.wait_ge(o_cp, 4 * t)
                    after(pe, c_add, t - 1)

                def o_product(m, u):
                    order = [(k, a, 0) for k in range(KT) for a in range(2)] + [(k, 0, 1) for k in range(KT)]
                    for i, (k, a, b) in enumerate(order):
                        if i == 0:
                            pe.wait_ge(t0_cp, m + 1)
                        if i == 2:
                            pe.wait_ge(t1_cp, m + 1)
                        if i == 4:
                            pe.wait_ge(pt_lo, m + 1)
                        last = pe.matmul(R4, kvr[:, u, a, k, :], pt[:, b, k, :], start=(i == 0), stop=(i == 5))
                    last.then_inc(o_done, 1)

                def pair(p):
                    first = isinstance(p, int) and p == 0
                    lastp = isinstance(p, int) and p == PAIRS - 1
                    for s, n, t, j in slots(p):
                        u = s % 2
                        more = not (lastp and s >= 4)
                        back = not (first and s == 0)
                        pe.wait_ge(cxl_s, n + 1)
                        pe.wait_ge(qrt_lo, n + 4 if more else B)
                        after(pe, kvt_s, n)
                        for i, (a, b) in enumerate(SPLIT):
                            for c in range(DC):
                                last = pe.matmul(R0[:, 0:LK + 1], wkvc[:, a, c, :], cxs[:, b, c, :],
                                                 start=(i + c == 0), stop=(i == 2 and c == DC - 1))
                        last.then_inc(kv_done, 1)
                        outputs = not (first and s < (5 if j else 8))
                        ty, h0 = (1 - s // 4 if j else s // 4), HEADS[j]
                        if outputs and not more:
                            if j == 1:
                                output_wait(t)
                            out_product(ty, h0, h0 + 1)
                        if more:
                            pe.wait_ge(qn_lo, n + 4)
                            qn_product(t + 1, j, range(3))
                        pe.wait_ge(kvt_s, n + 1)
                        after(pe, krl_s, n)
                        after(pe, pt_lo, n - 1)
                        for i, (a, b) in enumerate(SPLIT):
                            last = pe.matmul(R1[:, 0:LK + 1], wkr[:, a, :], kvt[:, u, b, :], start=(i == 0), stop=(i == 2))
                        last.then_inc(kr_done, 1)
                        after(pe, kvr_cp, n)
                        for i in range(2):
                            for k in range(KT):
                                m = (i * KT + k) * KVC
                                last = pe.transpose(R2[:, m:m + KVC].bitcast(F32R), kvt[:, u, i, k * P:(k + 1) * P], identr[:])
                        last.then_inc(kvr_done, 1)
                        if more:
                            pe.wait_ge(qr_read, n + 4)
                            after(pe, o_cp, n - 1)
                            if j == 0:
                                pe.wait_ge(qcur_s, t + 2)
                            qr_product(j)
                        after(pe, s_read, n)
                        pe.wait_ge(qn_lo, 4 * t + 4)
                        pe.wait_ge(qrt_lo, 4 * t + 4)
                        for g in (0, 2):
                            latent_scores(g, s // 4, j, u)
                        if more:
                            qn_product(t + 1, j, range(3, 4))
                        pe.wait_ge(kp_s, n + 1)
                        for i in range(2):
                            last = pe.matmul(R1[:, LM:2 * LM], fold[:], kps[:, i, :], start=(i == 0), stop=(i == 1))
                        last.then_inc(fold_s, 1)
                        if outputs:
                            if j == 1 and more:
                                output_wait(t)
                            h = h0 if more else h0 + 1
                            out_product(ty, h, h + 1)
                        pe.wait_ge(krh_s, n + 1)
                        for g in (0, 2):
                            rotary_scores(g, s // 4, j, 0)
                        pe.wait_ge(krl_s, n + 1)
                        for g in (0, 2):
                            rotary_scores(g, s // 4, j, 1)
                        for g in (1, 3):
                            latent_scores(g, s // 4, j, u)
                            rotary_scores(g, s // 4, j, 0)
                            last = rotary_scores(g, s // 4, j, 1)
                        last.then_inc(s_done, 1)
                        if back:
                            pe.wait_ge(kvr_cp, n + 1)
                            probs_turn(n - 1, 1 - u)
                        if outputs:
                            out_product(ty, h + 1, h + 2)
                        if more:
                            qr_turn(n + 4)
                        if outputs:
                            out_product(ty, h + 2, h0 + 4)
                        if back:
                            pe.wait_ge(qr_read, n + 5 if more else B)
                            after(pe, o_cp, n - 1)
                            o_product(n - 1, 1 - u)

                for a in range(5):
                    if a < 4:
                        after(pe, qr_read, a)
                        if a == 0:
                            pe.wait_ge(qcur_s, 1)
                        qr_product(a)
                        qn_product(0, a, out=FIRST_QN[a])
                    if a > 0:
                        after(pe, qrt_lo, a - 1)
                        qr_turn(a - 1)
                pair(0)
                with pe.Fori(1, PAIRS - 1) as p:
                    pair(p)
                pair(PAIRS - 1)
                probs_turn(B - 1, 1)
                out_product(0, HEADS[0], H)
                pe.wait_ge(o_cp, B - 1)
                o_product(B - 1, 1)
                pe.wait_ge(o_cp, B)
                pe.wait_ge(c_add, TILES - 1)
                out_product(1, 0, H)


def self_attention(nc, ctx, x_all, ident, wsum, wt, wsc, x_mid, Sq, Sk, Sv, So, Wffn, tab_s):
    def sb(name, shape, dt=F32):
        return ctx.enter_context(nc.sbuf_tensor(name, shape, dt))

    def sem(name):
        return ctx.enter_context(nc.semaphore(name))

    G = SH // 4
    wqkv = sb("self_wqkv", [P, 2, 3, DC, D], F32R)
    raw = wt[:, :, D * F // P // 2:].bitcast(F32)
    wo = sb("self_wo", [P, DC, D])
    ts = sb("ts", [P, 3 * SD // 2 + LQ])
    ones = sb("ones", [P, P])
    half = sb("half", [P, 2, 3])
    wmean = sb("wmean", [P, 3])
    wraw = sb("wraw", [P, 2, 3, D])
    wneg = sb("wneg", [P, 3, D], BF16)
    xn = sb("s_xn", [P, 2, D])
    xnt = sb("s_xnt", [P, 2, DC, P], F32R)
    rc = sb("s_rc", [P, 2, D])
    rs_ = sb("s_rs", [P, 2, D])
    qk = sb("s_qk", [P, 2, D])
    qbd = sb("s_qbd", [P, G * TB, P])
    kt = sb("s_kt", [P, G, P])
    vb = sb("s_v", [P, 2, D])
    pr = sb("s_pr", [P, G * TB, LQ])
    mx = sb("s_mx", [P, G * TB])
    tot = sb("s_tot", [P, G * TB])
    rinv = sb("s_rinv", [P, G * TB])
    pt = sb("s_pt", [P, G, P])
    ot = sb("s_ot", [P, G, TB, LQ])
    stats = sb("s_stats", [P, 6])
    mv = sb("s_mv", [P, 2])
    veps = sb("s_veps", [P, 1])
    rstd = sb("s_rstd", [P, 1])
    power = sb("s_power", [P, 1])
    carrier = sb("s_carrier", [P, 1])

    w_in = [sem(f"self_weights_loaded{i}") for i in range(3)]
    t_in = sem("self_tables_loaded")
    x_in, x_rest_in = sem("s_x_loaded"), sem("s_x_rest_loaded")
    wh_s, wl_s = sem("self_weights_high"), sem("self_weights_low")
    xl_s = sem("s_xn_low")
    o_in = sem("self_out_weights_loaded")
    wr_in = [sem("ffn_raw_loaded0"), sem("ffn_raw_loaded1")]
    set_s = sem("self_constants_set")
    mean_done, mean_cp, mean_c2, mean_s = sem("mean_done"), sem("mean_copied"), sem("mean_clipped"), sem("mean_ready")
    wneg_s, wt_s = sem("ffn_negative_ready"), sem("ffn_ternary_ready")
    bn_s, ve_s, rstd_s, xn_s = (sem("s_" + k) for k in ("mean_var", "var_eps", "rstd", "xn_ready"))
    xt_done, xt_cp = sem("s_xn_turned"), sem("s_xn_turned_copied")
    qk_done, qk_read, qk_sum = sem("s_qk_done"), sem("s_qk_read"), sem("s_qk_added")
    v_done, v_cp = sem("s_v_done"), sem("s_v_copied")
    qt_done, qbd_d, qbd_a = sem("s_q_turned"), sem("s_qbd_dve"), sem("s_qbd_act")
    kt_done, kt_cp = sem("s_k_turned"), sem("s_k_turned_copied")
    sc_done, sc_read, mx_s, sub_s = sem("s_scores_done"), sem("s_scores_read"), sem("s_max_ready"), sem("s_shifted")
    exp_s, tot_s, rinv_s, pr_s = sem("s_exp_done"), sem("s_total"), sem("s_rinv"), sem("s_probs_ready")
    pt_done, pt_cp = sem("s_probs_turned"), sem("s_probs_turned_copied")
    av_done, ot_d, ot_a = sem("s_values_done"), sem("s_values_dve"), sem("s_values_act")
    y_done, res_s = sem("s_out_done"), sem("s_out_added")

    with ExitStack() as pctx:
        ps = pctx.enter_context(nc.psum_tensor("s_ps", [P, 8, 512], F32))
        XT, QT = ps[:, 7, :], ps[:, 0, :]
        QK = ps[:, 1:3, :]
        AV = ps[:, 3:7, :].rearrange("p b (g h q) -> p b g h q", g=G, h=4)
        KTB, YB, SB = ps[:, 2, :], ps[:, 4, :], ps[:, 5, :]
        PT, V = ps[:, 7, :], ps[:, 1, :]

        def steps(p):
            for u in range(2):
                yield u, 2 * p + u

        with nc.Block() as block:
            @block.sync
            def _(sp):
                sp.dma_start(x_all[:, 0:2, :], x_mid[:, 0:2, :]).then_inc(x_in, 16)
                for i, src in enumerate((Sq, Sk, Sv)):
                    sp.dma_start(raw[:, i, :], src.rearrange("p c n -> p (c n)")).then_inc(w_in[i], 16)
                sp.dma_start(ts[:], tab_s).then_inc(t_in, 16)
                sp.dma_start(wo[:], So).then_inc(o_in, 16)
                sp.dma_start(x_all[:, 2:TILES, :], x_mid[:, 2:TILES, :]).then_inc(x_rest_in, 16)

                def load(p):
                    for u, n in steps(p):
                        if not isinstance(p, int):
                            sp.wait_ge(wt_s, n - 1)
                        sp.dma_start(wraw[:, u, :, :], Wffn[:, :, bass.ds(n * D, D)]).then_inc(wr_in[u], 16)
                load(0)
                with sp.Fori(1, PAIRS) as p:
                    load(p)

            @block.gpsimd
            def _(pool):
                pool.memset(power[:], -0.5)
                pool.memset(ones[:], 1.0).then_inc(set_s, 1)
                pool.memset(qbd[:], 0.0).then_inc(set_s, 1)
                pool.wait_ge(set_s, 2)

                def rsqrt(n):
                    pool.wait_ge(ve_s, n + 1)
                    pool.tensor_tensor(rstd[:], veps[:], power[:], ALU.pow).then_inc(rstd_s, 1)

                def scale_probs(n):
                    pool.wait_ge(rinv_s, n + 1)
                    pool.tensor_tensor(pr[:], pr[:], rinv[:].rearrange("p (a b) -> p a b", b=1).to_broadcast([P, G * TB, LQ]),
                                       ALU.mult).then_inc(pr_s, 1)

                def add_rope(n):
                    after(pool, qt_done, n)
                    after(pool, kt_done, n)
                    for i in range(2):
                        pool.wait_ge(qk_read, 2 * n + 1 + i)
                        pool.tensor_tensor(qk[:, i, :], rc[:, i, :], rs_[:, i, :], ALU.add).then_inc(qk_sum, 1)

                def pair(p):
                    for u, n in steps(p):
                        if not (isinstance(p, int) and n == 0):
                            scale_probs(n - 1)
                        add_rope(n)
                        if not (isinstance(p, int) and n == TILES - 1):
                            rsqrt(n + 1)
                rsqrt(0)
                pair(0)
                with pool.Fori(1, PAIRS - 1) as p:
                    pair(p)
                pair(PAIRS - 1)
                scale_probs(TILES - 1)

            @block.vector
            def _(dve):
                def norm_stats(n):
                    if isinstance(n, int) and n in (0, 2):
                        dve.wait_ge(x_rest_in if n else x_in, 16)
                    dve.bn_stats(stats[:], x_all[:, bass.ds(n, 1), :]).then_inc(bn_s, 1)
                    dve.wait_ge(bn_s, 2 * n + 1)
                    dve.memset(carrier[:], 0.0)
                    dve.bn_aggr(mv[:], stats[:]).then_inc(bn_s, 1)
                    dve.wait_ge(bn_s, 2 * n + 2)
                    dve.tensor_scalar(veps[:], mv[:, 1:2], EPS, None, ALU.add).then_inc(ve_s, 1)

                def norm(n, u):
                    after(dve, xt_done, n - 1)
                    dve.wait_ge(rstd_s, n + 1)
                    dve.tensor_scalar(xn[:, u, :], x_all[:, bass.ds(n, 1), :], mv[:, 0:1], rstd[:, 0:1],
                                      ALU.subtract, ALU.mult).then_inc(xn_s, 1)

                def low_tokens(n):
                    dve.wait_ge(xt_cp, n + 1)
                    dve.tensor_tensor(xnt[:, 1, :, :].rearrange("p c q -> p (c q)"), XT,
                                      xnt[:, 0, :, :].rearrange("p c q -> p (c q)").bitcast(F32), ALU.subtract).then_inc(xl_s, 1)

                def rope(n, i):
                    dve.wait_ge(qk_done, 2 * n + 1 + i)
                    after(dve, qk_sum, 2 * n - 1 + i)
                    q = QK[:, i, :].rearrange("p (g f) -> p g f", f=SD // 2)
                    qh = QK[:, i, :].rearrange("p (h a f) -> p h a f", a=2, f=SD // 2)
                    sh = rs_[:, i, :].rearrange("p (h a f) -> p h a f", a=2, f=SD // 2)
                    tab = lambda k, m: ts[:, k * SD // 2:(k + 1) * SD // 2].rearrange("p (a f) -> p a f", a=1).to_broadcast([P, m, SD // 2])
                    dve.tensor_tensor(rc[:, i, :].rearrange("p (g f) -> p g f", f=SD // 2), q, tab(0, 2 * SH), ALU.mult)
                    dve.tensor_tensor(sh[:, :, 0, :], qh[:, :, 1, :], tab(1, SH), ALU.mult)
                    dve.tensor_tensor(sh[:, :, 1, :], qh[:, :, 0, :], tab(2, SH), ALU.mult).then_inc(qk_read, 1)

                def softmax_front(n):
                    dve.wait_ge(sc_done, n + 1)
                    after(dve, pt_done, n)
                    dve.tensor_tensor(pr[:], SB.rearrange("p (a k) -> p a k", k=LQ),
                                      ts[:, 3 * SD // 2:].rearrange("p (a k) -> p a k", a=1).to_broadcast([P, G * TB, LQ]),
                                      ALU.add).then_inc(sc_read, 1)
                    dve.wait_ge(sc_read, n + 1)
                    dve.tensor_reduce(mx[:], pr[:], AX.X, ALU.max).then_inc(mx_s, 1)
                    dve.wait_ge(mx_s, n + 1)
                    dve.tensor_tensor(pr[:], pr[:], mx[:].rearrange("p (a b) -> p a b", b=1).to_broadcast([P, G * TB, LQ]),
                                      ALU.subtract).then_inc(sub_s, 1)

                def softmax_back(n):
                    dve.wait_ge(exp_s, n + 1)
                    dve.tensor_reduce(tot[:], pr[:], AX.X, ALU.add).then_inc(tot_s, 1)
                    dve.wait_ge(tot_s, n + 1)
                    dve.reciprocal(rinv[:], tot[:]).then_inc(rinv_s, 1)

                def values(n):
                    dve.wait_ge(av_done, n + 1)
                    after(dve, y_done, n)
                    for h in (0, 1):
                        r = slice(32 * h, 32 * h + 32)
                        last = dve.tensor_copy(ot[r, :, :, :], AV[r, :, :, h, :].rearrange("p b g q -> p g b q"))
                    last.then_inc(ot_d, 1)

                def queries(n):
                    dve.wait_ge(qt_done, n + 1)
                    after(dve, sc_done, n)
                    for h in (0, 1):
                        r = slice(32 * h, 32 * h + 32)
                        last = dve.tensor_copy(qbd[r, :, 32 * h:32 * h + 32], QT[r, :].rearrange("p (a q) -> p a q", q=LQ))
                    last.then_inc(qbd_d, 1)

                def residual(n):
                    dve.wait_ge(y_done, n + 1)
                    dve.tensor_tensor(x_all[:, bass.ds(n, 1), :], YB, x_all[:, bass.ds(n, 1), :], ALU.add).then_inc(res_s, 1)

                def ternary(p, u, n):
                    dve.wait_ge(wr_in[u], 16 * p + 16)
                    for i in range(3):
                        last = dve.tensor_scalar(wneg[:, i, :], wraw[:, u, i, :], half[:, 1, i:i + 1], None, ALU.is_lt)
                    last.then_inc(wneg_s, 1)
                    dve.wait_ge(wneg_s, n + 1)
                    for i in range(3):
                        last = dve.scalar_tensor_tensor(wt[:, i, bass.ds(n * D, D)], wraw[:, u, i, :], half[:, 0, i:i + 1],
                                                        wneg[:, i, :], ALU.is_gt, ALU.subtract)
                    last.then_inc(wt_s, 1)

                def pair(p):
                    for u, n in steps(p):
                        more = not (isinstance(p, int) and n == TILES - 1)
                        back = not (isinstance(p, int) and n == 0)
                        if back:
                            softmax_back(n - 1)
                        rope(n, 0)
                        if more:
                            norm_stats(n + 1)
                        rope(n, 1)
                        if more:
                            norm(n + 1, 1 - u)
                        if back:
                            values(n - 1)
                        queries(n)
                        if more:
                            low_tokens(n + 1)
                        ternary(p, u, n)
                        if back:
                            residual(n - 1)
                        softmax_front(n)

                norm_stats(0)
                norm(0, 0)
                dve.wait_ge(mean_done, 1)
                dve.tensor_scalar(wmean[:], ps[:, 7, 0:3], 1.0 / (D * F), EPS, ALU.mult, ALU.max).then_inc(mean_cp, 1)
                dve.wait_ge(mean_cp, 1)
                dve.tensor_scalar(half[:, 0, :], wmean[:], 0.5, None, ALU.mult)
                dve.tensor_scalar(half[:, 1, :], wmean[:], -0.5, None, ALU.mult)
                dve.tensor_scalar(wsc[:], wmean[:], 1.0 / 127.0, None, ALU.mult).then_inc(mean_s, 1)
                dve.wait_ge(mean_s, 1)
                for i in range(3):
                    if i == 0:
                        low_tokens(0)
                    dve.wait_ge(wh_s, i + 1)
                    dve.tensor_tensor(wqkv[:, 1, i, :, :].rearrange("p c n -> p (c n)"), raw[:, i, :],
                                      wqkv[:, 0, i, :, :].rearrange("p c n -> p (c n)").bitcast(F32), ALU.subtract).then_inc(wl_s, 1)
                dve.wait_ge(t_in, 16)
                dve.wait_ge(wl_s, 3)
                pair(0)
                with dve.Fori(1, PAIRS - 1) as p:
                    pair(p)
                pair(PAIRS - 1)
                softmax_back(TILES - 1)
                values(TILES - 1)
                residual(TILES - 1)

            @block.scalar
            def _(act):
                def tokens(n):
                    act.wait_ge(xt_done, n + 1)
                    after(act, v_done, n)
                    act.copy(xnt[:, 0, :, :].rearrange("p c q -> p (c q)"), XT).then_inc(xt_cp, 1)

                def probs(n):
                    act.wait_ge(pt_done, n + 1)
                    after(act, av_done, n)
                    act.copy(pt[:].rearrange("p g q -> p (g q)"), PT).then_inc(pt_cp, 1)

                def values(n):
                    act.wait_ge(av_done, n + 1)
                    after(act, y_done, n)
                    for h in (2, 3):
                        r = slice(32 * h, 32 * h + 32)
                        last = act.copy(ot[r, :, :, :], AV[r, :, :, h, :].rearrange("p b g q -> p g b q"))
                    last.then_inc(ot_a, 1)

                def pair(p):
                    for u, n in steps(p):
                        back = not (isinstance(p, int) and n == 0)
                        if back:
                            probs(n - 1)
                        act.wait_ge(v_done, n + 1)
                        after(act, av_done, n - 1)
                        act.copy(vb[:, u, :], V).then_inc(v_cp, 1)
                        if back:
                            values(n - 1)
                        act.wait_ge(qt_done, n + 1)
                        after(act, sc_done, n)
                        for h in (2, 3):
                            r = slice(32 * h, 32 * h + 32)
                            last = act.copy(qbd[r, :, 32 * h:32 * h + 32], QT[r, :].rearrange("p (a q) -> p a q", q=LQ))
                        last.then_inc(qbd_a, 1)
                        act.wait_ge(kt_done, n + 1)
                        act.copy(kt[:].rearrange("p g q -> p (g q)"), KTB).then_inc(kt_cp, 1)
                        if not (isinstance(p, int) and n == TILES - 1):
                            tokens(n + 1)
                        act.wait_ge(sub_s, n + 1)
                        act.activation(pr[:], pr[:], ACT.Exp, scale=SSCALE).then_inc(exp_s, 1)
                act.wait_ge(set_s, 2)
                for i in range(3):
                    act.wait_ge(w_in[i], 16)
                    act.copy(wqkv[:, 0, i, :, :].rearrange("p c n -> p (c n)"), raw[:, i, :]).then_inc(wh_s, 1)
                    if i == 0:
                        tokens(0)
                pair(0)
                with act.Fori(1, PAIRS - 1) as p:
                    pair(p)
                pair(PAIRS - 1)
                probs(TILES - 1)
                values(TILES - 1)

            @block.tensor
            def _(pe):
                def project(bank, i, between=None, first=False):
                    for k, (a, b) in enumerate(((0, 0), (1, 0), (0, 1))):
                        if first and k == 0:
                            pe.wait_ge(wh_s, i + 1)
                            if i == 0:
                                pe.wait_ge(xt_cp, 1)
                        if first and k == 1 and i == 0:
                            pe.wait_ge(xl_s, 1)
                        if first and k == 2:
                            pe.wait_ge(wl_s, i + 1)
                        for c in range(DC):
                            last = pe.matmul(bank, xnt[:, a, c, :], wqkv[:, b, i, c, :], start=(k + c == 0),
                                             stop=(k + c == 2 + DC - 1))
                            if between:
                                between(k * DC + c)
                    return last

                def tokens_turn(n, u):
                    pe.wait_ge(xn_s, n + 1)
                    after(pe, pt_cp, n - 1)
                    for c in range(DC):
                        last = pe.transpose(XT[:, c * P:(c + 1) * P], xn[:, u, c * P:(c + 1) * P], ident[:])
                    last.then_inc(xt_done, 1)

                def probs_turn(n):
                    pe.wait_ge(pr_s, n + 1)
                    if not (isinstance(n, int) and n == TILES - 1):
                        pe.wait_ge(xl_s, n + 2)
                    for g in range(G):
                        last = pe.transpose(PT[:, g * P:(g + 1) * P], pr[:, TB * g:TB * g + TB, :].rearrange("p b k -> p (b k)"), ident[:])
                    last.then_inc(pt_done, 1)

                def value_wait(n):
                    pe.wait_ge(pt_cp, n + 1)
                    pe.wait_ge(v_cp, n + 1)
                    after(pe, res_s, n)
                    pe.wait_ge(sc_read, n + 1)
                    after(pe, ot_d, n)
                    after(pe, ot_a, n)

                def value_product(n, u, first, count):
                    for a in range(first, first + count):
                        g, b = a // TB, a % TB
                        r = slice(32 * b, 32 * b + 32)
                        last = pe.matmul(ps[:, 3 + b, g * P:(g + 1) * P], vb[r, u, g * P:(g + 1) * P], pt[r, g, :],
                                         start=True, stop=True)
                    if first + count == G * TB:
                        last.then_inc(av_done, 1)

                def out_wait(n):
                    pe.wait_ge(ot_d, n + 1)
                    pe.wait_ge(ot_a, n + 1)

                def out_product(n, g):
                    last = pe.matmul(YB, ot[:, g, :, :].rearrange("p b q -> p (b q)"), wo[:, g, :], start=(g == 0), stop=(g == G - 1))
                    if g == G - 1:
                        last.then_inc(y_done, 1)

                def pair(p):
                    for u, n in steps(p):
                        back = not (isinstance(p, int) and n == 0)
                        start = isinstance(p, int) and n == 0
                        if not start:
                            pe.wait_ge(xl_s, n + 1)
                        for i in range(2):
                            after(pe, qk_read, 2 * n - 1 + i)
                            after(pe, v_cp if i == 0 else kt_cp, n)
                            project(QK[:, i, :], i, first=start).then_inc(qk_done, 1)
                        if back:
                            probs_turn(n - 1)
                        pe.wait_ge(qk_read, 2 * n + 1)
                        if back:
                            def values_between(k):
                                if k == 3:
                                    value_wait(n - 1)
                                if k >= 3:
                                    value_product(n - 1, 1 - u, k - 3, 1)
                            project(V, 2, values_between).then_inc(v_done, 1)
                            value_product(n - 1, 1 - u, DC * 3 - 3, G * TB - (DC * 3 - 3))
                        else:
                            project(V, 2, first=start).then_inc(v_done, 1)
                        pe.wait_ge(qk_sum, 2 * n + 2)
                        after(pe, qbd_d, n)
                        after(pe, qbd_a, n)
                        for g in range(G):
                            last = pe.transpose(QT[:, g * P:(g + 1) * P], qk[:, 0, g * P:(g + 1) * P], ident[:])
                        last.then_inc(qt_done, 1)
                        for g in range(G):
                            last = pe.transpose(KTB[:, g * P:(g + 1) * P], qk[:, 1, g * P:(g + 1) * P], ident[:])
                        last.then_inc(kt_done, 1)
                        if not (isinstance(p, int) and n == TILES - 1):
                            tokens_turn(n + 1, 1 - u)
                        if back:
                            if isinstance(p, int) and n == 1:
                                pe.wait_ge(o_in, 16)
                            out_wait(n - 1)
                            out_product(n - 1, 0)
                            out_product(n - 1, 1)
                        pe.wait_ge(qbd_d, n + 1)
                        pe.wait_ge(qbd_a, n + 1)
                        pe.wait_ge(kt_cp, n + 1)
                        for g in range(G):
                            if back and g in (1, 2):
                                out_product(n - 1, g + 1)
                            for b in range(TB):
                                a = g * TB + b
                                last = pe.matmul(SB[:, a * LQ:(a + 1) * LQ], qbd[:, a, :], kt[:, g, b * LQ:(b + 1) * LQ],
                                                 start=True, stop=True)
                        last.then_inc(sc_done, 1)
                pe.wait_ge(set_s, 2)
                pe.matmul(ps[:, 7, 0:4], ones[:], wsum[:, 0:4], start=True, stop=True).then_inc(mean_done, 1)
                pe.wait_ge(mean_cp, 1)
                tokens_turn(0, 0)
                pair(0)
                with pe.Fori(1, PAIRS - 1) as p:
                    pair(p)
                pair(PAIRS - 1)
                probs_turn(TILES - 1)
                value_wait(TILES - 1)
                value_product(TILES - 1, 1, 0, G * TB)
                out_wait(TILES - 1)
                for g in range(G):
                    out_product(TILES - 1, g)


def feed_forward(nc, ctx, x_all, ident, wt, wsc, out):
    def sb(name, shape, dt=F32):
        return ctx.enter_context(nc.sbuf_tensor(name, shape, dt))

    def sem(name):
        return ctx.enter_context(nc.semaphore(name))

    NCH = F // D
    identb = sb("identb", [P, P], BF16)
    magic = sb("magic", [P, 1])
    negmagic = sb("negmagic", [P, 1])
    xn = sb("f_xn", [P, D])
    xr = sb("f_xr", [P, D])
    xq = sb("f_xq", [P, D], BF16)
    xqt = sb("f_xqt", [P, DC, P], BF16)
    sg = sb("f_sg", [P, 2, D])
    hb = sb("f_h", [P, 2, F])
    hq = sb("f_hq", [P, F], BF16)
    hqt = sb("f_hqt", [P, FCH, P], BF16)
    xm, xm2, xinv, x127 = (sb("f_" + k, [P, 1]) for k in ("xm", "xm2", "xinv", "x127"))
    gu = sb("f_gu", [P, 2, 2])
    hm4 = sb("f_hm4", [P, NCH])
    hm, hm2, hinv, h127 = (sb("f_" + k, [P, 1]) for k in ("hm", "hm2", "hinv", "h127"))
    ysc = sb("f_ysc", [P, 2])
    stats = sb("f_stats", [P, 6])
    mv = sb("f_mv", [P, 2])
    veps = sb("f_veps", [P, 1])
    rstd = sb("f_rstd", [P, 1])
    power = sb("f_power", [P, 1])
    carrier = sb("f_carrier", [P, 1])

    set_s = sem("f_constants_set")
    bn_s, ve_s, rstd_s, xn_s = (sem("f_" + k) for k in ("mean_var", "var_eps", "rstd", "xn_ready"))
    xm_s, xinv_s, x127_s, xr_s, xq_s = (sem("f_" + k) for k in ("xmax", "xinv", "x127", "xrounded", "xq"))
    xt_done, xt_cp = sem("f_x_turned"), sem("f_x_turned_copied")
    g_done, u_done, sg_s, h_s = sem("f_gate_done"), sem("f_up_done"), sem("f_silu_ready"), sem("f_h_ready")
    hm4_s, hm_s, hinv_s, h127_s, hr_s, hq_s = (sem("f_" + k) for k in ("hmax4", "hmax", "hinv", "h127", "hrounded", "hq"))
    ht_done, ht_d, ht_a = sem("f_h_turned"), sem("f_h_turned_dve"), sem("f_h_turned_act")
    y_done, res_s, out_s = sem("f_down_done"), sem("f_added"), sem("out_stored")

    with ExitStack() as pctx:
        GB = pctx.enter_context(nc.psum_tensor("f_g", [P, 2, D], F32))
        UB = pctx.enter_context(nc.psum_tensor("f_u", [P, 2, D], F32))
        YB = pctx.enter_context(nc.psum_tensor("f_y", [P, D], F32))
        XT = pctx.enter_context(nc.psum_tensor("f_xt", [P, 2 * D], BF16))
        HT = pctx.enter_context(nc.psum_tensor("f_ht", [P, F], BF16))

        def steps(p):
            for u in range(2):
                yield u, 2 * p + u

        with nc.Block() as block:
            @block.sync
            def _(sp):
                with sp.Fori(0, TILES) as n:
                    sp.wait_ge(res_s, n + 1)
                    sp.dma_start(out[bass.ds(n * P, P), :], x_all[:, bass.ds(n, 1), :].rearrange("p a d -> p (a d)")).then_inc(out_s, 16)
                sp.wait_ge(out_s, 16 * TILES)

            @block.gpsimd
            def _(pool):
                pool.tensor_copy(identb[:], ident[:]).then_inc(set_s, 1)
                pool.memset(magic[:], MAGIC).then_inc(set_s, 1)
                pool.memset(negmagic[:], -MAGIC).then_inc(set_s, 1)
                pool.memset(power[:], -0.5).then_inc(set_s, 1)
                pool.wait_ge(set_s, 4)

                def rsqrt(n):
                    pool.wait_ge(ve_s, n + 1)
                    pool.tensor_tensor(rstd[:], veps[:], power[:], ALU.pow).then_inc(rstd_s, 1)

                def quantise_h(n, u):
                    pool.wait_ge(hr_s, n + 1)
                    after(pool, ht_done, n)
                    pool.tensor_tensor(hq[:], hb[:, u, :], negmagic[:].to_broadcast([P, F]), ALU.add).then_inc(hq_s, 1)

                def quantise_x(n):
                    pool.wait_ge(xr_s, n + 1)
                    after(pool, xt_done, n)
                    pool.tensor_tensor(xq[:], xr[:], negmagic[:].to_broadcast([P, D]), ALU.add).then_inc(xq_s, 1)
                def pair(p):
                    for u, n in steps(p):
                        if not (isinstance(p, int) and p == PAIRS - 1):
                            rsqrt(n + 2)
                        if not (isinstance(p, int) and n == TILES - 1):
                            quantise_h(n, u)
                        if not (isinstance(p, int) and p == PAIRS - 1):
                            quantise_x(n + 2)
                for n in range(2):
                    rsqrt(n)
                    quantise_x(n)
                with pool.Fori(0, PAIRS - 1) as p:
                    pair(p)
                pair(PAIRS - 1)

            @block.vector
            def _(dve):
                def norm_stats(n):
                    dve.bn_stats(stats[:], x_all[:, bass.ds(n, 1), :]).then_inc(bn_s, 1)
                    dve.wait_ge(bn_s, 2 * n + 1)
                    dve.memset(carrier[:], 0.0)
                    dve.bn_aggr(mv[:], stats[:]).then_inc(bn_s, 1)
                    dve.wait_ge(bn_s, 2 * n + 2)
                    dve.tensor_scalar(veps[:], mv[:, 1:2], EPS, None, ALU.add).then_inc(ve_s, 1)

                def norm(n):
                    dve.wait_ge(rstd_s, n + 1)
                    after(dve, xr_s, n)
                    dve.tensor_scalar(xn[:], x_all[:, bass.ds(n, 1), :], mv[:, 0:1], rstd[:, 0:1],
                                      ALU.subtract, ALU.mult).then_inc(xn_s, 1)
                    dve.wait_ge(xn_s, n + 1)
                    dve.tensor_reduce(xm[:], xn[:], AX.X, ALU.max, apply_absolute_value=True).then_inc(xm_s, 1)

                def scale_x(n, u):
                    dve.wait_ge(xm_s, 2 * n + 1)
                    dve.tensor_scalar(xm2[:], xm[:], EPS, None, ALU.max).then_inc(xm_s, 1)
                    dve.wait_ge(xm_s, 2 * n + 2)
                    dve.tensor_scalar(gu[:, u, :], wsc[:, 0:2], xm2[:, 0:1], None, ALU.mult)
                    dve.reciprocal(xinv[:], xm2[:]).then_inc(xinv_s, 1)
                    dve.wait_ge(xinv_s, n + 1)
                    dve.tensor_scalar(x127[:], xinv[:], 127.0, None, ALU.mult).then_inc(x127_s, 1)

                def hidden(n, c, u):
                    dve.wait_ge(sg_s, 4 * n + c + 1)
                    dve.wait_ge(u_done, 4 * n + c + 1)
                    if c == 0:
                        after(dve, hq_s, n - 1)
                    dve.scalar_tensor_tensor(hb[:, u, c * D:(c + 1) * D], UB[:, c % 2, :], gu[:, u, 1:2], sg[:, c % 2, :],
                                             ALU.mult, ALU.mult).then_inc(h_s, 1)
                    dve.wait_ge(h_s, 4 * n + c + 1)
                    dve.tensor_reduce(hm4[:, c:c + 1], hb[:, u, c * D:(c + 1) * D], AX.X, ALU.max, apply_absolute_value=True).then_inc(hm4_s, 1)

                def scale_h(n, u):
                    dve.wait_ge(hm4_s, 4 * n + 4)
                    dve.tensor_reduce(hm[:], hm4[:], AX.X, ALU.max).then_inc(hm_s, 1)
                    dve.wait_ge(hm_s, 2 * n + 1)
                    dve.tensor_scalar(hm2[:], hm[:], EPS, None, ALU.max).then_inc(hm_s, 1)
                    dve.wait_ge(hm_s, 2 * n + 2)
                    dve.tensor_scalar(ysc[:, u:u + 1], wsc[:, 2:3], hm2[:, 0:1], None, ALU.mult)
                    dve.reciprocal(hinv[:], hm2[:]).then_inc(hinv_s, 1)
                    dve.wait_ge(hinv_s, n + 1)
                    dve.tensor_scalar(h127[:], hinv[:], 127.0, None, ALU.mult).then_inc(h127_s, 1)

                def copy_turned(n):
                    dve.wait_ge(ht_done, n + 1)
                    after(dve, y_done, n)
                    dve.tensor_copy(hqt[:, 0:8, :].rearrange("p c q -> p (c q)"), HT[:, 0:8 * P]).then_inc(ht_d, 1)

                def residual(n, u):
                    dve.wait_ge(y_done, n + 1)
                    dve.scalar_tensor_tensor(x_all[:, bass.ds(n, 1), :].rearrange("p a d -> p (a d)"), YB[:], ysc[:, u:u + 1],
                                             x_all[:, bass.ds(n, 1), :].rearrange("p a d -> p (a d)"), ALU.mult, ALU.add).then_inc(res_s, 1)

                def pair(p):
                    for u, n in steps(p):
                        back = not (isinstance(p, int) and n == 0)
                        hidden(n, 0, u)
                        hidden(n, 1, u)
                        hidden(n, 2, u)
                        if back:
                            copy_turned(n - 1)
                        hidden(n, 3, u)
                        scale_h(n, u)
                        if not (isinstance(p, int) and p == PAIRS - 1):
                            norm_stats(n + 2)
                            norm(n + 2)
                            scale_x(n + 2, u)
                        if back:
                            residual(n - 1, 1 - u)

                for n in range(2):
                    norm_stats(n)
                    norm(n)
                    scale_x(n, n)
                pair(0)
                with dve.Fori(1, PAIRS - 1) as p:
                    pair(p)
                pair(PAIRS - 1)
                dve.wait_ge(ht_done, TILES - 1)
                dve.wait_ge(hr_s, TILES)
                dve.tensor_scalar(hq[:], hb[:, 1, :], MAGIC, None, ALU.subtract).then_inc(hq_s, 1)
                copy_turned(TILES - 1)
                residual(TILES - 1, 1)

            @block.scalar
            def _(act):
                def round_x(n):
                    act.wait_ge(x127_s, n + 1)
                    after(act, xq_s, n)
                    act.activation(xr[:], xn[:], ACT.Identity, bias=magic[:, 0:1], scale=x127[:, 0:1]).then_inc(xr_s, 1)

                def copy_x(n):
                    act.wait_ge(xt_done, n + 1)
                    after(act, u_done, 4 * n)
                    act.copy(xqt[:].rearrange("p c q -> p (c q)"), XT[:, 0:D]).then_inc(xt_cp, 1)

                def copy_turned(n):
                    act.wait_ge(ht_done, n + 1)
                    after(act, y_done, n)
                    act.copy(hqt[:, 8:16, :].rearrange("p c q -> p (c q)"), HT[:, 8 * P:16 * P]).then_inc(ht_a, 1)

                def pair(p):
                    for u, n in steps(p):
                        for c in range(NCH):
                            if c == 3 and not (isinstance(p, int) and n == 0):
                                copy_turned(n - 1)
                            act.wait_ge(g_done, 4 * n + c + 1)
                            after(act, h_s, 4 * n + c - 1)
                            act.activation(sg[:, c % 2, :], GB[:, c % 2, :], ACT.Silu, scale=gu[:, u, 0:1]).then_inc(sg_s, 1)
                            if c == 1 and not (isinstance(p, int) and n in (0, TILES - 1)):
                                round_x(n + 1)
                        if not (isinstance(p, int) and n == TILES - 1):
                            copy_x(n + 1)
                        act.wait_ge(h127_s, n + 1)
                        act.activation(hb[:, u, :], hb[:, u, :], ACT.Identity, bias=magic[:, 0:1], scale=h127[:, 0:1]).then_inc(hr_s, 1)
                act.wait_ge(set_s, 4)
                act.activation(sg[:, 0, 0:1], magic[:], ACT.Silu)
                round_x(0)
                copy_x(0)
                round_x(1)
                pair(0)
                with act.Fori(1, PAIRS - 1) as p:
                    pair(p)
                pair(PAIRS - 1)
                copy_turned(TILES - 1)

            @block.tensor
            def _(pe):
                def turn_x(n):
                    pe.wait_ge(xq_s, n + 1)
                    after(pe, xt_cp, n)
                    for c in range(DC):
                        last = pe.transpose(XT[:, c * P:(c + 1) * P], xq[:, c * P:(c + 1) * P], identb[:])
                    last.then_inc(xt_done, 1)

                def turn_h(n):
                    pe.wait_ge(hq_s, n + 1)
                    after(pe, ht_d, n)
                    after(pe, ht_a, n)
                    for c in range(FCH):
                        last = pe.transpose(HT[:, c * P:(c + 1) * P], hq[:, c * P:(c + 1) * P], identb[:])
                    last.then_inc(ht_done, 1)

                def down(n):
                    pe.wait_ge(ht_d, n + 1)
                    pe.wait_ge(ht_a, n + 1)
                    after(pe, res_s, n)
                    for c in range(FCH):
                        last = pe.matmul(YB[:], hqt[:, c, :], wt[:, 2, c * D:(c + 1) * D], start=(c == 0), stop=(c == FCH - 1))
                    last.then_inc(y_done, 1)

                def pair(p):
                    for u, n in steps(p):
                        pe.wait_ge(xt_cp, n + 1)
                        for c in range(NCH):
                            if c == 3 and not (isinstance(p, int) and n == 0):
                                turn_h(n - 1)
                            after(pe, sg_s, 4 * n + c - 1)
                            for k in range(DC):
                                last = pe.matmul(GB[:, c % 2, :], xqt[:, k, :], wt[:, 0, k * F + c * D:k * F + (c + 1) * D],
                                                 start=(k == 0), stop=(k == DC - 1))
                            last.then_inc(g_done, 1)
                            after(pe, h_s, 4 * n + c - 1)
                            for k in range(DC):
                                last = pe.matmul(UB[:, c % 2, :], xqt[:, k, :], wt[:, 1, k * F + c * D:k * F + (c + 1) * D],
                                                 start=(k == 0), stop=(k == DC - 1))
                            last.then_inc(u_done, 1)
                        if not (isinstance(p, int) and n == TILES - 1):
                            turn_x(n + 1)
                        if not (isinstance(p, int) and n == 0):
                            down(n - 1)
                pe.wait_ge(set_s, 4)
                turn_x(0)
                pair(0)
                with pe.Fori(1, PAIRS - 1) as p:
                    pair(p)
                pair(PAIRS - 1)
                turn_h(TILES - 1)
                down(TILES - 1)


def kernel(**inputs):
    import numpy as np
    import concourse.bacc as bacc
    from concourse.bass_utils import run_bass_kernel_spmd

    f32 = np.float32
    a = {k: np.asarray(v) for k, v in inputs.items()}
    g = lambda name: a["L0_" + name]
    rows = lambda w: np.ascontiguousarray(w.reshape(-1, P, w.shape[1]).transpose(1, 0, 2))
    heads_T = lambda w: np.ascontiguousarray(w.reshape(w.shape[0], H, HD).transpose(2, 1, 0))
    inv = (f32(1.0) / f32(10000.0) ** (np.arange(R // 2, dtype=f32) / f32(R // 2))).astype(f32)
    ang = np.arange(LK, dtype=f32)[None, :] * inv[:, None]
    tab_k = np.concatenate([np.cos(ang), np.cos(ang), -np.sin(ang), np.sin(ang)], 0).astype(f32)
    angq = (np.arange(P) % LQ).astype(f32)[:, None] * inv
    tab_q = np.stack([np.cos(angq), -np.sin(angq), np.sin(angq)], 1).astype(f32)
    invs = np.exp(f32(-np.log(10000.0)) * np.arange(0, SD, 2, dtype=f32) / f32(SD)).astype(f32)
    angs = (np.arange(P) % LQ).astype(f32)[:, None] * invs
    causal = np.where(np.arange(LQ)[None, :] <= (np.arange(P) % LQ)[:, None], 0.0, -1e30)
    tab_s = np.concatenate([np.cos(angs), -np.sin(angs), np.sin(angs), causal], 1).astype(f32)
    tab_i = np.ascontiguousarray(np.broadcast_to(np.arange(LK, dtype=f32), (P, LK)))
    swap = (np.arange(R) + R // 2) % R
    wkr = g("xattn_W_kr")
    halves = np.concatenate([np.arange(0, SD, 2), np.arange(1, SD, 2)])
    order = (np.arange(SH)[:, None] * SD + halves).ravel()
    ffn = [g("ffn_w_gate").T, g("ffn_w_up").T, g("ffn_w_down").T]
    arrays = {
        "x": rows(a["x"].reshape(B * LQ, D)),
        "ctxT": np.ascontiguousarray(a["ctx_2048"].transpose(0, 2, 1).reshape(B, DC, P, LK)
                                     .transpose(0, 2, 1, 3)).reshape(B, P, DC * LK),
        "seg": np.ascontiguousarray(np.tile(a["itok_BxS_0_1023"].T, (TB, 1))),
        "Wkvc": rows(g("xattn_W_kvc")),
        "Wkr2": np.concatenate([wkr, wkr[:, swap]], 1),
        "Wdq": rows(g("xattn_W_dq")),
        "WuqT": heads_T(g("xattn_W_uq")),
        "WukT": heads_T(g("xattn_W_uk")),
        "WuvT": heads_T(g("xattn_W_uv")),
        "Wo": rows(g("xattn_W_o")),
        "Wqr": g("xattn_W_qr"),
        "Sq": rows(g("attn_Wq").T[:, order]),
        "Sk": rows(g("attn_Wk").T[:, order]),
        "Sv": rows(g("attn_Wv").T),
        "So": rows(g("attn_Wo").T),
        "Wffn": np.ascontiguousarray(np.stack([rows(w).reshape(P, -1) for w in ffn], 1)),
        "tab_k": tab_k, "tab_q": tab_q, "tab_s": tab_s, "tab_i": tab_i,
    }
    nc = bacc.Bacc("TRN2", target_bir_lowering=False, num_devices=1)
    aps = [nc.dram_tensor(f"in_{k}", v.shape, mybir.dt.from_np(v.dtype), kind="ExternalInput").ap()
           for k, v in arrays.items()]
    out = nc.dram_tensor("out", (B * LQ, D), F32, kind="ExternalOutput").ap()
    x_mid = nc.dram_tensor("x_mid", (P, TILES, D), F32).ap()
    build(nc, *aps, x_mid, out)
    r = run_bass_kernel_spmd(nc, [{f"in_{k}": np.ascontiguousarray(v) for k, v in arrays.items()}], core_ids=[0])
    return r.results[0]["out"].reshape(B, LQ, D)
```
